# Optimizing a Trainium2 kernel written in Bass

```python
import numpy as np
import jax
import jax.numpy as jnp

def _softmax(x, axis=-1):
    return jax.nn.softmax(x, axis=axis)

def _gelu(x):
    return jax.nn.gelu(x, approximate=True)

def _silu(x):
    return jax.nn.silu(x)

def _sigmoid(x):
    return jax.nn.sigmoid(x)

def _layernorm(x, axis=-1, eps=1e-05):
    m = jnp.mean(x, axis=axis, keepdims=True)
    v = jnp.var(x, axis=axis, keepdims=True)
    return (x - m) / jnp.sqrt(v + eps)

def _scatter_add(tgt, idx, src, axis=0):
    return tgt.at[idx].add(src)

def _segment_sum(src, seg, n):
    return jax.ops.segment_sum(src, seg, n)
kernel_name = 'mk_gnn_resnorm_d4_gnn_r8_db66be'

def setup_inputs(seed: int=0):
    np.random.seed(seed)
    _w = jnp.asarray

    def _rec_inputs():
        import jax
        import jax.numpy as jnp
        _gk = jax.random.key(seed)
        x = -0.000202 + 1 * jax.random.normal(jax.random.fold_in(_gk, 1), (12500, 64), jnp.float32)
        src = jax.random.randint(jax.random.fold_in(_gk, 2), (200000,), 0, 12500, jnp.int32)
        dst = jnp.minimum((12500 * jax.random.uniform(jax.random.fold_in(_gk, 3), (200000,)) ** 2.0).astype(jnp.int32), 99999)
        _o = jnp.argsort(dst, stable=True)
        src = src[_o]
        dst = dst[_o]
        edge_attr_64 = -4.21973e-05 + 0.999841 * jax.random.normal(jax.random.fold_in(_gk, 12), (200000, 64), jnp.float32)
        edge_type_8 = jax.random.randint(jax.random.fold_in(_gk, 14), (200000,), 0, 8, jnp.int32)
        edge_weight = jax.random.uniform(jax.random.fold_in(_gk, 15), (200000,), jnp.float32, 0.0, 0.999999)
        node_type_4 = jax.random.randint(jax.random.fold_in(_gk, 16), (12500,), 0, 4, jnp.int32)
        return (x, src, dst, edge_attr_64, edge_type_8, edge_weight, node_type_4)
    x, src, dst, edge_attr_64, edge_type_8, edge_weight, node_type_4 = _rec_inputs()

    def _L0_gnn_setup():
        import jax, jax.numpy as jnp
        import numpy as np
        N_NODES = 12500
        N_EDGES = 200000
        D_IN = 64
        D_OUT = 64
        key = jax.random.key(seed)
        k1, k2, k3, k4 = jax.random.split(key, 4)
        x = jax.random.normal(k1, (N_NODES, D_IN), dtype=jnp.float32)
        edge_index = jax.random.randint(k2, (2, N_EDGES), 0, N_NODES, dtype=jnp.int64)
        s1 = (6.0 / (D_IN + D_OUT)) ** 0.5
        s2 = (6.0 / (D_OUT + D_OUT)) ** 0.5
        W1 = jax.random.uniform(k3, (D_IN, D_OUT), dtype=jnp.float32, minval=-s1, maxval=s1)
        b1 = jnp.zeros((D_OUT,), dtype=jnp.float32)
        W2 = jax.random.uniform(k4, (D_OUT, D_OUT), dtype=jnp.float32, minval=-s2, maxval=s2)
        b2 = jnp.zeros((D_OUT,), dtype=jnp.float32)
        return {'x': x, 'edge_index': edge_index, 'W1': W1, 'b1': b1, 'W2': W2, 'b2': b2}
    _L0_gnn_all = _L0_gnn_setup()
    _L0_gnn_in = {k: v for k, v in _L0_gnn_all.items() if k in ('W1', 'b1', 'W2', 'b2')}
    del _L0_gnn_all

    def _L1_gnn_setup():
        import jax, jax.numpy as jnp
        import numpy as np
        N_NODES = 12500
        N_EDGES = 150000
        D = 64
        key = jax.random.key(seed)
        k1, k2, k3, k4, k5 = jax.random.split(key, 5)
        node_feat = jax.random.normal(k1, (N_NODES, D), dtype=jnp.float32)
        edge_feat = jax.random.normal(k2, (N_EDGES, D), dtype=jnp.float32)
        edge_index = jax.random.randint(k3, (2, N_EDGES), 0, N_NODES, dtype=jnp.int32)
        W1 = jax.random.normal(k4, (D, 2 * D), dtype=jnp.float32) / np.sqrt(D)
        b1 = jnp.zeros((2 * D,), dtype=jnp.float32)
        W2 = jax.random.normal(k5, (2 * D, D), dtype=jnp.float32) / np.sqrt(2 * D)
        b2 = jnp.zeros((D,), dtype=jnp.float32)
        return {'node_feat': node_feat, 'edge_feat': edge_feat, 'edge_index': edge_index, 'W1': W1, 'b1': b1, 'W2': W2, 'b2': b2}
    _L1_gnn_all = _L1_gnn_setup()
    _L1_gnn_in = {k: v for k, v in _L1_gnn_all.items() if k in ('W1', 'b1', 'W2', 'b2')}
    del _L1_gnn_all

    def _L2_gnn_setup():
        import jax, jax.numpy as jnp
        import numpy as np
        N = 6250
        E = 160000
        D = 64
        HEADS = 1
        NEG_SLOPE = 0.2
        EPS_COS = 1e-08
        EPS_SM = 1e-16

        def _xavier(key, shape):
            fan_in, fan_out = (shape[0], shape[-1])
            lim = float(np.sqrt(6.0 / (fan_in + fan_out)))
            return jax.random.uniform(key, shape, jnp.float32, -lim, lim)

        def _seg_softmax(logits, idx, n):
            m = jax.ops.segment_max(logits, idx, num_segments=n)
            ex = jnp.exp(logits - m[idx])
            s = jax.ops.segment_sum(ex, idx, num_segments=n)
            return ex / (s[idx] + EPS_SM)

        def _cosgat(x, src, dst, w, W, att, beta, bias):
            n = x.shape[0]
            H = (x @ W).reshape(n, HEADS, -1)
            Hi, Hj = (H[dst], H[src])
            logits = jnp.einsum('ehc,hc->eh', Hi, att[:, :H.shape[-1]]) + jnp.einsum('ehc,hc->eh', Hj, att[:, H.shape[-1]:])
            logits = jnp.where(logits >= 0, logits, NEG_SLOPE * logits)
            xi, xj = (x[dst], x[src])
            ni = jnp.maximum(jnp.linalg.norm(xi, axis=-1), EPS_COS)
            nj = jnp.maximum(jnp.linalg.norm(xj, axis=-1), EPS_COS)
            cos = jnp.sum(xi * xj, axis=-1) / (ni * nj)
            cos = jnp.broadcast_to(cos[:, None], logits.shape)
            gat_alpha = _seg_softmax(logits, dst, n)
            cos_alpha = _seg_softmax(cos, dst, n)
            b = jax.nn.sigmoid(beta)[None, :]
            fused = (1.0 - b) * gat_alpha + b * cos_alpha
            w_cl = jnp.minimum(w, 4.0)
            gate = jnp.clip(1.0 - w_cl / 4.0, 0.0, 1.0)[:, None]
            final = _seg_softmax(fused * gate, dst, n)
            msg = Hj * final[:, :, None]
            out = jax.ops.segment_sum(msg, dst, num_segments=n)
            out = out.reshape(n, -1) + bias
            return jax.nn.elu(out)
        key = jax.random.key(seed)
        ks = jax.random.split(key, 16)
        x = jax.random.normal(ks[0], (N, D), jnp.float32)
        edge_index = jax.random.randint(ks[1], (2, E), 0, N, jnp.int64)
        edge_attr = jax.random.uniform(ks[2], (E,), jnp.float32)
        return {'x': x, 'edge_index': edge_index, 'edge_attr': edge_attr, 'W0': _xavier(ks[3], (D, HEADS * D)), 'att0': _xavier(ks[4], (HEADS, 2 * D)), 'beta0': jnp.zeros((HEADS,), jnp.float32), 'b0': jnp.zeros((HEADS * D,), jnp.float32), 'W1': _xavier(ks[5], (D, HEADS * D)), 'att1': _xavier(ks[6], (HEADS, 2 * D)), 'beta1': jnp.zeros((HEADS,), jnp.float32), 'b1': jnp.zeros((HEADS * D,), jnp.float32), 'rW1': _xavier(ks[7], (D, D)), 'rb1': jnp.zeros((D,), jnp.float32), 'rW2': _xavier(ks[8], (D, D)), 'rb2': jnp.zeros((D,), jnp.float32)}
    _L2_gnn_all = _L2_gnn_setup()
    _L2_gnn_in = {k: v for k, v in _L2_gnn_all.items() if k in ('W0', 'att0', 'beta0', 'b0', 'W1', 'att1', 'beta1', 'b1', 'rW1', 'rb1', 'rW2', 'rb2')}
    del _L2_gnn_all

    def _L3_gnn_setup():
        import jax, jax.numpy as jnp
        import numpy as np
        N_TYPES = 4
        N_RELS = 8
        N, E, IN_DIM, OUT_DIM = (12500, 200000, 64, 64)
        SQRT_DK = float(np.sqrt(OUT_DIM))

        def _typed_matmul(x, W, node_type):
            out = jnp.zeros((x.shape[0], W.shape[-1]), x.dtype)
            for t in range(W.shape[0]):
                out = out + jnp.where((node_type == t)[:, None], x @ W[t], 0.0)
            return out
        key = jax.random.key(seed)
        ks = jax.random.split(key, 12)
        s = 0.05
        h = jax.random.normal(ks[0], (N, IN_DIM), jnp.float32)
        node_type = jax.random.randint(ks[1], (N,), 0, N_TYPES, jnp.int32)
        src = jax.random.randint(ks[2], (E,), 0, N, jnp.int32)
        dst = jax.random.randint(ks[3], (E,), 0, N, jnp.int32)
        etype = jax.random.randint(ks[4], (E,), 0, N_RELS, jnp.int32)
        k_lin = jax.random.normal(ks[5], (N_TYPES, IN_DIM, OUT_DIM), jnp.float32) * s
        q_lin = jax.random.normal(ks[6], (N_TYPES, IN_DIM, OUT_DIM), jnp.float32) * s
        v_lin = jax.random.normal(ks[7], (N_TYPES, IN_DIM, OUT_DIM), jnp.float32) * s
        a_lin = jax.random.normal(ks[8], (N_TYPES, OUT_DIM, OUT_DIM), jnp.float32) * s
        rel_att = jax.random.normal(ks[9], (N_RELS, OUT_DIM, OUT_DIM), jnp.float32) * s
        rel_msg = jax.random.normal(ks[10], (N_RELS, OUT_DIM, OUT_DIM), jnp.float32) * s
        rel_pri = jnp.ones((N_RELS,), jnp.float32)
        skip = jnp.ones((N_TYPES,), jnp.float32)
        return dict(h=h, node_type=node_type, src=src, dst=dst, etype=etype, k_lin=k_lin, q_lin=q_lin, v_lin=v_lin, a_lin=a_lin, rel_att=rel_att, rel_msg=rel_msg, rel_pri=rel_pri, skip=skip)
    _L3_gnn_all = _L3_gnn_setup()
    _L3_gnn_in = {k: v for k, v in _L3_gnn_all.items() if k in ('k_lin', 'q_lin', 'v_lin', 'a_lin', 'rel_att', 'rel_msg', 'rel_pri', 'skip')}
    del _L3_gnn_all
    return {'x': x, 'src': src, 'dst': dst, 'edge_attr_64': edge_attr_64, 'edge_type_8': edge_type_8, 'edge_weight': edge_weight, 'node_type_4': node_type_4, 'L0_gnn_W1': _L0_gnn_in['W1'], 'L0_gnn_b1': _L0_gnn_in['b1'], 'L0_gnn_W2': _L0_gnn_in['W2'], 'L0_gnn_b2': _L0_gnn_in['b2'], 'L1_gnn_W1': _L1_gnn_in['W1'], 'L1_gnn_b1': _L1_gnn_in['b1'], 'L1_gnn_W2': _L1_gnn_in['W2'], 'L1_gnn_b2': _L1_gnn_in['b2'], 'L2_gnn_W0': _L2_gnn_in['W0'], 'L2_gnn_att0': _L2_gnn_in['att0'], 'L2_gnn_beta0': _L2_gnn_in['beta0'], 'L2_gnn_b0': _L2_gnn_in['b0'], 'L2_gnn_W1': _L2_gnn_in['W1'], 'L2_gnn_att1': _L2_gnn_in['att1'], 'L2_gnn_beta1': _L2_gnn_in['beta1'], 'L2_gnn_b1': _L2_gnn_in['b1'], 'L2_gnn_rW1': _L2_gnn_in['rW1'], 'L2_gnn_rb1': _L2_gnn_in['rb1'], 'L2_gnn_rW2': _L2_gnn_in['rW2'], 'L2_gnn_rb2': _L2_gnn_in['rb2'], 'L3_gnn_k_lin': _L3_gnn_in['k_lin'], 'L3_gnn_q_lin': _L3_gnn_in['q_lin'], 'L3_gnn_v_lin': _L3_gnn_in['v_lin'], 'L3_gnn_a_lin': _L3_gnn_in['a_lin'], 'L3_gnn_rel_att': _L3_gnn_in['rel_att'], 'L3_gnn_rel_msg': _L3_gnn_in['rel_msg'], 'L3_gnn_rel_pri': _L3_gnn_in['rel_pri'], 'L3_gnn_skip': _L3_gnn_in['skip']}

def reference(x, src, dst, edge_attr_64, edge_type_8, edge_weight, node_type_4, L0_gnn_W1, L0_gnn_b1, L0_gnn_W2, L0_gnn_b2, L1_gnn_W1, L1_gnn_b1, L1_gnn_W2, L1_gnn_b2, L2_gnn_W0, L2_gnn_att0, L2_gnn_beta0, L2_gnn_b0, L2_gnn_W1, L2_gnn_att1, L2_gnn_beta1, L2_gnn_b1, L2_gnn_rW1, L2_gnn_rb1, L2_gnn_rW2, L2_gnn_rb2, L3_gnn_k_lin, L3_gnn_q_lin, L3_gnn_v_lin, L3_gnn_a_lin, L3_gnn_rel_att, L3_gnn_rel_msg, L3_gnn_rel_pri, L3_gnn_skip):
    import jax
    import jax.numpy as jnp

    def _L0_gnn_ref(x, edge_index, W1, b1, W2, b2):
        import jax, jax.numpy as jnp
        import numpy as np
        N_NODES = 12500
        N_EDGES = 200000
        D_IN = 64
        D_OUT = 64
        src, dst = (edge_index[0], edge_index[1])
        agg = jax.ops.segment_sum(x[src], dst, num_segments=N_NODES)
        h = x + agg
        h = jax.nn.relu(h @ W1 + b1)
        return h @ W2 + b2

    def _L1_gnn_ref(node_feat, edge_feat, edge_index, W1, b1, W2, b2):
        import jax, jax.numpy as jnp
        import numpy as np
        N_NODES = 12500
        N_EDGES = 150000
        D = 64
        src, dst = (edge_index[0], edge_index[1])
        msg = node_feat[src] + edge_feat
        agg = jax.ops.segment_sum(msg, dst, num_segments=node_feat.shape[0])
        h = jax.nn.relu(agg @ W1 + b1)
        out = h @ W2 + b2
        return out

    def _L2_gnn_ref(x, edge_index, edge_attr, W0, att0, beta0, b0, W1, att1, beta1, b1, rW1, rb1, rW2, rb2):
        import jax, jax.numpy as jnp
        import numpy as np
        N = 6250
        E = 160000
        D = 64
        HEADS = 1
        NEG_SLOPE = 0.2
        EPS_COS = 1e-08
        EPS_SM = 1e-16

        def _xavier(key, shape):
            fan_in, fan_out = (shape[0], shape[-1])
            lim = float(np.sqrt(6.0 / (fan_in + fan_out)))
            return jax.random.uniform(key, shape, jnp.float32, -lim, lim)

        def _seg_softmax(logits, idx, n):
            m = jax.ops.segment_max(logits, idx, num_segments=n)
            ex = jnp.exp(logits - m[idx])
            s = jax.ops.segment_sum(ex, idx, num_segments=n)
            return ex / (s[idx] + EPS_SM)

        def _cosgat(x, src, dst, w, W, att, beta, bias):
            n = x.shape[0]
            H = (x @ W).reshape(n, HEADS, -1)
            Hi, Hj = (H[dst], H[src])
            logits = jnp.einsum('ehc,hc->eh', Hi, att[:, :H.shape[-1]]) + jnp.einsum('ehc,hc->eh', Hj, att[:, H.shape[-1]:])
            logits = jnp.where(logits >= 0, logits, NEG_SLOPE * logits)
            xi, xj = (x[dst], x[src])
            ni = jnp.maximum(jnp.linalg.norm(xi, axis=-1), EPS_COS)
            nj = jnp.maximum(jnp.linalg.norm(xj, axis=-1), EPS_COS)
            cos = jnp.sum(xi * xj, axis=-1) / (ni * nj)
            cos = jnp.broadcast_to(cos[:, None], logits.shape)
            gat_alpha = _seg_softmax(logits, dst, n)
            cos_alpha = _seg_softmax(cos, dst, n)
            b = jax.nn.sigmoid(beta)[None, :]
            fused = (1.0 - b) * gat_alpha + b * cos_alpha
            w_cl = jnp.minimum(w, 4.0)
            gate = jnp.clip(1.0 - w_cl / 4.0, 0.0, 1.0)[:, None]
            final = _seg_softmax(fused * gate, dst, n)
            msg = Hj * final[:, :, None]
            out = jax.ops.segment_sum(msg, dst, num_segments=n)
            out = out.reshape(n, -1) + bias
            return jax.nn.elu(out)
        src, dst = (edge_index[0], edge_index[1])
        x_res = jax.nn.relu(x @ rW1 + rb1) @ rW2 + rb2
        h = _cosgat(x, src, dst, edge_attr, W0, att0, beta0, b0)
        h = jax.nn.elu(h)
        h = _cosgat(h, src, dst, edge_attr, W1, att1, beta1, b1)
        return h + x_res

    def _L3_gnn_ref(h, node_type, src, dst, etype, k_lin, q_lin, v_lin, a_lin, rel_att, rel_msg, rel_pri, skip):
        import jax, jax.numpy as jnp
        import numpy as np
        N_TYPES = 4
        N_RELS = 8
        N, E, IN_DIM, OUT_DIM = (12500, 200000, 64, 64)
        SQRT_DK = float(np.sqrt(OUT_DIM))

        def _typed_matmul(x, W, node_type):
            out = jnp.zeros((x.shape[0], W.shape[-1]), x.dtype)
            for t in range(W.shape[0]):
                out = out + jnp.where((node_type == t)[:, None], x @ W[t], 0.0)
            return out
        k = _typed_matmul(h, k_lin, node_type)
        q = _typed_matmul(h, q_lin, node_type)
        v = _typed_matmul(h, v_lin, node_type)
        qW = jnp.einsum('nd,rde->rne', q, rel_att)
        t_edge = qW[etype, dst]
        score = jnp.sum(t_edge * k[src], axis=-1)
        logits = score * (rel_pri / SQRT_DK)[etype]
        m = jax.ops.segment_max(logits, dst, num_segments=N)
        ex = jnp.exp(logits - m[dst])
        den = jax.ops.segment_sum(ex, dst, num_segments=N)
        alpha = ex / jnp.where(den[dst] == 0, 1.0, den[dst])
        vW = jnp.einsum('nd,rde->rne', v, rel_msg)
        msg = vW[etype, src]
        agg = jax.ops.segment_sum(alpha[:, None] * msg, dst, num_segments=N)
        W_out = jax.nn.sigmoid(skip)[:, None, None] * a_lin
        return _typed_matmul(agg, W_out, node_type)
    edge_index = jnp.stack([src, dst])
    x = _layernorm(x + _L0_gnn_ref(x, edge_index, L0_gnn_W1, L0_gnn_b1, L0_gnn_W2, L0_gnn_b2), axis=-1)
    x = _layernorm(x + _L1_gnn_ref(x, edge_attr_64, edge_index, L1_gnn_W1, L1_gnn_b1, L1_gnn_W2, L1_gnn_b2), axis=-1)
    x = _layernorm(x + _L2_gnn_ref(x, edge_index, edge_weight, L2_gnn_W0, L2_gnn_att0, L2_gnn_beta0, L2_gnn_b0, L2_gnn_W1, L2_gnn_att1, L2_gnn_beta1, L2_gnn_b1, L2_gnn_rW1, L2_gnn_rb1, L2_gnn_rW2, L2_gnn_rb2), axis=-1)
    x = _layernorm(x + _L3_gnn_ref(x, node_type_4, src, dst, edge_type_8, L3_gnn_k_lin, L3_gnn_q_lin, L3_gnn_v_lin, L3_gnn_a_lin, L3_gnn_rel_att, L3_gnn_rel_msg, L3_gnn_rel_pri, L3_gnn_skip), axis=-1)
    return x

_drawn_inputs = setup_inputs


def setup_inputs(seed=0):
    import zlib

    import numpy as np

    out = dict(_drawn_inputs(seed))
    spreads = {'L0_gnn_b1': (0.0, 0.294),
     'L0_gnn_b2': (0.0, 0.1),
     'L1_gnn_b1': (0.0, 0.594),
     'L1_gnn_b2': (0.0, 0.32),
     'L2_gnn_b0': (0.0, 0.1),
     'L2_gnn_b1': (0.0, 0.1),
     'L2_gnn_rb1': (0.0, 0.1),
     'L2_gnn_rb2': (0.0, 0.1),
     'L3_gnn_rel_pri': (1.0, 0.6),
     'L3_gnn_skip': (1.0, 0.6)}
    factors = {'edge_weight': 8.0,
     'L2_gnn_att0': 8.0,
     'L2_gnn_att1': 8.0,
     'L3_gnn_k_lin': 8.0,
     'L3_gnn_q_lin': 8.0,
     'L3_gnn_v_lin': 3.518,
     'L3_gnn_a_lin': 3.504,
     'L3_gnn_rel_att': 8.0,
     'L3_gnn_rel_msg': 3.515}
    for name, (base, spread) in spreads.items():
        noise = np.random.default_rng([zlib.crc32(name.encode()), seed]).standard_normal(out[name].shape)
        drawn = base * np.exp(spread * noise) if base else spread * noise
        out[name] = jnp.asarray(drawn.astype(out[name].dtype))
    for name, factor in factors.items():
        out[name] = (out[name] * factor).astype(out[name].dtype)
    return out
```

```python
from contextlib import ExitStack

import concourse.bass as bass
from concourse import mybir

ALU = mybir.AluOpType
ACT = mybir.ActivationFunctionType
AX = mybir.AxisListType
F32 = mybir.dt.float32
BF16 = mybir.dt.bfloat16
I16 = mybir.dt.int16
I32 = mybir.dt.int32
U32 = mybir.dt.uint32

P = 128
C = 4
GE = P * C
N, E, F = 12500, 200000, 64
NT, NR = 4, 8
FULL = E // GE
GROUPS = -(-(FULL + 1) // C) * C
TAIL = E - GE
OVER = (FULL + 1) * GE - E
WIN = -(-N // P)
ND = -(-(N + P) // P) * P
OFF_IDLE = N
FRONT = 4
CAP = -(-(GROUPS * WIN + 2 * FRONT + 24) // P) * P
RING = 4
PRIME = 8
Q, J = 125, 4
CH = Q * J
CHUNKS = N // CH
BIG = 1.0e30
LN_EPS = 1e-5
SM_EPS = 1e-16
COS_EPS2 = 1e-16
SLOPE = 0.2


def build(nc, io, out):
    with ExitStack() as ctx:
        def sb(name, shape, dt=F32):
            return ctx.enter_context(nc.sbuf_tensor(name, shape, dt))

        def sem(name):
            return ctx.enter_context(nc.semaphore(name))

        phase_sems = []

        def psem(name):
            phase_sems.append(nc.alloc_semaphore(name))
            return phase_sems[-1]

        def next_phase():
            nc.clear_and_free_semaphores(list(phase_sems))
            nc.all_engine_barrier()
            phase_sems.clear()

        def dram(name, shape, dt=F32):
            return nc.dram_tensor(name, shape, dt).ap()

        x1_d, x2_d, x3_d, h1_d, h2_d = (dram(f"{n}_d", (N, F)) for n in ("x1", "x2", "x3", "h1", "h2"))
        src_d = dram("src_d", (GROUPS + 1, P, C), I32)
        rel_d = dram("rel_d", (GROUPS + 1, P, C), I32)
        iota_d = dram("iota_d", (ND, 1), I32)
        base_d = dram("base_d", (GROUPS, 1), I32)
        nwin_d = dram("nwin_d", (GROUPS, 1), I32)
        off_d = dram("off_d", (CAP, 1), I32)
        grp_d = dram("grp_d", (CAP, 1), I32)
        iters_d = dram("iters_d", (1, 2), I32)
        srctab_d = dram("srctab_d", (N, F + 2))
        dsttab_d = dram("dsttab_d", (ND, F + 2))
        stat_d = dram("stat_d", (ND, 4))
        stash_d = dram("stash_d", (GROUPS + 1, P, C * (F + 2)))
        reltab_d = dram("reltab_d", (NR * N, 2 * F))
        trash_d = dram("trash_d", (P, C * (F + 2)))

        acc = sb("acc", [P, ND])
        top = sb("top", [P, ND])
        iota16 = sb("iota16", [P, ND], I16)
        dstf = sb("dstf", [P, GROUPS * C + C])
        gate = sb("gate", [P, GROUPS * C + C])
        logit = sb("logit", [P, GROUPS * C + C])
        ecos = sb("ecos", [P, GROUPS * C + C])
        ident = sb("ident", [P, P])
        work = sb("work", [P, 6144])
        rows = [sb(f"rows{k}", [P, C, 2 * F]) for k in range(RING)]
        pay = [sb(f"pay{k}", [P, C, F + 1]) for k in range(RING)]
        dwin = [sb(f"dwin{k}", [P, F + 2]) for k in range(RING)]
        idx = [sb(f"idx{k}", [P, C], I32) for k in range(RING)]
        small = sb("small", [P, 256])
        wts = sb("wts", [P, 2400])
        bias = sb("bias", [P, 640])
        bank = [ctx.enter_context(nc.psum_tensor(f"bank{b}", [P, 512], F32)) for b in range(8)]

        onehot = [work[:, k * 512:(k + 1) * 512].rearrange("p (c n) -> p c n", c=C) for k in range(RING)]
        turned = [work[:, 2048 + k * 512:2048 + (k + 1) * 512] for k in range(RING)]
        block_ = [work[:, 4096 + k * 256:4096 + (k + 1) * 256].bitcast(BF16) for k in range(RING)]
        diag = [work[:, 5120 + k * 512:5120 + (k + 1) * 512].rearrange("p (c n) -> p c n", c=C) for k in range(2)]

        at, wcols, bcols = 0, {}, {}
        for name, w in (("W01", 64), ("W02", 64), ("W11", 128), ("W12", 64), ("G0", 65), ("G1", 65), ("R1", 64),
                        ("R2", 64), ("K", 128), ("Qw", 128), ("V", 128), ("A", 128), ("RA", 512), ("RM", 512),
                        ("U0", 2), ("U1", 2), ("pri", 8), ("skip", 2), ("beta", 2), ("mix", 4)):
            wcols[name] = (at, at + w)
            at += w
        at = 0
        for name, w in (("b02", 64), ("b12", 64), ("bg0", 64), ("bg1", 64), ("rb2", 64), ("att0", 128), ("att1", 128),
                        ("b01", 1), ("b11", 1), ("rb1", 1)):
            bcols[name] = (at, at + w)
            at += w

        def wt(name, k=64):
            a, b = wcols[name]
            return wts[0:k, a:b]

        def bs(name, k=P):
            a, b = bcols[name]
            return bias[0:k, a:b]

        def grouped(x):
            return x[0:FULL * GE].rearrange("(g p c) -> p g c", p=P, c=C)

        def tail(x):
            return x[TAIL:E].rearrange("(p c) -> p c", c=C)

        loaded, made, stored, sched = (sem(n) for n in ("loaded", "made", "prep_stored", "sched_stored"))
        acted, pooled, summed = sem("prep_acted"), sem("prep_pooled"), sem("steps_summed")
        cols = C * GROUPS
        raw_i = [top[:, k * 2048:k * 2048 + cols].bitcast(I32) for k in range(4)]
        raw_f = [acc[:, k * 2048:k * 2048 + cols] for k in range(6)]
        QP = GROUPS // 4
        spans = top[0:QP, 8192:8192 + 2048].bitcast(I32).rearrange("p (g e) -> p g e", g=4)
        spansf = acc[0:QP, 10240:10240 + 2048].rearrange("p (g e) -> p g e", g=4)
        lo, hi, nwin = small[0:QP, 0:4], small[0:QP, 4:8], small[0:QP, 8:12]
        lo_i, hi_i = small[0:QP, 16:20].bitcast(I32), small[0:QP, 20:24].bitcast(I32)
        nsum = small[0:QP, 24:25]
        total, total_i = small[0:1, 32:34], small[0:1, 36:38].bitcast(I32)
        idle_i = work[:, 0:CAP // P].bitcast(I32)
        iota_i = work[:, 512:512 + ND // P].bitcast(I32)
        dpad = work[:, 1024:1024 + 2 * (F + 2)].rearrange("p (a b) -> p a b", a=2)
        zero_i = work[:, 2048:2048 + C].bitcast(I32)
        idle_g = work[:, 2100:2100 + CAP // P].bitcast(I32)
        ones = small[:, 40:41]
        prod64 = work[0:64, 3072:3136]
        sg = wts[:, wcols["skip"][0]:wcols["beta"][1]]
        rel_made, windows_made, counts_made, total_made = (sem(n) for n in ("rel_made", "windows_made", "counts_made", "total_made"))

        with nc.Block() as block:
            loads = []

            @block.sync
            def _(sp):
                def load(dst, src):
                    loads.append(1)
                    sp.dma_start(dst, src).then_inc(loaded, 16)

                for k, name in enumerate(("dst", "src", "edge_weight", "edge_type_8")):
                    t = raw_i[k] if name != "edge_weight" else raw_f[5]
                    load(t[:, 0:C * FULL].rearrange("p (g c) -> p g c", c=C), grouped(io[name]))
                    for g in range(FULL, GROUPS):
                        load(t[:, C * g:C * g + C], tail(io[name]))
                full4 = FULL // 4
                load(spans[0:full4, :, :], io["dst"][0:full4 * 4 * GE].rearrange("(p g e) -> p g e", g=4, e=GE))
                for g in range(full4 * 4, GROUPS):
                    a = min(g * GE, TAIL)
                    load(spans[g // 4:g // 4 + 1, g % 4, :], io["dst"][a:a + GE].rearrange("(p e) -> p e", p=1))
                sp.wait_ge(pooled, 1)
                for name, key, k in (("W01", "L0_gnn_W1", 64), ("W02", "L0_gnn_W2", 64), ("W12", "L1_gnn_W2", 128),
                                     ("R1", "L2_gnn_rW1", 64), ("R2", "L2_gnn_rW2", 64)):
                    load(wt(name, k), io[key])
                load(wts[0:64, wcols["W11"][0]:wcols["W11"][1]], io["L1_gnn_W1"])
                load(wts[64:128, wcols["W11"][0]:wcols["W11"][1]], io["L1_gnn_W1"])
                for name, key in (("G0", "L2_gnn_W0"), ("G1", "L2_gnn_W1")):
                    a = wcols[name][0]
                    load(wts[0:64, a:a + 64], io[key])
                for name, key in (("K", "L3_gnn_k_lin"), ("Qw", "L3_gnn_q_lin"), ("V", "L3_gnn_v_lin"), ("A", "L3_gnn_a_lin")):
                    load(wt(name, 128).rearrange("p (h e) -> p h e", h=2), io[key].rearrange("(h p) e -> p h e", h=2))
                load(wt("RA"), io["L3_gnn_rel_att"])
                load(wt("RM"), io["L3_gnn_rel_msg"])
                load(wt("pri"), io["L3_gnn_rel_pri"].partition_broadcast(64))
                for t in range(NT):
                    a = wcols["skip"][0] + t // 2
                    load(wts[64 * (t % 2):64 * (t % 2) + 64, a:a + 1], io["L3_gnn_skip"][t:t + 1].partition_broadcast(64))
                for i, key in enumerate(("L2_gnn_beta0", "L2_gnn_beta1")):
                    a = wcols["beta"][0] + i
                    load(wts[:, a:a + 1], io[key].partition_broadcast(P))
                for name, key in (("b02", "L0_gnn_b2"), ("b12", "L1_gnn_b2"), ("bg0", "L2_gnn_b0"), ("bg1", "L2_gnn_b1"),
                                  ("rb2", "L2_gnn_rb2")):
                    load(bs(name), io[key].partition_broadcast(P))
                for name, key in (("att0", "L2_gnn_att0"), ("att1", "L2_gnn_att1")):
                    load(bs(name, 64), io[key].rearrange("a b -> (a b)").partition_broadcast(64))
                for name, key, k in (("b01", "L0_gnn_b1", 64), ("b11", "L1_gnn_b1", 128), ("rb1", "L2_gnn_rb1", 64)):
                    load(bs(name, k), io[key].rearrange("(a b) -> a b", b=1))
                sp.wait_ge(rel_made, 1)
                sp.dma_start(src_d[0:GROUPS].rearrange("g p c -> p g c"), raw_i[1].rearrange("p (g c) -> p g c", c=C)).then_inc(stored, 16)
                sp.dma_start(rel_d[0:GROUPS].rearrange("g p c -> p g c"), raw_i[2].rearrange("p (g c) -> p g c", c=C)).then_inc(stored, 16)
                sp.wait_ge(pooled, 2)
                sp.dma_start(iota_d.rearrange("(p a) b -> p (a b)", p=P), iota_i).then_inc(stored, 16)
                for d in (src_d, rel_d):
                    sp.dma_start(d[GROUPS], zero_i[:, 0:C]).then_inc(stored, 16)
                sp.dma_start(off_d.rearrange("(p a) b -> p (a b)", p=P), idle_i).then_inc(stored, 16)
                sp.dma_start(grp_d.rearrange("(p a) b -> p (a b)", p=P), idle_g).then_inc(stored, 16)
                sp.dma_start(dsttab_d[N:ND, :].rearrange("(p a) b -> p a b", p=(ND - N) // 2), dpad[0:(ND - N) // 2, :, :]).then_inc(stored, 16)
                sp.dma_start(stat_d[N:ND, :].rearrange("(p a) b -> p a b", p=(ND - N) // 2), dpad[0:(ND - N) // 2, :, 0:4]).then_inc(stored, 16)
                sp.wait_ge(windows_made, 1)
                sp.dma_start(base_d.rearrange("(p a) b -> p (a b)", p=QP), lo_i).then_inc(stored, 16)
                sp.dma_start(nwin_d.rearrange("(p a) b -> p (a b)", p=QP), hi_i).then_inc(stored, 16)
                sp.wait_ge(total_made, 1)
                sp.dma_start(iters_d, total_i).then_inc(stored, 16)
                sp.wait_ge(stored, 16 * 12)

            @block.gpsimd
            def _(pool):
                nc.gpsimd.memset(wts[:], 0.0).then_inc(pooled, 1)
                nc.gpsimd.memset(idle_i, OFF_IDLE)
                nc.gpsimd.memset(zero_i, 0)
                nc.gpsimd.memset(idle_g, GROUPS)
                nc.gpsimd.memset(dpad, 0.0)
                nc.gpsimd.memset(ones, 1.0)
                nc.gpsimd.iota(iota16[:], pattern=[[1, ND]], base=0, channel_multiplier=0)
                nc.gpsimd.memset(ident[:], 0.0)
                nc.gpsimd.iota(iota_i, pattern=[[1, ND // P]], base=0, channel_multiplier=ND // P).then_inc(pooled, 1)
                pool.wait_ge(pooled, 2)
                nc.gpsimd.affine_select(out=ident[:], in_=ident[:], compare_op=ALU.not_equal, fill=1.0, base=0,
                                        pattern=[[-1, P]], channel_multiplier=1).then_inc(pooled, 1)

            @block.vector
            def _(dve):
                V = nc.vector
                add, mul = ALU.add, ALU.mult
                chained = [0]

                def link(ins):
                    chained[0] += 1
                    ins.then_inc(made, 1)
                    dve.wait_ge(made, chained[0])

                def show(ins, signal):
                    ins.then_inc(signal, 1)
                    dve.wait_ge(signal, 1)

                dve.wait_ge(loaded, 16 * len(loads))
                dve.wait_ge(pooled, 3)
                link(V.tensor_copy(dstf[:, 0:cols], raw_i[0]))
                link(V.memset(dstf[0:OVER // C, C * FULL:C * FULL + C], -1.0))
                link(V.memset(dstf[:, C * (FULL + 1):], -1.0))
                link(V.tensor_copy(raw_f[1], raw_i[1]))
                link(V.tensor_copy(raw_f[2], raw_i[3]))
                link(V.scalar_tensor_tensor(raw_f[1], raw_f[2], float(N), raw_f[1], mul, add))
                show(V.tensor_copy(raw_i[2], raw_f[1]), rel_made)
                link(V.tensor_scalar(gate[:, 0:cols], raw_f[5], 4.0, -0.25, ALU.min, mul))
                link(V.memset(gate[:, cols:], 1.0))
                link(V.tensor_scalar(gate[:], gate[:], 1.0, 0.0, add, ALU.max))
                link(V.tensor_scalar(gate[:], gate[:], 1.0, None, ALU.min))
                link(V.tensor_copy(spansf, spans))
                link(V.tensor_reduce(lo, spansf, AX.X, ALU.min))
                link(V.tensor_reduce(hi, spansf, AX.X, ALU.max))
                link(V.tensor_copy(lo_i, lo))
                link(V.tensor_tensor(hi, hi, lo, ALU.subtract))
                link(V.tensor_scalar(hi, hi, float(P), None, add))
                link(V.tensor_copy(hi_i, hi))
                link(V.tensor_scalar(hi_i, hi_i, 7, None, ALU.arith_shift_right))
                show(V.tensor_copy(nwin, hi_i), windows_made)
                show(V.tensor_reduce(nsum, nwin, AX.X, add), counts_made)
                dve.wait_ge(summed, 1)
                link(V.tensor_scalar(total[:, 0:1], bank[0][0:1, 0:1], float(FRONT + RING - 1), None, add))
                link(V.tensor_copy(total[:, 1:2], bank[0][0:1, 0:1]))
                link(V.tensor_copy(total_i, total))
                show(V.tensor_scalar(total_i[:, 0:1], total_i[:, 0:1], 2, None, ALU.arith_shift_right), total_made)
                for i in range(2):
                    g, a = wcols[f"G{i}"][0], wcols[f"U{i}"][0]
                    att = bs(f"att{i}", 64)
                    for h in range(2):
                        link(V.tensor_tensor(prod64, wts[0:64, g:g + 64], att[:, 64 * h:64 * h + 64], mul))
                        link(V.tensor_reduce(wts[0:64, a + h:a + h + 1], prod64, AX.X, add))
                    link(V.memset(wts[64:65, g + 64:g + 65], 1.0))
                link(V.tensor_scalar(wt("pri"), wt("pri"), 1.0 / 8.0, None, mul))
                ra = wt("RA").rearrange("p (r d) -> p r d", r=NR)
                link(V.tensor_tensor(ra, ra, wt("pri").unsqueeze(2).to_broadcast([64, NR, F]), mul))
                dve.wait_ge(acted, 1)
                link(V.tensor_scalar(sg, sg, 1.0, None, add))
                link(V.reciprocal(sg, sg))
                for i in range(2):
                    m, b = wcols["mix"][0] + 2 * i, wcols["beta"][0] + i
                    link(V.tensor_copy(wts[:, m + 1:m + 2], wts[:, b:b + 1]))
                    link(V.tensor_scalar(wts[:, m:m + 1], wts[:, b:b + 1], -1.0, 1.0, mul, add))
                    a, s = wcols["A"][0] + 64 * i, wcols["skip"][0] + i
                    link(V.tensor_scalar(wts[:, a:a + 64], wts[:, a:a + 64], wts[:, s:s + 1], None, mul))

            @block.tensor
            def _(pe):
                pe.wait_ge(counts_made, 1)
                pe.matmul(bank[0][0:1, 0:1], nsum, ones[0:QP, :], start=True, stop=True).then_inc(summed, 1)

            @block.scalar
            def _(act):
                act.wait_ge(loaded, 16 * len(loads))
                nc.scalar.activation(sg, sg, ACT.Exp, scale=-1.0).then_inc(acted, 1)

        with nc.Block() as block:
            @block.sync
            def _(sp):
                steps_n = sp.value_load(iters_d[0:1, 1:2], min_val=GROUPS, max_val=GROUPS * WIN)
                at_reg, off_reg = sp.alloc_register("step_at"), sp.alloc_register("step_off")
                with sp.If(steps_n == GROUPS):
                    sp.dma_start(off_d[FRONT:FRONT + GROUPS, :], base_d[:, :]).then_inc(sched, 16)
                    sp.dma_start(grp_d[FRONT:FRONT + GROUPS, :],
                                 iota_d[0:GROUPS, :]).then_inc(sched, 16)
                    sp.wait_ge(sched, 32)
                with sp.Else():
                    sp.reg_mov(at_reg, 0)
                    with sp.Fori(0, GROUPS) as g:
                        first = sp.value_load(base_d[bass.ds(g, 1), :], min_val=0, max_val=N - 1)
                        count = sp.value_load(nwin_d[bass.ds(g, 1), :], min_val=1, max_val=WIN)
                        with sp.Fori(0, count) as w:
                            s = sp.snap(at_reg, min_val=0, max_val=GROUPS * WIN - 1)
                            sp.reg_mov(off_reg, first + w * P)
                            o = sp.snap(off_reg, min_val=0, max_val=N - 1)
                            sp.dma_start(off_d[bass.ds(s + FRONT, 1), :],
                                         iota_d[bass.ds(o, 1), :]).then_inc(sched, 16)
                            sp.dma_start(grp_d[bass.ds(s + FRONT, 1), :],
                                         iota_d[bass.ds(g, 1), :]).then_inc(sched, 16)
                            sp.reg_add(at_reg, at_reg, 1)
                            sp.wait_ge(sched, (s + 1) * 32)
                            sp.nop(nofuse=True)

        lag_of = {}

        def sweep(tag, kind, table=None, index_d=None):
            expand = kind in ("gat", "mix", "hgt")
            online = kind in ("gat", "hgt")
            R = {"sum": F, "sum_attr": 2 * F, "gat": 2, "mix": F + 1, "hgt": F + 1}[kind]
            width = {"sum": F, "sum_attr": F, "gat": F + 2, "mix": F + 2, "hgt": 2 * F}[kind]
            L = dict(onehot=0, turned=0, turn_copied=0, blocked=0, expanded=0, scored=1, weighed=2, diag_made=1, spread=1,
                     max_found=2, max_sent=2, shifted=2, exped=2, top_moved=2, factors=2, paid=2, summed_=2, added=3)
            if kind in ("sum", "sum_attr"):
                L.update(summed_=0, added=1)
            if kind == "mix":
                L.update(shifted=1, exped=1, weighed=2, gated=2, paid=3, summed_=3, added=4)
            S = {n: psem(f"{tag}_{n}") for n in L if expand or n in ("onehot", "summed_", "added")}
            if not online:
                for n in ("blocked", "diag_made", "spread", "max_found", "max_sent", "top_moved", "factors"):
                    S.pop(n, None)
            chain_s, chain_v = psem(f"{tag}_score_step"), psem(f"{tag}_add_step")
            s_idx = [psem(f"{tag}_idx{k}") for k in range(RING)]
            s_rows = [psem(f"{tag}_rows{k}") for k in range(RING)]
            s_dwin = [psem(f"{tag}_dwin{k}") for k in range(RING)] if expand else None
            s_attr = [psem(f"{tag}_attr{k}") for k in range(RING)] if kind == "sum_attr" else None
            s_stash = [psem(f"{tag}_stash{k}") for k in range(RING)] if kind == "gat" else None
            pool_cleared, dve_cleared = psem(f"{tag}_pool_cleared"), psem(f"{tag}_dve_cleared")
            dw = 4 if kind == "mix" else F + 2
            last_rows = "scored" if kind == "gat" else "paid" if kind in ("mix", "hgt") else "summed_"

            def rowv(k):
                flat = rows[k][:].rearrange("p c f -> p (c f)")
                if kind in ("sum", "sum_attr"):
                    return rows[k][:, :, 0:F]
                return flat[:, 0:C * width].rearrange("p (c f) -> p c f", c=C)

            turn_b = [bank[0], bank[1]]
            exp_b = [bank[2], bank[3]]
            spread_b, max_b = bank[4], bank[5]
            sum_b = [bank[6], bank[7]]

            def w(eng, t, mine, name, ring=0):
                eng.wait_ge(S[name], t - L[mine] + L[name] + 1 + PRIME - ring)

            def prime(eng, *names):
                for n in names:
                    if n in S:
                        eng.sem_inc(S[n], PRIME)

            def steps_of(eng, i, array, back, count, hi):
                vals = []
                for c in range(count):
                    vals.append(eng.value_load(array[bass.ds(i * RING + (FRONT - back + c), 1), :], min_val=0, max_val=hi))
                return vals

            block = ctx2.enter_context(nc.Block())

            def iters(eng):
                return eng.value_load(iters_d[0:1, 0:1], min_val=1, max_val=CAP // RING - 2)

            @block.sync
            def _(sp):
                sp.wait_ge(pool_cleared, 1)
                sp.wait_ge(dve_cleared, 1)
                for k in range(RING):
                    if expand:
                        sp.dma_start(dwin[k][:, 0:dw], (stat_d if kind == "mix" else dsttab_d)[0:P, :]).then_inc(s_dwin[k], 16)
                    if kind == "mix":
                        sp.dma_start(rowv(k), stash_d[k].rearrange("p (c f) -> p c f", c=C)).then_inc(s_rows[k], 16)
                    if kind == "gat":
                        sp.wait_ge(s_rows[k], 16)
                        sp.dma_start(stash_d[GROUPS].rearrange("p (c f) -> p c f", c=C), rowv(k)).then_inc(s_stash[k], 16)
                        sp.wait_ge(s_stash[k], 16)
                for k in range(RING):
                    if expand:
                        sp.wait_ge(s_dwin[k], 16)
                    if kind == "mix":
                        sp.wait_ge(s_rows[k], 16)
                n = iters(sp)
                attr_reg = sp.alloc_register(f"{tag}_attr_at")
                with sp.Fori(0, n) as i:
                    cols_ = steps_of(sp, i, grp_d, 3 if kind == "gat" else 0, RING + (3 if kind == "gat" else 0), GROUPS)
                    offs = steps_of(sp, i, off_d, 0, RING, N) if expand else None
                    for u in range(RING):
                        t = i * RING + u
                        col = cols_[u + (3 if kind == "gat" else 0)]
                        g = col
                        sp.wait_ge(S[last_rows], t + L[last_rows] + 1 + PRIME - RING)
                        sp.nop(nofuse=True)
                        if kind != "mix":
                            sp.dma_start(idx[u][:], index_d[bass.ds(g, 1), :, :].rearrange("g p c -> (g p) c")).then_inc(s_idx[u], 16)
                        else:
                            sp.dma_start(rowv(u), stash_d[bass.ds(g, 1), :, :].rearrange("g p (c f) -> (g p) c f", c=C)).then_inc(s_rows[u], 16)
                        if kind == "sum_attr":
                            sp.reg_alu(attr_reg, g * GE, TAIL, ALU.min)
                            e = sp.snap(attr_reg, min_val=0, max_val=TAIL)
                            sp.dma_start(rows[u][:, :, F:2 * F],
                                         io["edge_attr_64"][bass.ds(e, GE), :].rearrange("(p c) f -> p c f", c=C)).then_inc(s_attr[u], 16)
                        if expand:
                            sp.wait_ge(S["expanded"], t + 1 + PRIME - RING)
                            sp.nop(nofuse=True)
                            sp.dma_start(dwin[u][:, 0:dw], (stat_d if kind == "mix" else dsttab_d)[bass.ds(offs[u], P), :]).then_inc(s_dwin[u], 16)
                        if kind == "gat":
                            k = (u - 3) % RING
                            gb = cols_[u]
                            sp.wait_ge(s_rows[k], (i - (1 if u < 3 else 0)) * 64 + 64 + 16)
                            sp.nop(nofuse=True)
                            sp.wait_ge(s_stash[k], i * 16 + 16)
                            sp.nop(nofuse=True)
                            sp.wait_ge(s_stash[u], i * 16 + (16 if u == 0 else 32))
                            sp.nop(nofuse=True)
                            sp.dma_start(stash_d[bass.ds(gb, 1), :, :].rearrange("g p (c f) -> (g p) c f", c=C), rowv(k)).then_inc(s_stash[k], 16)
                if kind == "gat":
                    for k in range(RING):
                        sp.wait_ge(s_stash[k], n * 16 + 16)
                        sp.nop(nofuse=True)
                        sp.nop(nofuse=True)
            @block.gpsimd
            def _(pool):
                if online:
                    nc.gpsimd.memset(top[0:R, :], -BIG)
                if expand:
                    for k in range(RING):
                        nc.gpsimd.memset(pay[k][:], 0.0)
                        nc.gpsimd.memset(gmax[k][:], 0.0)
                        nc.gpsimd.memset(factor[k][:], 1.0)
                nc.gpsimd.memset(small[:], 0.0).then_inc(pool_cleared, 1)
                if kind == "mix":
                    return
                pool.wait_ge(pool_cleared, 1)
                pool.wait_ge(dve_cleared, 1)
                for k in range(RING):
                    nc.gpsimd.dma_start(rowv(k), table[0:P * C, :].rearrange("(p c) f -> p c f", c=C)).then_inc(s_rows[k], 16)
                n = iters(pool)
                with pool.Fori(0, n) as i:
                    for u in range(RING):
                        t = i * RING + u
                        pool.wait_ge(s_idx[u], i * 16 + 16)
                        pool.wait_ge(S[last_rows], t + L[last_rows] + 1 + PRIME - RING)
                        pool.wait_ge(s_rows[u], i * 64 + 16)
                        if kind == "gat":
                            pool.wait_ge(s_stash[u], i * 16 + (16 if u == 0 else 32))
                        pool.nop(nofuse=True)
                        for c in range(C):
                            dst = rowv(u)[:, c, :]
                            nc.gpsimd.indirect_dma_start(
                                out=dst, out_offset=None, in_=table,
                                in_offset=bass.IndirectOffsetOnAxis(ap=idx[u][:, c:c + 1].bitcast(U32), axis=0)).then_inc(s_rows[u], 16)

            def rows_in(eng, i, u, lag):
                k = (u - lag) % RING
                back = 1 if u < lag else 0
                per = 16 if kind == "mix" else 64
                eng.wait_ge(s_rows[k], (i - back) * per + per + 16)

            @block.tensor
            def _(pe):
                prime(pe, "turned", "expanded", "spread", "max_sent", "summed_")
                pe.wait_ge(pool_cleared, 1)
                pe.wait_ge(dve_cleared, 1)
                n = iters(pe)
                with pe.Fori(0, n) as i:
                    for u in range(RING):
                        t = i * RING + u
                        if online:
                            k = (u - 2) % RING
                            w(pe, t, "max_sent", "max_found")
                            w(pe, t, "max_sent", "shifted", 1)
                            w(pe, t, "max_sent", "top_moved", 1)
                            for c in range(C):
                                pe.matmul(max_b[:, 128 + c:129 + c], turned[k][:, c * P:(c + 1) * P], gmax[k][:, 0:1], start=True, stop=True)
                            lhs = gmax[k][:, 0:2] if kind == "gat" else gmax[k][:, 0:1].to_broadcast([P, R])
                            pe.matmul(max_b[0:R, 0:P], lhs, ident[:], start=True, stop=True).then_inc(S["max_sent"], 1)
                        if expand:
                            w(pe, t, "turned", "onehot")
                            w(pe, t, "turned", "turn_copied", 2)
                            if online:
                                w(pe, t, "turned", "blocked", 2)
                            for c in range(C):
                                mm = pe.transpose(turn_b[u % 2][:, c * P:(c + 1) * P], onehot[u][:, c, :], ident[:])
                            mm.then_inc(S["turned"], 1)
                        if online:
                            k = (u - 1) % RING
                            w(pe, t, "spread", "diag_made")
                            w(pe, t, "spread", "max_found", 1)
                            for c in range(C):
                                mm = pe.matmul(spread_b[:, c * P:(c + 1) * P], onehot[k][:, c, :], diag[k % 2][:, c, :], start=True, stop=True)
                            mm.then_inc(S["spread"], 1)
                        if expand:
                            w(pe, t, "expanded", "turn_copied")
                            pe.wait_ge(s_dwin[u], i * 16 + 32)
                            w(pe, t, "expanded", "shifted" if kind == "mix" else "scored", 2)
                            if kind == "mix":
                                w(pe, t, "expanded", "weighed", 2)
                            for c in range(C):
                                mm = pe.matmul(exp_b[u % 2][:, c * dw:(c + 1) * dw], turned[u][:, c * P:(c + 1) * P],
                                               dwin[u][:, 0:dw], start=True, stop=True)
                            mm.then_inc(S["expanded"], 1)
                        lag = L["summed_"]
                        k = (u - lag) % RING
                        w(pe, t, "summed_", "paid" if expand and kind != "gat" else "exped" if kind == "gat" else "onehot")
                        w(pe, t, "summed_", "added", 2)
                        if kind == "gat":
                            pass
                        elif not expand:
                            rows_in(pe, i, u, 0)
                            if kind == "sum_attr":
                                pe.wait_ge(s_attr[u], i * 16 + 16)
                        for c in range(C):
                            if kind == "sum":
                                lhs = rows[k][:, c, 0:F]
                            elif kind == "sum_attr":
                                lhs = rows[k][:, c, :]
                            else:
                                lhs = pay[k][:, c, 0:R]
                            mm = pe.matmul(sum_b[k % 2][0:R, 0:P], lhs, onehot[k][:, c, :], start=c == 0, stop=c == C - 1)
                        mm.then_inc(S["summed_"], 1)

            @block.scalar
            def _(act):
                prime(act, "turn_copied", "blocked", "diag_made", "exped", "factors")
                if kind == "mix":
                    prime(act, "gated")
                if not expand:
                    return
                act.wait_ge(pool_cleared, 1)
                act.wait_ge(dve_cleared, 1)
                n = iters(act)
                with act.Fori(0, n) as i:
                    for u in range(RING):
                        t = i * RING + u
                        w(act, t, "turn_copied", "turned")
                        w(act, t, "turn_copied", "summed_", RING)
                        nc.scalar.copy(turned[u], turn_b[u % 2][:, :]).then_inc(S["turn_copied"], 1)
                        if online:
                            w(act, t, "blocked", "max_found", RING)
                            nc.scalar.activation(block_[u], turn_b[u % 2][:, :], ACT.Copy, bias=-BIG, scale=BIG).then_inc(S["blocked"], 1)
                            k = (u - 1) % RING
                            w(act, t, "diag_made", "scored")
                            w(act, t, "diag_made", "spread", 2)
                            for c in range(C):
                                last = nc.scalar.mul(diag[k % 2][:, c, :], ident[:], score[k][:, c:c + 1])
                            last.then_inc(S["diag_made"], 1)
                            k = (u - 2) % RING
                            w(act, t, "exped", "shifted")
                            w(act, t, "exped", "summed_", RING)
                            if kind == "gat":
                                nc.scalar.activation(pay[k][:, :, 0], shift[k], ACT.Exp)
                                nc.scalar.activation(pay[k][:, :, 1], cosine[k], ACT.Exp).then_inc(S["exped"], 1)
                            else:
                                nc.scalar.activation(pay[k][:, :, F], shift[k], ACT.Exp).then_inc(S["exped"], 1)
                            w(act, t, "factors", "top_moved")
                            w(act, t, "factors", "added", RING)
                            nc.scalar.activation(factor[k][0:R, :], drop[k % 2][0:R, :], ACT.Exp).then_inc(S["factors"], 1)
                        else:
                            k = (u - 1) % RING
                            w(act, t, "exped", "shifted")
                            nc.scalar.activation(shift[k], shift[k], ACT.Exp).then_inc(S["exped"], 1)
                            k = (u - 2) % RING
                            w(act, t, "gated", "weighed")
                            w(act, t, "gated", "summed_", RING)
                            nc.scalar.activation(pay[k][:, :, F], score[k], ACT.Exp).then_inc(S["gated"], 1)

            @block.vector
            def _(dve):
                prime(dve, "onehot", "scored", "weighed", "max_found", "shifted", "top_moved", "paid", "added")
                V = nc.vector
                for b in bank:
                    V.memset(b[:], 0.0)
                V.memset(acc[0:R, :], 0.0)
                if online:
                    V.memset(logit[:], 0.0)
                    V.memset(ecos[:], 0.0)
                V.memset(work[:], 0.0).then_inc(dve_cleared, 1)
                dve.wait_ge(pool_cleared, 1)
                dve.wait_ge(dve_cleared, 1)
                n = iters(dve)
                back = L["added"]
                with dve.Fori(0, n) as i:
                    offs = steps_of(dve, i, off_d, back, RING + back, N)
                    cback = 1 if expand else 0
                    cols_ = steps_of(dve, i, grp_d, cback, RING + cback, GROUPS)
                    cs, cv = [0], [0]

                    def at_s(u, n_, per):
                        return (i * RING + u) * per + n_

                    for u in range(RING):
                        t = i * RING + u
                        if online:
                            k = (u - 2) % RING
                            w(dve, t, "max_found", "spread")
                            w(dve, t, "max_found", "blocked")
                            dve.nop(nofuse=True)
                            V.tensor_tensor_reduce(out=block_[k], in0=spread_b[:, :], in1=block_[k], scale=1.0, scalar=-BIG,
                                                   op0=ALU.add, op1=ALU.max, accum_out=gmax[k][:, 0:1]).then_inc(S["max_found"], 1)
                        w(dve, t, "onehot", "summed_", RING)
                        V.tensor_tensor(onehot[u], iota16[:, bass.ds(offs[u + back], P)].unsqueeze(1).to_broadcast([P, C, P]),
                                        dstf[:, bass.ds(cols_[u + cback] * C, C)].unsqueeze(2).to_broadcast([P, C, P]),
                                        ALU.is_equal).then_inc(S["onehot"], 1)
                        if kind in ("gat", "hgt"):
                            k = (u - 1) % RING
                            ex = exp_b[k % 2][:, 0:C * dw].rearrange("p (c f) -> p c f", c=C)
                            w(dve, t, "scored", "expanded")
                            w(dve, t, "scored", "exped", RING)
                            rows_in(dve, i, u, 1)
                            per = 7 if kind == "gat" else 1
                            c0 = at_s(u, 0, per)
                            V.tensor_tensor(prod[:], rowv(k)[:, :, 0:F], ex[:, :, 0:F], ALU.mult).then_inc(chain_s, 1)
                            dve.wait_ge(chain_s, c0 + 1)
                            if kind == "hgt":
                                V.tensor_reduce(score[k], prod[:], AX.X, ALU.add).then_inc(S["scored"], 1)
                            else:
                                V.tensor_reduce(cosine[k], prod[:], AX.X, ALU.add).then_inc(chain_s, 1)
                                V.tensor_tensor(score[k], rowv(k)[:, :, F], ex[:, :, F], ALU.add).then_inc(chain_s, 1)
                                dve.wait_ge(chain_s, c0 + 2)
                                V.tensor_tensor(cosine[k], cosine[k], rowv(k)[:, :, F + 1], ALU.mult).then_inc(chain_s, 1)
                                dve.wait_ge(chain_s, c0 + 3)
                                V.scalar_tensor_tensor(score[k], score[k], SLOPE, score[k], ALU.mult, ALU.max).then_inc(chain_s, 1)
                                col = cols_[u] * C
                                dve.wait_ge(chain_s, c0 + 4)
                                V.tensor_tensor(ecos[:, bass.ds(col, C)], ecos[:, bass.ds(col, C)], cosine[k], ALU.add).then_inc(chain_s, 1)
                                dve.wait_ge(chain_s, c0 + 5)
                                V.tensor_tensor(score[k], score[k], ex[:, :, F + 1], ALU.mult).then_inc(chain_s, 1)
                                dve.wait_ge(chain_s, c0 + 7)
                                V.tensor_tensor(logit[:, bass.ds(col, C)], logit[:, bass.ds(col, C)], score[k], ALU.add).then_inc(S["scored"], 1)
                        if online:
                            k = (u - 2) % RING
                            w(dve, t, "shifted", "max_sent")
                            w(dve, t, "shifted", "exped", RING)
                            V.tensor_tensor(shift[k], score[k], max_b[:, 128:128 + C], ALU.subtract).then_inc(S["shifted"], 1)
                            o = offs[u - 2 + back]
                            c0 = (i * RING + u) * 3
                            w(dve, t, "top_moved", "factors", 2)
                            w(dve, t, "top_moved", "top_moved", 1)
                            V.tensor_tensor(drop[k % 2][0:R, 0:P], top[0:R, bass.ds(o, P)], max_b[0:R, 0:P], ALU.subtract).then_inc(chain_v, 1)
                            V.tensor_tensor(top[0:R, bass.ds(o, P)], top[0:R, bass.ds(o, P)], max_b[0:R, 0:P], ALU.max).then_inc(chain_v, 1)
                            dve.wait_ge(chain_v, c0 + 1)
                            V.tensor_scalar(drop[k % 2][0:R, P:2 * P], drop[k % 2][0:R, 0:P], -1.0, 0.0, ALU.mult, ALU.min).then_inc(chain_v, 1)
                            dve.wait_ge(chain_v, c0 + 3)
                            V.tensor_scalar(drop[k % 2][0:R, 0:P], drop[k % 2][0:R, 0:P], 0.0, None, ALU.min).then_inc(S["top_moved"], 1)
                            if kind == "hgt":
                                w(dve, t, "paid", "exped")
                                w(dve, t, "paid", "summed_", RING)
                                V.tensor_tensor(pay[k][:, :, 0:F], rowv(k)[:, :, F:2 * F], pay[k][:, :, F:F + 1].to_broadcast([P, C, F]),
                                                ALU.mult).then_inc(S["paid"], 1)
                        if kind == "mix":
                            k = (u - 1) % RING
                            ex = exp_b[k % 2][:, 0:C * dw].rearrange("p (c f) -> p c f", c=C)
                            c0 = (i * RING + u) * 3
                            w(dve, t, "shifted", "expanded")
                            V.tensor_tensor(shift[k], logit[:, bass.ds(cols_[u] * C, C)], ex[:, :, 0], ALU.subtract).then_inc(chain_s, 1)
                            V.tensor_copy(gcol[k], gate[:, bass.ds(cols_[u] * C, C)]).then_inc(chain_s, 1)
                            V.tensor_tensor(ccol[k], ecos[:, bass.ds(cols_[u] * C, C)], ex[:, :, 2], ALU.mult).then_inc(chain_s, 1)
                            dve.wait_ge(chain_s, c0 + 1)
                            V.tensor_tensor(shift[k], shift[k], ex[:, :, 3], ALU.mult).then_inc(S["shifted"], 1)
                            k = (u - 2) % RING
                            exk = exp_b[k % 2][:, 0:C * dw].rearrange("p (c f) -> p c f", c=C)
                            w(dve, t, "weighed", "exped")
                            w(dve, t, "weighed", "gated", RING)
                            V.tensor_tensor(score[k], shift[k], exk[:, :, 1], ALU.mult).then_inc(chain_v, 1)
                            v0 = (i * RING + u) * 2
                            dve.wait_ge(chain_v, v0 + 1)
                            V.tensor_tensor(score[k], score[k], ccol[k], ALU.add).then_inc(chain_v, 1)
                            dve.wait_ge(chain_v, v0 + 2)
                            V.tensor_tensor(score[k], score[k], gcol[k], ALU.mult).then_inc(S["weighed"], 1)
                            k = (u - 3) % RING
                            rows_in(dve, i, u, 3)
                            w(dve, t, "paid", "gated")
                            w(dve, t, "paid", "summed_", RING)
                            V.tensor_tensor(pay[k][:, :, 0:F], rowv(k)[:, :, 0:F], pay[k][:, :, F:F + 1].to_broadcast([P, C, F]),
                                            ALU.mult).then_inc(S["paid"], 1)
                        lag = L["added"]
                        k = (u - lag) % RING
                        o = offs[u]
                        total_ = acc[0:R, bass.ds(o, P)]
                        w(dve, t, "added", "summed_")
                        w(dve, t, "added", "added", 1)
                        if online:
                            w(dve, t, "added", "factors")
                            v1 = (i * RING + u) * 2
                            V.tensor_tensor(scaled[0:R, 0:P], sum_b[k % 2][0:R, 0:P], factor[k][0:R, P:2 * P], ALU.mult).then_inc(chain_a, 1)
                            V.tensor_tensor(scaled[0:R, P:2 * P], total_, factor[k][0:R, 0:P], ALU.mult).then_inc(chain_a, 1)
                            dve.wait_ge(chain_a, v1 + 2)
                            V.tensor_tensor(total_, scaled[0:R, 0:P], scaled[0:R, P:2 * P], ALU.add).then_inc(S["added"], 1)
                        else:
                            V.tensor_tensor(total_, total_, sum_b[k % 2][0:R, 0:P], ALU.add).then_inc(S["added"], 1)

        def bass_const(eng, v):
            return eng.snap(eng.to_reg(v), min_val=v, max_val=v)

        gmax = [sb(f"gmax{k}", [P, 2]) for k in range(RING)]
        score = [small[:, 64 + 4 * k:68 + 4 * k] for k in range(RING)]
        cosine = [small[:, 96 + 4 * k:100 + 4 * k] for k in range(RING)]
        shift = [small[:, 128 + 4 * k:132 + 4 * k] for k in range(RING)]
        gcol = [small[:, 160 + 4 * k:164 + 4 * k] for k in range(RING)]
        ccol = [small[:, 192 + 4 * k:196 + 4 * k] for k in range(RING)]
        prod = sb("prod", [P, C, F])
        drop = [sb(f"drop{k}", [P, 2 * P]) for k in range(2)]
        factor = [sb(f"factor{k}", [P, 2 * P]) for k in range(RING)]
        scaled = sb("scaled", [P, 2 * P])
        chain_a = None
        ctx2 = ExitStack()

        def run_sweep(*a, **kw):
            nonlocal chain_a, ctx2
            with ExitStack() as c2:
                ctx2 = c2
                chain_a = psem(f"{a[0]}_sum_step")
                sweep(*a, **kw)
            next_phase()

        def chunk(x, it):
            return x[bass.ds(it * CH, CH), :].rearrange("(p j) f -> p j f", j=J)

        def by_j(x, rows_, it):
            return x[0:rows_, bass.ds(it * CH, CH)].rearrange("r (p j) -> r j p", j=J)

        def area(k, at_, size):
            return work[0:k, at_:at_ + size]

        def jf(ap, f=F):
            return ap.rearrange("p (j f) -> p j f", j=J)

        def jp(ap):
            return ap.rearrange("r (j p) -> r j p", j=J)

        x_t, more_t, y_t, sq_t = (jf(area(Q, k * 256, 256)) for k in range(4))
        m1, m2, m3 = (area(Q, 1024 + 4 * k, 4) for k in range(3))
        t_a, t_b, t_c = (area(P, 1100 + 500 * k, 500) for k in range(3))
        s_row, d_row = (jf(area(Q, 2600 + 264 * k, 264), F + 2) for k in range(2))
        typed_t = area(Q, 3200, 1024).rearrange("p (j t f) -> p j t f", j=J, t=NT)
        typ_i, typ_f = area(Q, 4300, 4).bitcast(I32), area(Q, 4304, 4)
        masks = [area(Q, 4308 + 4 * t, 4) for t in range(NT)]

        def wide(v, f=F):
            return v.unsqueeze(2).to_broadcast([Q, J, f])

        def linker(dve, signal, it, per):
            count = [0]

            def link(ins):
                count[0] += 1
                ins.then_inc(signal, 1)
                dve.wait_ge(signal, it * per + count[0])
                assert count[0] <= per

            link.count = count
            return link

        def layernorm(dve, link, y, S, it):
            V = nc.vector
            link(V.tensor_reduce(m1, y, AX.X, ALU.add))
            link(V.tensor_scalar(m1, m1, 1.0 / F, None, ALU.mult))
            link(V.tensor_tensor(y, y, wide(m1), ALU.subtract))
            link(V.tensor_tensor(sq_t, y, y, ALU.mult))
            link(V.tensor_reduce(m2, sq_t, AX.X, ALU.add))
            V.tensor_scalar(m2, m2, 1.0 / F, LN_EPS, ALU.mult, ALU.add).then_inc(S["var_ready"], 1)
            dve.wait_ge(S["std_ready"], it + 1)
            link(V.reciprocal(m2, m3))
            V.tensor_tensor(y, y, wide(m2), ALU.mult).then_inc(S["y_ready"], 1)

        LN_LINKS = 6

        def deviation(act, S, it):
            act.wait_ge(S["var_ready"], it + 1)
            nc.scalar.activation(m3, m2, ACT.Sqrt).then_inc(S["std_ready"], 1)

        def node_mlp(tag, x_in, x_out, w1, b1, w2, b2, k1, m1_, source, extra=None):
            names = ["x_in", "x_turned", "h_ready", "hidden", "relu_ready", "mlp_out", "x_used", "y_ready", "y_stored", "var_ready", "std_ready", "link"]
            S = {n: psem(f"{tag}_{n}") for n in names}
            per = 1 + (1 if extra is not None else 0) + 1 + LN_LINKS - 1
            loads_n = 32 if extra is not None else 16
            with nc.Block() as block:
                @block.sync
                def _(sp):
                    def load(at_it):
                        sp.dma_start(x_t, chunk(x_in, at_it)).then_inc(S["x_in"], 16)
                        if extra is not None:
                            sp.dma_start(more_t, chunk(extra, at_it)).then_inc(S["x_in"], 16)

                    load(0)
                    sp.dma_start(trash_d[0:Q, 0:256].rearrange("p (j f) -> p j f", j=J), y_t).then_inc(S["y_stored"], 16)
                    with sp.Fori(0, CHUNKS) as it:
                        sp.wait_ge(S["x_used"], it + 1)
                        sp.nop(nofuse=True)
                        nxt = ahead(sp, it)
                        load(nxt)
                        sp.wait_ge(S["y_ready"], it + 1)
                        sp.nop(nofuse=True)
                        sp.dma_start(chunk(x_out, it), y_t).then_inc(S["y_stored"], 16)
                    sp.wait_ge(S["y_stored"], 16 * (CHUNKS + 1))
                    sp.wait_ge(S["x_in"], loads_n * (CHUNKS + 1))

                @block.tensor
                def _(pe):
                    with pe.Fori(0, CHUNKS) as it:
                        if source != "sums":
                            pe.wait_ge(S["x_in"], it * loads_n + loads_n)
                            for j in range(J):
                                mm = pe.matmul(bank[0][0:F, j * Q:(j + 1) * Q], x_t[:, j, :], ident[0:Q, 0:Q], start=True, stop=True)
                            mm.then_inc(S["x_turned"], 1)
                        pe.wait_ge(S["h_ready"], it + 1)
                        pe.nop(nofuse=True)
                        pe.matmul(bank[1][0:m1_, 0:CH], wt(w1, k1), t_a[0:k1, :], start=True, stop=True).then_inc(S["hidden"], 1)
                        pe.wait_ge(S["relu_ready"], it + 1)
                        for j in range(J):
                            mm = pe.matmul(bank[2][0:Q, j * F:(j + 1) * F], t_b[0:m1_, j * Q:(j + 1) * Q], wt(w2, m1_), start=True, stop=True)
                        mm.then_inc(S["mlp_out"], 1)

                @block.scalar
                def _(act):
                    with act.Fori(0, CHUNKS) as it:
                        act.wait_ge(S["hidden"], it + 1)
                        nc.scalar.activation(t_b[0:m1_, :], bank[1][0:m1_, 0:CH], ACT.Relu, bias=bs(b1, m1_)).then_inc(S["relu_ready"], 1)
                        deviation(act, S, it)

                @block.vector
                def _(dve):
                    V = nc.vector
                    with dve.Fori(0, CHUNKS) as it:
                        link = linker(dve, S["link"], it, per)
                        if source == "x_and_sums":
                            dve.wait_ge(S["x_turned"], it + 1)
                            V.tensor_tensor(jp(t_a[0:F, :]), jp(bank[0][0:F, 0:CH]), by_j(acc, F, it), ALU.add).then_inc(S["h_ready"], 1)
                        elif source == "sums":
                            V.tensor_copy(jp(t_a[0:k1, :]), by_j(acc, k1, it)).then_inc(S["h_ready"], 1)
                        else:
                            dve.wait_ge(S["x_turned"], it + 1)
                            V.tensor_copy(t_a[0:F, :], bank[0][0:F, 0:CH]).then_inc(S["h_ready"], 1)
                        dve.wait_ge(S["mlp_out"], it + 1)
                        dve.wait_ge(S["y_stored"], it * 16 + 16)
                        dve.wait_ge(S["x_in"], it * loads_n + loads_n)
                        link(V.tensor_tensor(y_t, jf(bank[2][0:Q, 0:256]), bs(b2, Q).unsqueeze(1).to_broadcast([Q, J, F]), ALU.add))
                        if extra is not None:
                            link(V.tensor_tensor(y_t, y_t, more_t, ALU.add))
                        V.tensor_tensor(y_t, y_t, x_t, ALU.add).then_inc(S["x_used"], 1)
                        dve.wait_ge(S["x_used"], it + 1)
                        layernorm(dve, link, y_t, S, it)
                        dve.wait_ge(S["y_ready"], it + 1)
                        assert link.count[0] == per

        def ahead(eng, it):
            key = str(eng.engine)
            if key not in next_reg:
                next_reg[key] = eng.alloc_register("next_chunk")
            eng.reg_alu(next_reg[key], it + 1, CHUNKS - 1, ALU.min)
            return eng.snap(next_reg[key], min_val=0, max_val=CHUNKS - 1)

        next_reg = {}

        def node_gat_tables(tag, x_in, layer):
            S = {n: psem(f"{tag}_{n}") for n in ("x_in", "x_turned", "h_ready", "logits", "x_used", "rows_ready", "rows_stored", "var_ready", "std_ready", "link")}
            per = 6
            with nc.Block() as block:
                @block.sync
                def _(sp):
                    sp.dma_start(x_t, chunk(x_in, 0)).then_inc(S["x_in"], 16)
                    sp.wait_ge(S["rows_ready"], 1)
                    sp.dma_start(trash_d[0:Q, :].rearrange("p (j f) -> p j f", j=J), s_row).then_inc(S["rows_stored"], 16)
                    sp.dma_start(trash_d[0:Q, :].rearrange("p (j f) -> p j f", j=J), s_row).then_inc(S["rows_stored"], 16) if False else None
                    with sp.Fori(0, CHUNKS) as it:
                        sp.wait_ge(S["x_used"], it + 1)
                        sp.nop(nofuse=True)
                        sp.dma_start(x_t, chunk(x_in, ahead(sp, it))).then_inc(S["x_in"], 16)
                        sp.wait_ge(S["rows_ready"], it + 2)
                        sp.nop(nofuse=True)
                        sp.dma_start(chunk(srctab_d, it), s_row).then_inc(S["rows_stored"], 16)
                        sp.dma_start(chunk(dsttab_d, it), d_row).then_inc(S["rows_stored"], 16)
                    sp.wait_ge(S["rows_stored"], 32 * CHUNKS + 16)
                    sp.wait_ge(S["x_in"], 16 * (CHUNKS + 1))

                @block.tensor
                def _(pe):
                    with pe.Fori(0, CHUNKS) as it:
                        pe.wait_ge(S["x_in"], it * 16 + 16)
                        for j in range(J):
                            mm = pe.matmul(bank[0][0:F, j * Q:(j + 1) * Q], x_t[:, j, :], ident[0:Q, 0:Q], start=True, stop=True)
                        mm.then_inc(S["x_turned"], 1)
                        pe.wait_ge(S["h_ready"], it + 1)
                        for j in range(J):
                            mm = pe.matmul(bank[1][0:Q, 2 * j:2 * j + 2], t_a[0:F, j * Q:(j + 1) * Q], wt(f"U{layer}"), start=True, stop=True)
                        mm.then_inc(S["logits"], 1)

                @block.scalar
                def _(act):
                    with act.Fori(0, CHUNKS) as it:
                        deviation(act, S, it)

                @block.vector
                def _(dve):
                    V = nc.vector
                    V.memset(work[0:Q, 2600:2600 + 528], 1.0).then_inc(S["rows_ready"], 1)
                    dve.wait_ge(S["rows_ready"], 1)
                    with dve.Fori(0, CHUNKS) as it:
                        link = linker(dve, S["link"], it, per)
                        dve.wait_ge(S["x_turned"], it + 1)
                        V.tensor_copy(t_a[0:F, :], bank[0][0:F, 0:CH]).then_inc(S["h_ready"], 1)
                        link(V.tensor_tensor(sq_t, x_t, x_t, ALU.mult))
                        link(V.tensor_reduce(m1, sq_t, AX.X, ALU.add))
                        V.tensor_scalar(m2, m1, COS_EPS2, None, ALU.max).then_inc(S["var_ready"], 1)
                        dve.wait_ge(S["std_ready"], it + 1)
                        link(V.reciprocal(m1, m3))
                        dve.wait_ge(S["rows_stored"], it * 32 + 16)
                        link(V.tensor_copy(s_row[:, :, 0:F], x_t))
                        link(V.tensor_copy(s_row[:, :, F + 1], m1))
                        V.tensor_tensor(d_row[:, :, 0:F], x_t, wide(m1), ALU.mult).then_inc(S["x_used"], 1)
                        dve.wait_ge(S["logits"], it + 1)
                        lg = jf(bank[1][0:Q, 0:2 * J], 2)
                        link(V.tensor_copy(s_row[:, :, F], lg[:, :, 1]))
                        V.tensor_copy(d_row[:, :, F], lg[:, :, 0]).then_inc(S["rows_ready"], 1)
                        dve.wait_ge(S["rows_ready"], it + 2)
                        assert link.count[0] == per

        def node_stats(tag, layer):
            S = {n: psem(f"{tag}_{n}") for n in ("rows_copied", "stats_turned", "stats_ready", "stats_stored", "link", "cos_exped")}
            stat_t = jf(area(Q, 2600, 16), 4)
            mix = wts[0:Q, wcols["mix"][0] + 2 * layer:wcols["mix"][0] + 2 * layer + 2]
            per = 4
            with nc.Block() as block:
                @block.sync
                def _(sp):
                    sp.wait_ge(S["stats_ready"], 1)
                    sp.dma_start(trash_d[0:Q, 0:16].rearrange("p (j f) -> p j f", j=J), stat_t).then_inc(S["stats_stored"], 16)
                    with sp.Fori(0, CHUNKS) as it:
                        sp.wait_ge(S["stats_ready"], it + 2)
                        sp.nop(nofuse=True)
                        sp.dma_start(chunk(stat_d, it), stat_t).then_inc(S["stats_stored"], 16)
                    sp.wait_ge(S["stats_stored"], 16 * CHUNKS + 16)

                @block.scalar
                def _(act):
                    nc.scalar.activation(ecos[:], ecos[:], ACT.Exp).then_inc(S["cos_exped"], 1)
                    act.wait_ge(S["cos_exped"], 1)

                @block.tensor
                def _(pe):
                    with pe.Fori(0, CHUNKS) as it:
                        pe.wait_ge(S["rows_copied"], it + 1)
                        for j in range(J):
                            pe.matmul(bank[0][0:Q, 4 * j:4 * j + 1], t_a[0:1, j * Q:(j + 1) * Q], ident[0:1, 0:1], start=True, stop=True)
                            mm = pe.matmul(bank[0][0:Q, 4 * j + 1:4 * j + 3], t_b[0:2, j * Q:(j + 1) * Q], ident[0:2, 0:2], start=True, stop=True)
                        mm.then_inc(S["stats_turned"], 1)

                @block.vector
                def _(dve):
                    V = nc.vector
                    V.memset(stat_t, 1.0).then_inc(S["stats_ready"], 1)
                    dve.wait_ge(S["stats_ready"], 1)
                    with dve.Fori(0, CHUNKS) as it:
                        link = linker(dve, S["link"], it, per)
                        link(V.tensor_copy(jp(t_a[0:1, :]), by_j(top, 1, it)))
                        V.tensor_copy(jp(t_b[0:2, :]), by_j(acc, 2, it)).then_inc(S["rows_copied"], 1)
                        dve.wait_ge(S["stats_turned"], it + 1)
                        dve.wait_ge(S["stats_stored"], it * 16 + 16)
                        ps = jf(bank[0][0:Q, 0:16], 4)
                        link(V.tensor_copy(stat_t[:, :, 0], ps[:, :, 0]))
                        link(V.tensor_scalar(stat_t[:, :, 1:3], ps[:, :, 1:3], SM_EPS, None, ALU.add))
                        link(V.reciprocal(stat_t[:, :, 1:3], stat_t[:, :, 1:3]))
                        V.tensor_tensor(stat_t[:, :, 1:3], stat_t[:, :, 1:3], mix.unsqueeze(1).to_broadcast([Q, J, 2]),
                                        ALU.mult).then_inc(S["stats_ready"], 1)
                        dve.wait_ge(S["stats_ready"], it + 2)
                        assert link.count[0] == per

        def node_gat_out(tag, layer, h_out, twice):
            S = {n: psem(f"{tag}_{n}") for n in ("h_ready", "out_ready", "low", "exped", "h_made", "h_stored", "link")}
            rounds = 2 if twice else 1
            per = 4 + 1 + (rounds - 1) * 2
            with nc.Block() as block:
                @block.sync
                def _(sp):
                    sp.dma_start(trash_d[0:Q, 0:256].rearrange("p (j f) -> p j f", j=J), y_t).then_inc(S["h_stored"], 16)
                    with sp.Fori(0, CHUNKS) as it:
                        sp.wait_ge(S["h_made"], it + 1)
                        sp.nop(nofuse=True)
                        sp.dma_start(chunk(h_out, it), y_t).then_inc(S["h_stored"], 16)
                    sp.wait_ge(S["h_stored"], 16 * CHUNKS + 16)

                @block.tensor
                def _(pe):
                    with pe.Fori(0, CHUNKS) as it:
                        pe.wait_ge(S["h_ready"], it + 1)
                        for j in range(J):
                            mm = pe.matmul(bank[0][0:Q, j * (F + 1):(j + 1) * (F + 1)], t_a[0:F + 1, j * Q:(j + 1) * Q],
                                           wt(f"G{layer}", F + 1), start=True, stop=True)
                        mm.then_inc(S["out_ready"], 1)

                @block.scalar
                def _(act):
                    with act.Fori(0, CHUNKS) as it:
                        for r in range(rounds):
                            act.wait_ge(S["low"], it * rounds + r + 1)
                            nc.scalar.activation(sq_t, sq_t, ACT.Exp).then_inc(S["exped"], 1)

                @block.vector
                def _(dve):
                    V = nc.vector
                    with dve.Fori(0, CHUNKS) as it:
                        link = linker(dve, S["link"], it, per)
                        V.tensor_copy(jp(t_a[0:F + 1, :]), by_j(acc, F + 1, it)).then_inc(S["h_ready"], 1)
                        dve.wait_ge(S["out_ready"], it + 1)
                        ps = jf(bank[0][0:Q, 0:J * (F + 1)], F + 1)
                        link(V.tensor_scalar(m1, ps[:, :, F], SM_EPS, None, ALU.add))
                        link(V.reciprocal(m1, m1))
                        dve.wait_ge(S["h_stored"], it * 16 + 16)
                        link(V.tensor_tensor(y_t, ps[:, :, 0:F], wide(m1), ALU.mult))
                        link(V.tensor_tensor(y_t, y_t, bs(f"bg{layer}", Q).unsqueeze(1).to_broadcast([Q, J, F]), ALU.add))
                        for r in range(rounds):
                            V.tensor_scalar(sq_t, y_t, 0.0, None, ALU.min).then_inc(S["low"], 1)
                            link(V.tensor_scalar(y_t, y_t, 0.0, None, ALU.max))
                            dve.wait_ge(S["exped"], it * rounds + r + 1)
                            last = V.scalar_tensor_tensor(y_t, sq_t, -1.0, y_t, ALU.add, ALU.add)
                            if r < rounds - 1:
                                link(last)
                        last.then_inc(S["h_made"], 1)
                        dve.wait_ge(S["h_made"], it + 1)
                        assert link.count[0] == per

        def typed(link, last, x):
            V = nc.vector
            for t in range(NT):
                ins = V.tensor_tensor(typed_t[:, :, t, :], x, wide(masks[t]), ALU.mult)
                if t < NT - 1:
                    link(ins)
            ins.then_inc(last, 1)

        def make_masks(link):
            V = nc.vector
            link(V.tensor_copy(typ_f, typ_i))
            for t in range(NT):
                link(V.tensor_scalar(masks[t], typ_f, float(t), None, ALU.is_equal))

        def turn_typed(pe, signal):
            for h in range(2):
                for j in range(J):
                    mm = pe.matmul(bank[h][:, j * Q:(j + 1) * Q], typed_t[:, j, 2 * h:2 * h + 2, :].rearrange("p t f -> p (t f)"),
                                   ident[0:Q, 0:Q], start=True, stop=True)
            mm.then_inc(signal, 1)

        types = io["node_type_4"].rearrange("(n j) -> n j", j=J)
        rel_t = top[0:Q, 0:NR * J * 2 * F].rearrange("p (r j f) -> p r j f", r=NR, j=J)

        def node_relations(tag, x_in):
            S = {n: psem(f"{tag}_{n}") for n in ("x_in", "typed", "turned", "half0", "half1", "kv", "k_copied", "v_copied", "q_ready",
                                                "rel_out", "att_copied", "msg_copied", "q_copied", "q_set", "stored", "link")}
            per = 5 + NT - 1
            wk, wq, wv = (wt(n, P).rearrange("p (h e) -> p h e", h=2) for n in ("K", "Qw", "V"))
            with nc.Block() as block:
                @block.sync
                def _(sp):
                    def load(at_it):
                        sp.dma_start(x_t, chunk(x_in, at_it)).then_inc(S["x_in"], 16)
                        sp.dma_start(typ_i, types[bass.ds(at_it * Q, Q), :]).then_inc(S["x_in"], 16)

                    load(0)
                    sp.wait_ge(S["q_set"], 1)
                    sp.dma_start(trash_d[0:Q, :].rearrange("p (j f) -> p j f", j=J), d_row).then_inc(S["stored"], 16)
                    with sp.Fori(0, CHUNKS) as it:
                        sp.wait_ge(S["typed"], it + 1)
                        sp.nop(nofuse=True)
                        load(ahead(sp, it))
                        sp.wait_ge(S["q_copied"], it + 1)
                        sp.nop(nofuse=True)
                        sp.dma_start(chunk(dsttab_d, it), d_row).then_inc(S["stored"], 16)
                        sp.wait_ge(S["att_copied"], it * J + J)
                        sp.wait_ge(S["msg_copied"], it * J + J)
                        sp.nop(nofuse=True)
                        for r in range(NR):
                            sp.dma_start(reltab_d[r * N:(r + 1) * N, :][bass.ds(it * CH, CH), :].rearrange("(p j) f -> p j f", j=J),
                                         rel_t[:, r, :, :]).then_inc(S["stored"], 16)
                    sp.wait_ge(S["stored"], 16 + (NR + 1) * 16 * CHUNKS)
                    sp.wait_ge(S["x_in"], 32 * (CHUNKS + 1))

                @block.tensor
                def _(pe):
                    with pe.Fori(0, CHUNKS) as it:
                        pe.wait_ge(S["typed"], it + 1)
                        turn_typed(pe, S["turned"])
                        pe.wait_ge(S["half0"], it + 1)
                        pe.wait_ge(S["half1"], it + 1)
                        for b, w_ in ((2, wk), (3, wv)):
                            for h in range(2):
                                mm = pe.matmul(bank[b][0:F, 0:CH], w_[:, h, :], (t_a, t_b)[h], start=h == 0, stop=h == 1)
                        mm.then_inc(S["kv"], 1)
                        for j in range(J):
                            for h in range(2):
                                mm = pe.matmul(bank[4][0:Q, j * F:(j + 1) * F], (t_a, t_b)[h][:, j * Q:(j + 1) * Q], wq[:, h, :],
                                               start=h == 0, stop=h == 1)
                        mm.then_inc(S["q_ready"], 1)
                        pe.wait_ge(S["k_copied"], it + 1)
                        pe.wait_ge(S["v_copied"], it + 1)
                        for j in range(J):
                            if j >= 2:
                                pe.wait_ge(S["att_copied"], it * J + j - 1)
                                pe.wait_ge(S["msg_copied"], it * J + j - 1)
                            pe.matmul(bank[5 + j % 2][0:Q, :], t_c[0:F, j * Q:(j + 1) * Q], wt("RA"), start=True, stop=True)
                            pe.matmul(bank[7 * (1 - j % 2)][0:Q, :], vT[0:F, j * Q:(j + 1) * Q], wt("RM"), start=True, stop=True).then_inc(S["rel_out"], 1)
                        pe.wait_ge(S["msg_copied"], it * J + J)

                @block.scalar
                def _(act):
                    with act.Fori(0, CHUNKS) as it:
                        act.wait_ge(S["turned"], it + 1)
                        nc.scalar.copy(t_a, bank[0][:, 0:CH]).then_inc(S["half0"], 1)
                        act.wait_ge(S["kv"], it + 1)
                        nc.scalar.copy(t_c[0:F, :], bank[2][0:F, 0:CH]).then_inc(S["k_copied"], 1)
                        act.wait_ge(S["stored"], it * (NR + 1) * 16 + 16)
                        for j in range(J):
                            act.wait_ge(S["rel_out"], it * J + j + 1)
                            nc.scalar.copy(rel_t[:, :, j, 0:F], bank[5 + j % 2][0:Q, :].rearrange("p (r d) -> p r d", r=NR)).then_inc(S["att_copied"], 1)

                @block.vector
                def _(dve):
                    V = nc.vector
                    V.memset(d_row, 1.0).then_inc(S["q_set"], 1)
                    dve.wait_ge(S["q_set"], 1)
                    with dve.Fori(0, CHUNKS) as it:
                        link = linker(dve, S["link"], it, per)
                        dve.wait_ge(S["x_in"], it * 32 + 32)
                        make_masks(link)
                        typed(link, S["typed"], x_t)
                        dve.wait_ge(S["turned"], it + 1)
                        V.tensor_copy(t_b, bank[1][:, 0:CH]).then_inc(S["half1"], 1)
                        dve.wait_ge(S["kv"], it + 1)
                        V.tensor_copy(vT[0:F, :], bank[3][0:F, 0:CH]).then_inc(S["v_copied"], 1)
                        dve.wait_ge(S["stored"], it * (NR + 1) * 16 + 16)
                        dve.wait_ge(S["q_ready"], it + 1)
                        V.tensor_copy(d_row[:, :, 0:F], jf(bank[4][0:Q, 0:256])).then_inc(S["q_copied"], 1)
                        for j in range(J):
                            dve.wait_ge(S["rel_out"], it * J + j + 1)
                            V.tensor_copy(rel_t[:, :, j, F:2 * F], bank[7 * (1 - j % 2)][0:Q, :].rearrange("p (r d) -> p r d", r=NR)).then_inc(S["msg_copied"], 1)
                        assert link.count[0] == per

        vT = area(P, 4400, 500)

        def node_last(tag, x_in):
            S = {n: psem(f"{tag}_{n}") for n in ("x_in", "h_ready", "sums_turned", "typed", "turned", "half0", "half1", "mapped", "x_used",
                                                "y_ready", "y_stored", "var_ready", "std_ready", "link")}
            per = 5 + 4 + NT - 1 + LN_LINKS
            wa = wt("A", P).rearrange("p (h e) -> p h e", h=2)
            with nc.Block() as block:
                @block.sync
                def _(sp):
                    def load(at_it):
                        sp.dma_start(x_t, chunk(x_in, at_it)).then_inc(S["x_in"], 16)
                        sp.dma_start(typ_i, types[bass.ds(at_it * Q, Q), :]).then_inc(S["x_in"], 16)

                    load(0)
                    sp.dma_start(trash_d[0:Q, 0:256].rearrange("p (j f) -> p j f", j=J), y_t).then_inc(S["y_stored"], 16)
                    with sp.Fori(0, CHUNKS) as it:
                        sp.wait_ge(S["x_used"], it + 1)
                        sp.nop(nofuse=True)
                        load(ahead(sp, it))
                        sp.wait_ge(S["y_ready"], it + 1)
                        sp.nop(nofuse=True)
                        sp.dma_start(chunk(out, it), y_t).then_inc(S["y_stored"], 16)
                    sp.wait_ge(S["y_stored"], 16 * (CHUNKS + 1))
                    sp.wait_ge(S["x_in"], 32 * (CHUNKS + 1))

                @block.tensor
                def _(pe):
                    with pe.Fori(0, CHUNKS) as it:
                        pe.wait_ge(S["h_ready"], it + 1)
                        for j in range(J):
                            mm = pe.matmul(bank[2][0:Q, j * (F + 1):(j + 1) * (F + 1)], t_c[0:F + 1, j * Q:(j + 1) * Q],
                                           ident[0:F + 1, 0:F + 1], start=True, stop=True)
                        mm.then_inc(S["sums_turned"], 1)
                        pe.wait_ge(S["typed"], it + 1)
                        turn_typed(pe, S["turned"])
                        pe.wait_ge(S["half0"], it + 1)
                        pe.wait_ge(S["half1"], it + 1)
                        for j in range(J):
                            for h in range(2):
                                mm = pe.matmul(bank[3][0:Q, j * F:(j + 1) * F], (t_a, t_b)[h][:, j * Q:(j + 1) * Q], wa[:, h, :],
                                               start=h == 0, stop=h == 1)
                        mm.then_inc(S["mapped"], 1)

                @block.scalar
                def _(act):
                    with act.Fori(0, CHUNKS) as it:
                        act.wait_ge(S["turned"], it + 1)
                        nc.scalar.copy(t_a, bank[0][:, 0:CH]).then_inc(S["half0"], 1)
                        deviation(act, S, it)

                @block.vector
                def _(dve):
                    V = nc.vector
                    with dve.Fori(0, CHUNKS) as it:
                        link = linker(dve, S["link"], it, per)
                        V.tensor_copy(jp(t_c[0:F + 1, :]), by_j(acc, F + 1, it)).then_inc(S["h_ready"], 1)
                        dve.wait_ge(S["x_in"], it * 32 + 32)
                        make_masks(link)
                        dve.wait_ge(S["sums_turned"], it + 1)
                        ps = jf(bank[2][0:Q, 0:J * (F + 1)], F + 1)
                        link(V.tensor_scalar(m1, ps[:, :, F], 0.0, None, ALU.is_equal))
                        link(V.tensor_tensor(m1, m1, ps[:, :, F], ALU.add))
                        link(V.reciprocal(m1, m1))
                        link(V.tensor_tensor(more_t, ps[:, :, 0:F], wide(m1), ALU.mult))
                        typed(link, S["typed"], more_t)
                        dve.wait_ge(S["turned"], it + 1)
                        V.tensor_copy(t_b, bank[1][:, 0:CH]).then_inc(S["half1"], 1)
                        dve.wait_ge(S["mapped"], it + 1)
                        dve.wait_ge(S["y_stored"], it * 16 + 16)
                        V.tensor_tensor(y_t, jf(bank[3][0:Q, 0:256]), x_t, ALU.add).then_inc(S["x_used"], 1)
                        dve.wait_ge(S["x_used"], it + 1)
                        layernorm(dve, link, y_t, S, it)
                        dve.wait_ge(S["y_ready"], it + 1)
                        assert link.count[0] == per

        run_sweep("s0", "sum_attr", io["x"], src_d)
        node_mlp("n0", io["x"], x1_d, "W01", "b01", "W02", "b02", F, F, "x_and_sums")
        next_phase()
        run_sweep("s1", "sum", x1_d, src_d)
        node_mlp("n1", x1_d, x2_d, "W11", "b11", "W12", "b12", P, P, "sums")
        next_phase()
        for layer, x_l, h_l in ((0, x2_d, h1_d), (1, h1_d, h2_d)):
            node_gat_tables(f"t{layer}", x_l, layer)
            next_phase()
            run_sweep(f"a{layer}", "gat", srctab_d, src_d)
            node_stats(f"st{layer}", layer)
            next_phase()
            run_sweep(f"b{layer}", "mix")
            node_gat_out(f"h{layer}", layer, h_l, layer == 0)
            next_phase()
        node_mlp("n2", x2_d, x3_d, "R1", "rb1", "R2", "rb2", F, F, "x", extra=h2_d)
        next_phase()
        node_relations("r", x3_d)
        next_phase()
        run_sweep("s3", "hgt", reltab_d, rel_d)
        node_last("last", x3_d)
        next_phase()


_INS = ['x', 'src', 'dst', 'edge_attr_64', 'edge_type_8', 'edge_weight', 'node_type_4', 'L0_gnn_W1', 'L0_gnn_b1',
        'L0_gnn_W2', 'L0_gnn_b2', 'L1_gnn_W1', 'L1_gnn_b1', 'L1_gnn_W2', 'L1_gnn_b2', 'L2_gnn_W0', 'L2_gnn_att0',
        'L2_gnn_beta0', 'L2_gnn_b0', 'L2_gnn_W1', 'L2_gnn_att1', 'L2_gnn_beta1', 'L2_gnn_b1', 'L2_gnn_rW1',
        'L2_gnn_rb1', 'L2_gnn_rW2', 'L2_gnn_rb2', 'L3_gnn_k_lin', 'L3_gnn_q_lin', 'L3_gnn_v_lin', 'L3_gnn_a_lin',
        'L3_gnn_rel_att', 'L3_gnn_rel_msg', 'L3_gnn_rel_pri', 'L3_gnn_skip']


def kernel(**inputs):
    import numpy as _np
    import concourse.bacc as _bacc
    from concourse import mybir as _mybir
    from concourse.bass_utils import run_bass_kernel_spmd as _run

    nc = _bacc.Bacc("TRN2", target_bir_lowering=False, num_devices=1)
    arrays, io = {}, {}
    for name in _INS:
        a = _np.asarray(inputs[name])
        if name == "L3_gnn_rel_att":
            a = a.transpose(2, 0, 1).reshape(64, -1)
        elif name == "L3_gnn_rel_msg":
            a = a.transpose(1, 0, 2).reshape(64, -1)
        elif name.endswith("_lin"):
            a = a.reshape(-1, a.shape[-1])
        a = _np.ascontiguousarray(a)
        arrays[f"in_{name}_dram"] = a
        io[name] = nc.dram_tensor(f"in_{name}_dram", a.shape, _mybir.dt.from_np(a.dtype), kind="ExternalInput").ap()
    out = nc.dram_tensor("out_0_dram", (12500, 64), _mybir.dt.float32, kind="ExternalOutput").ap()
    build(nc, io, out)
    r = _run(nc, [arrays], core_ids=[0])
    return r.results[0]["out_0_dram"]
```

```python
from contextlib import ExitStack

import concourse.bass as bass
from concourse import mybir

ALU = mybir.AluOpType
ACT = mybir.ActivationFunctionType
AX = mybir.AxisListType
F32 = mybir.dt.float32
BF16 = mybir.dt.bfloat16
I16 = mybir.dt.int16
I32 = mybir.dt.int32
U32 = mybir.dt.uint32

P = 128
C = 4
GE = P * C
N, E, F = 12500, 200000, 64
NT, NR = 4, 8
FULL = E // GE
STEPS = 8
GROUPS = -(-(FULL + 1) // STEPS) * STEPS
TAIL = E - GE
OVER = (FULL + 1) * GE - E
WIN = -(-N // P)
ND = -(-(N + P) // P) * P
OFF_IDLE = N
RING = 4
LAG = 4
ROUNDS = -(-(GROUPS * WIN + LAG + STEPS) // (STEPS * P)) * P
PRIME = 8
Q, J = 125, 4
CH = Q * J
CHUNKS = N // CH
BIG = 2.0 ** 99
LN_EPS = 1e-5
SM_EPS = 1e-16
COS_EPS2 = 1e-16
SLOPE = 0.2


def build(nc, io, out):
    with ExitStack() as ctx:
        def sb(name, shape, dt=F32):
            return ctx.enter_context(nc.sbuf_tensor(name, shape, dt))

        def sem(name):
            return ctx.enter_context(nc.semaphore(name))

        phase_sems = []

        def psem(name):
            phase_sems.append(nc.alloc_semaphore(name))
            return phase_sems[-1]

        def next_phase():
            nc.clear_and_free_semaphores(list(phase_sems))
            nc.all_engine_barrier()
            phase_sems.clear()

        def dram(name, shape, dt=F32):
            return nc.dram_tensor(name, shape, dt).ap()

        x1_d, x2_d, x3_d, h1_d, h2_d = (dram(f"{n}_d", (N, F)) for n in ("x1", "x2", "x3", "h1", "h2"))
        src_d = dram("src_d", (GROUPS + 1, P, C), I32)
        rel_d = dram("rel_d", (GROUPS + 1, P, C), I32)
        iota_d = dram("iota_d", (ND, 1), I32)
        base_d = dram("base_d", (GROUPS, 1), I32)
        nwin_d = dram("nwin_d", (GROUPS, 1), I32)
        sched_d = dram("sched_d", (ROUNDS, 2 * STEPS), I32)
        iters_d = dram("iters_d", (1, 2), I32)
        srctab_d = dram("srctab_d", (N, F + 2))
        dsttab_d = dram("dsttab_d", (ND, 3 * (F + 2)), BF16)
        stat_d = dram("stat_d", (ND, 3 * 4), BF16)
        stash_d = dram("stash_d", (GROUPS + 1, P, C * (F + 2)))
        reltab_d = dram("reltab_d", (NR * N, 2 * F))
        trash_d = dram("trash_d", (P, C * (F + 2)))

        acc = sb("acc", [P, ND])
        top = sb("top", [P, ND])
        iota16 = sb("iota16", [P, ND], I16)
        dstf = sb("dstf", [P, GROUPS * C + C])
        gate = sb("gate", [P, GROUPS * C + C])
        logit = sb("logit", [P, GROUPS * C + C])
        ecos = sb("ecos", [P, GROUPS * C + C])
        ident = sb("ident", [P, P])
        work = sb("work", [P, 5440])
        rows = [sb(f"rows{k}", [P, C, 2 * F]) for k in range(RING)]
        pay = [sb(f"pay{k}", [P, C, F + 1]) for k in range(RING)]
        dwin = [sb(f"dwin{k}", [P, 3 * (F + 2)], BF16) for k in range(RING)]
        idx = [sb(f"idx{k}", [P, C], I32) for k in range(RING)]
        small = sb("small", [P, 256])
        wts = sb("wts", [P, 2400])
        bias = sb("bias", [P, 640])
        bank = [ctx.enter_context(nc.psum_tensor(f"bank{b}", [P, 512], F32)) for b in range(8)]

        onehot = [work[:, k * 512:(k + 1) * 512].rearrange("p (c n) -> p c n", c=C) for k in range(RING)]
        turned = [work[:, 2048 + k * 256:2048 + (k + 1) * 256].bitcast(BF16) for k in range(RING)]
        block_ = [work[:, 3072 + k * 256:3072 + (k + 1) * 256].bitcast(BF16) for k in range(RING)]

        at, wcols, bcols = 0, {}, {}
        for name, w in (("W01", 64), ("W02", 64), ("W11", 128), ("W12", 64), ("G0", 65), ("G1", 65), ("R1", 64),
                        ("R2", 64), ("K", 128), ("Qw", 128), ("V", 128), ("A", 128), ("RA", 512), ("RM", 512),
                        ("U0", 2), ("U1", 2), ("pri", 8), ("skip", 2), ("beta", 2), ("mix", 4)):
            wcols[name] = (at, at + w)
            at += w
        at = 0
        for name, w in (("b02", 64), ("b12", 64), ("bg0", 64), ("bg1", 64), ("rb2", 64), ("att0", 128), ("att1", 128),
                        ("b01", 1), ("b11", 1), ("rb1", 1)):
            bcols[name] = (at, at + w)
            at += w

        def wt(name, k=64):
            a, b = wcols[name]
            return wts[0:k, a:b]

        def bs(name, k=P):
            a, b = bcols[name]
            return bias[0:k, a:b]

        def grouped(x):
            return x[0:FULL * GE].rearrange("(g p c) -> p g c", p=P, c=C)

        def tail(x):
            return x[TAIL:E].rearrange("(p c) -> p c", c=C)

        loaded, made, stored, sched = (sem(n) for n in ("loaded", "made", "prep_stored", "sched_stored"))
        acted, pooled, summed = sem("prep_acted"), sem("prep_pooled"), sem("steps_summed")
        cols = C * GROUPS
        raw_i = [top[:, k * 2048:k * 2048 + cols].bitcast(I32) for k in range(4)]
        raw_f = [acc[:, k * 2048:k * 2048 + cols] for k in range(6)]
        QP = GROUPS // 4
        spans = top[0:QP, 8192:8192 + 2048].bitcast(I32).rearrange("p (g e) -> p g e", g=4)
        spansf = acc[0:QP, 10240:10240 + 2048].rearrange("p (g e) -> p g e", g=4)
        lo, hi, nwin = small[0:QP, 0:4], small[0:QP, 4:8], small[0:QP, 8:12]
        lo_i, hi_i = small[0:QP, 16:20].bitcast(I32), small[0:QP, 20:24].bitcast(I32)
        nsum = small[0:QP, 24:25]
        total, total_i = small[0:1, 32:34], small[0:1, 36:38].bitcast(I32)
        idle = work[:, 0:ROUNDS // P * 2 * STEPS].bitcast(I32).rearrange("p (a b) -> p a b", b=2 * STEPS)
        iota_i = work[:, 1024:1024 + ND // P].bitcast(I32)
        dpad = work[:, 1200:1200 + 3 * (F + 2)].bitcast(BF16).rearrange("p (a b) -> p a b", a=2)
        zero_i = work[:, 2048:2048 + C].bitcast(I32)
        ones = small[:, 40:41]
        prod64 = work[0:64, 3072:3136]
        sg = wts[:, wcols["skip"][0]:wcols["beta"][1]]
        rel_made, windows_made, counts_made, total_made = (sem(n) for n in ("rel_made", "windows_made", "counts_made", "total_made"))

        with nc.Block() as block:
            loads = []

            @block.sync
            def _(sp):
                def load(dst, src):
                    loads.append(1)
                    sp.dma_start(dst, src).then_inc(loaded, 16)

                for k, name in enumerate(("dst", "src", "edge_weight", "edge_type_8")):
                    t = raw_i[k] if name != "edge_weight" else raw_f[5]
                    load(t[:, 0:C * FULL].rearrange("p (g c) -> p g c", c=C), grouped(io[name]))
                    for g in range(FULL, GROUPS):
                        load(t[:, C * g:C * g + C], tail(io[name]))
                full4 = FULL // 4
                load(spans[0:full4, :, :], io["dst"][0:full4 * 4 * GE].rearrange("(p g e) -> p g e", g=4, e=GE))
                for g in range(full4 * 4, GROUPS):
                    a = min(g * GE, TAIL)
                    load(spans[g // 4:g // 4 + 1, g % 4, :], io["dst"][a:a + GE].rearrange("(p e) -> p e", p=1))
                sp.wait_ge(pooled, 1)
                for name, key, k in (("W01", "L0_gnn_W1", 64), ("W02", "L0_gnn_W2", 64), ("W12", "L1_gnn_W2", 128),
                                     ("R1", "L2_gnn_rW1", 64), ("R2", "L2_gnn_rW2", 64)):
                    load(wt(name, k), io[key])
                load(wts[0:64, wcols["W11"][0]:wcols["W11"][1]], io["L1_gnn_W1"])
                load(wts[64:128, wcols["W11"][0]:wcols["W11"][1]], io["L1_gnn_W1"])
                for name, key in (("G0", "L2_gnn_W0"), ("G1", "L2_gnn_W1")):
                    a = wcols[name][0]
                    load(wts[0:64, a:a + 64], io[key])
                for name, key in (("K", "L3_gnn_k_lin"), ("Qw", "L3_gnn_q_lin"), ("V", "L3_gnn_v_lin"), ("A", "L3_gnn_a_lin")):
                    load(wt(name, 128).rearrange("p (h e) -> p h e", h=2), io[key].rearrange("(h p) e -> p h e", h=2))
                load(wt("RA"), io["L3_gnn_rel_att"])
                load(wt("RM"), io["L3_gnn_rel_msg"])
                load(wt("pri"), io["L3_gnn_rel_pri"].partition_broadcast(64))
                for t in range(NT):
                    a = wcols["skip"][0] + t // 2
                    load(wts[64 * (t % 2):64 * (t % 2) + 64, a:a + 1], io["L3_gnn_skip"][t:t + 1].partition_broadcast(64))
                for i, key in enumerate(("L2_gnn_beta0", "L2_gnn_beta1")):
                    a = wcols["beta"][0] + i
                    load(wts[:, a:a + 1], io[key].partition_broadcast(P))
                for name, key in (("b02", "L0_gnn_b2"), ("b12", "L1_gnn_b2"), ("bg0", "L2_gnn_b0"), ("bg1", "L2_gnn_b1"),
                                  ("rb2", "L2_gnn_rb2")):
                    load(bs(name), io[key].partition_broadcast(P))
                for name, key in (("att0", "L2_gnn_att0"), ("att1", "L2_gnn_att1")):
                    load(bs(name, 64), io[key].rearrange("a b -> (a b)").partition_broadcast(64))
                for name, key, k in (("b01", "L0_gnn_b1", 64), ("b11", "L1_gnn_b1", 128), ("rb1", "L2_gnn_rb1", 64)):
                    load(bs(name, k), io[key].rearrange("(a b) -> a b", b=1))
                sp.wait_ge(rel_made, 1)
                sp.dma_start(src_d[0:GROUPS].rearrange("g p c -> p g c"), raw_i[1].rearrange("p (g c) -> p g c", c=C)).then_inc(stored, 16)
                sp.dma_start(rel_d[0:GROUPS].rearrange("g p c -> p g c"), raw_i[2].rearrange("p (g c) -> p g c", c=C)).then_inc(stored, 16)
                sp.wait_ge(pooled, 2)
                sp.dma_start(iota_d.rearrange("(p a) b -> p (a b)", p=P), iota_i).then_inc(stored, 16)
                for d in (src_d, rel_d):
                    sp.dma_start(d[GROUPS], zero_i[:, 0:C]).then_inc(stored, 16)
                sp.dma_start(sched_d.rearrange("(p a) b -> p a b", p=P), idle).then_inc(stored, 16)
                sp.dma_start(dsttab_d[N:ND, :].rearrange("(p a) b -> p a b", p=(ND - N) // 2), dpad[0:(ND - N) // 2, :, :]).then_inc(stored, 16)
                sp.dma_start(stat_d[N:ND, :].rearrange("(p a) b -> p a b", p=(ND - N) // 2), dpad[0:(ND - N) // 2, :, 0:12]).then_inc(stored, 16)
                sp.wait_ge(windows_made, 1)
                sp.dma_start(base_d.rearrange("(p a) b -> p (a b)", p=QP), lo_i).then_inc(stored, 16)
                sp.dma_start(nwin_d.rearrange("(p a) b -> p (a b)", p=QP), hi_i).then_inc(stored, 16)
                sp.wait_ge(total_made, 1)
                sp.dma_start(iters_d, total_i).then_inc(stored, 16)
                sp.wait_ge(stored, 16 * 11)

            @block.gpsimd
            def _(pool):
                nc.gpsimd.memset(wts[:], 0.0).then_inc(pooled, 1)
                nc.gpsimd.memset(idle[:, :, 0:STEPS], OFF_IDLE)
                nc.gpsimd.memset(idle[:, :, STEPS:], GROUPS)
                nc.gpsimd.memset(zero_i, 0)
                nc.gpsimd.memset(dpad, 0.0)
                nc.gpsimd.memset(ones, 1.0)
                nc.gpsimd.iota(iota16[:], pattern=[[1, ND]], base=0, channel_multiplier=0)
                nc.gpsimd.memset(ident[:], 0.0)
                nc.gpsimd.iota(iota_i, pattern=[[1, ND // P]], base=0, channel_multiplier=ND // P).then_inc(pooled, 1)
                pool.wait_ge(pooled, 2)
                nc.gpsimd.affine_select(out=ident[:], in_=ident[:], compare_op=ALU.not_equal, fill=1.0, base=0,
                                        pattern=[[-1, P]], channel_multiplier=1).then_inc(pooled, 1)

            @block.vector
            def _(dve):
                V = nc.vector
                add, mul = ALU.add, ALU.mult
                chained = [0]

                def link(ins):
                    chained[0] += 1
                    ins.then_inc(made, 1)
                    dve.wait_ge(made, chained[0])

                def show(ins, signal):
                    ins.then_inc(signal, 1)
                    dve.wait_ge(signal, 1)

                dve.wait_ge(loaded, 16 * len(loads))
                dve.wait_ge(pooled, 3)
                link(V.tensor_copy(dstf[:, 0:cols], raw_i[0]))
                link(V.memset(dstf[0:OVER // C, C * FULL:C * FULL + C], -1.0))
                link(V.memset(dstf[:, C * (FULL + 1):], -1.0))
                link(V.tensor_copy(raw_f[1], raw_i[1]))
                link(V.tensor_copy(raw_f[2], raw_i[3]))
                link(V.scalar_tensor_tensor(raw_f[1], raw_f[2], float(N), raw_f[1], mul, add))
                show(V.tensor_copy(raw_i[2], raw_f[1]), rel_made)
                link(V.tensor_scalar(gate[:, 0:cols], raw_f[5], 4.0, -0.25, ALU.min, mul))
                link(V.memset(gate[:, cols:], 1.0))
                link(V.tensor_scalar(gate[:], gate[:], 1.0, 0.0, add, ALU.max))
                link(V.tensor_scalar(gate[:], gate[:], 1.0, None, ALU.min))
                link(V.tensor_copy(spansf, spans))
                link(V.tensor_reduce(lo, spansf, AX.X, ALU.min))
                link(V.tensor_reduce(hi, spansf, AX.X, ALU.max))
                link(V.tensor_copy(lo_i, lo))
                link(V.tensor_tensor(hi, hi, lo, ALU.subtract))
                link(V.tensor_scalar(hi, hi, float(P), None, add))
                link(V.tensor_copy(hi_i, hi))
                link(V.tensor_scalar(hi_i, hi_i, 7, None, ALU.arith_shift_right))
                show(V.tensor_copy(nwin, hi_i), windows_made)
                show(V.tensor_reduce(nsum, nwin, AX.X, add), counts_made)
                dve.wait_ge(summed, 1)
                link(V.tensor_scalar(total[:, 0:1], bank[0][0:1, 0:1], float(LAG + STEPS - 1), None, add))
                link(V.tensor_copy(total[:, 1:2], bank[0][0:1, 0:1]))
                link(V.tensor_copy(total_i, total))
                show(V.tensor_scalar(total_i[:, 0:1], total_i[:, 0:1], STEPS.bit_length() - 1, None, ALU.arith_shift_right), total_made)
                for i in range(2):
                    g, a = wcols[f"G{i}"][0], wcols[f"U{i}"][0]
                    att = bs(f"att{i}", 64)
                    for h in range(2):
                        link(V.tensor_tensor(prod64, wts[0:64, g:g + 64], att[:, 64 * h:64 * h + 64], mul))
                        link(V.tensor_reduce(wts[0:64, a + h:a + h + 1], prod64, AX.X, add))
                    link(V.memset(wts[64:65, g + 64:g + 65], 1.0))
                link(V.tensor_scalar(wt("pri"), wt("pri"), 1.0 / 8.0, None, mul))
                ra = wt("RA").rearrange("p (r d) -> p r d", r=NR)
                link(V.tensor_tensor(ra, ra, wt("pri").unsqueeze(2).to_broadcast([64, NR, F]), mul))
                dve.wait_ge(acted, 1)
                link(V.tensor_scalar(sg, sg, 1.0, None, add))
                link(V.reciprocal(sg, sg))
                for i in range(2):
                    m, b = wcols["mix"][0] + 2 * i, wcols["beta"][0] + i
                    link(V.tensor_copy(wts[:, m + 1:m + 2], wts[:, b:b + 1]))
                    link(V.tensor_scalar(wts[:, m:m + 1], wts[:, b:b + 1], -1.0, 1.0, mul, add))
                    a, s = wcols["A"][0] + 64 * i, wcols["skip"][0] + i
                    link(V.tensor_scalar(wts[:, a:a + 64], wts[:, a:a + 64], wts[:, s:s + 1], None, mul))

            @block.tensor
            def _(pe):
                pe.wait_ge(counts_made, 1)
                pe.matmul(bank[0][0:1, 0:1], nsum, ones[0:QP, :], start=True, stop=True).then_inc(summed, 1)

            @block.scalar
            def _(act):
                act.wait_ge(loaded, 16 * len(loads))
                nc.scalar.activation(sg, sg, ACT.Exp, scale=-1.0).then_inc(acted, 1)

        with nc.Block() as block:
            @block.sync
            def _(sp):
                steps_n = sp.value_load(iters_d[0:1, 1:2], min_val=GROUPS, max_val=GROUPS * WIN)
                at_reg, off_reg, place_reg = (sp.alloc_register(n) for n in ("step_at", "step_off", "step_place"))
                cells = sched_d.rearrange("r (q b) -> (r q) b", b=1)
                with sp.If(steps_n == GROUPS):
                    sp.dma_start(sched_d[0:GROUPS // STEPS, 0:STEPS], base_d.rearrange("(r q) b -> r (q b)", q=STEPS)).then_inc(sched, 16)
                    sp.dma_start(sched_d[0:GROUPS // STEPS, STEPS:2 * STEPS],
                                 iota_d[0:GROUPS, :].rearrange("(r q) b -> r (q b)", q=STEPS)).then_inc(sched, 16)
                    sp.wait_ge(sched, 32)
                with sp.Else():
                    sp.reg_mov(at_reg, 0)
                    with sp.Fori(0, GROUPS) as g:
                        first = sp.value_load(base_d[bass.ds(g, 1), :], min_val=0, max_val=N - 1)
                        count = sp.value_load(nwin_d[bass.ds(g, 1), :], min_val=1, max_val=WIN)
                        with sp.Fori(0, count) as w:
                            s = sp.snap(at_reg, min_val=0, max_val=GROUPS * WIN - 1)
                            sp.reg_mov(off_reg, first + w * P)
                            o = sp.snap(off_reg, min_val=0, max_val=N - 1)
                            place = s * 2 - s % STEPS
                            sp.reg_mov(place_reg, place)
                            place = sp.snap(place_reg, min_val=0, max_val=2 * STEPS * ROUNDS - STEPS - 1)
                            sp.dma_start(cells[bass.ds(place, 1), :], iota_d[bass.ds(o, 1), :]).then_inc(sched, 16)
                            sp.dma_start(cells[bass.ds(place + STEPS, 1), :], iota_d[bass.ds(g, 1), :]).then_inc(sched, 16)
                            sp.reg_add(at_reg, at_reg, 1)
                            sp.wait_ge(sched, (s + 1) * 32)
                            sp.nop(nofuse=True)

        def sweep(tag, kind, table=None, index_d=None):
            expand = kind in ("gat", "mix", "hgt")
            online = kind in ("gat", "hgt")
            R = {"sum": F, "sum_attr": 2 * F, "gat": 2, "mix": F + 1, "hgt": F + 1}[kind]
            width = {"sum": F, "sum_attr": F, "gat": F + 2, "mix": F + 2, "hgt": 2 * F}[kind]
            dw = 4 if kind == "mix" else F + 2
            L = dict(onehot=0, turned=0, turn_copied=0, blocked=0, expanded=0,
                     products=1, cos_summed=1, logit_summed=1, cos_scaled=1, leaky=1, cos_kept=1, masked=1, scored=1, spread=1,
                     max_found=2, max_hi=2, max_rest=2, max_mid=2, max_split=2, max_row=2, max_edge=2, fall=2, top_moved=2,
                     shifted=2, exped=2, relus=2, factors=2, paid=2, summed_=2, new_scaled=3, old_scaled=3, added=3)
            if kind in ("sum", "sum_attr"):
                L = dict(onehot=0, summed_=0, added=1)
            if kind == "mix":
                L = dict(onehot=0, turned=0, turn_copied=0, expanded=0, below=1, cos_part=1, gate_kept=1, shifted=1, exped=1,
                         gat_part=2, fused=2, weighed=2, gated=2, paid=3, summed_=3, added=4)
            S = {n: psem(f"{tag}_{n}") for n in L}
            s_idx = [psem(f"{tag}_idx{k}") for k in range(RING)]
            s_rows = [psem(f"{tag}_rows{k}") for k in range(RING)]
            s_dwin = [psem(f"{tag}_dwin{k}") for k in range(RING)] if expand else None
            s_attr = [psem(f"{tag}_attr{k}") for k in range(RING)] if kind == "sum_attr" else None
            s_stash = [psem(f"{tag}_stash{k}") for k in range(RING)] if kind == "gat" else None
            pool_cleared, dve_cleared = psem(f"{tag}_pool_cleared"), psem(f"{tag}_dve_cleared")
            last_rows = "scored" if kind == "gat" else "paid" if kind in ("mix", "hgt") else "summed_"
            by_target = stat_d if kind == "mix" else dsttab_d

            def rowv(k):
                if kind in ("sum", "sum_attr"):
                    return rows[k][:, :, 0:F]
                flat = rows[k][:].rearrange("p c f -> p (c f)")
                return flat[:, 0:C * width].rearrange("p (c f) -> p c f", c=C)

            turn_b, exp_b, sum_b = bank[0:2], bank[2:4], bank[6:8]
            spread_b, max_b = bank[4], bank[5]

            def w(eng, t, mine, name, ring=0):
                eng.wait_ge(S[name], t[0] + (t[1] - L[mine] + L[name] + 1 + PRIME - ring))

            def landed(eng, sem_, i, u, lag, per=16):
                eng.wait_ge(sem_, i * (per * (STEPS // RING)) + ((u - lag) // RING + 1) * per + 16)

            def prime(eng, *names):
                for n in names:
                    if n in S:
                        eng.sem_inc(S[n], PRIME)

            def load_round(eng, i, lag_off, lag_grp):
                regs, old_off, old_grp = carried[eng.engine.name]
                eng.load(regs, sched_d[bass.ds(i, 1), :])
                off = {u: eng.snap(regs[u], min_val=0, max_val=N) for u in range(STEPS)}
                grp = {u: eng.snap(regs[STEPS + u], min_val=0, max_val=GROUPS) for u in range(STEPS)}
                for b in range(1, lag_off + 1):
                    off[-b] = eng.snap(old_off[b], min_val=0, max_val=N)
                for b in range(1, lag_grp + 1):
                    grp[-b] = eng.snap(old_grp[b], min_val=0, max_val=GROUPS)
                return off, grp

            def carry_round(eng, lag_off, lag_grp):
                regs, old_off, old_grp = carried[eng.engine.name]
                for b in range(1, lag_off + 1):
                    eng.reg_mov(old_off[b], regs[STEPS - b])
                for b in range(1, lag_grp + 1):
                    eng.reg_mov(old_grp[b], regs[2 * STEPS - b])

            def idle_before(eng, lag_off, lag_grp):
                if eng.engine.name not in carried:
                    regs = [eng.alloc_register(f"round_{q}") for q in range(2 * STEPS)]
                    old_off = [eng.alloc_register(f"old_off_{q}") for q in range(RING + 1)]
                    old_grp = [eng.alloc_register(f"old_grp_{q}") for q in range(RING + 1)]
                    carried[eng.engine.name] = regs, old_off, old_grp
                _, old_off, old_grp = carried[eng.engine.name]
                for b in range(1, lag_off + 1):
                    eng.reg_mov(old_off[b], OFF_IDLE)
                for b in range(1, lag_grp + 1):
                    eng.reg_mov(old_grp[b], GROUPS)

            block = ctx2.enter_context(nc.Block())

            def rounds(eng):
                return eng.value_load(iters_d[0:1, 0:1], min_val=1, max_val=ROUNDS)

            @block.sync
            def _(sp):
                sp.wait_ge(pool_cleared, 1)
                sp.wait_ge(dve_cleared, 1)
                for k in range(RING):
                    if expand:
                        sp.dma_start(dwin[k][:, 0:3 * dw], by_target[0:P, :]).then_inc(s_dwin[k], 16)
                    if kind == "mix":
                        sp.dma_start(rowv(k), stash_d[k].rearrange("p (c f) -> p c f", c=C)).then_inc(s_rows[k], 16)
                    if kind == "gat":
                        sp.wait_ge(s_rows[k], 16)
                        sp.dma_start(stash_d[GROUPS].rearrange("p (c f) -> p c f", c=C), rowv(k)).then_inc(s_stash[k], 16)
                        sp.wait_ge(s_stash[k], 16)
                for k in range(RING):
                    if expand:
                        sp.wait_ge(s_dwin[k], 16)
                    if kind == "mix":
                        sp.wait_ge(s_rows[k], 16)
                n = rounds(sp)
                attr_reg = sp.alloc_register(f"{tag}_attr_at") if kind == "sum_attr" else None
                lag_g = 3 if kind == "gat" else 0
                idle_before(sp, 0, lag_g)
                with sp.Fori(0, n) as i:
                    off, grp = load_round(sp, i, 0, lag_g)
                    i4 = sp.snap(i * STEPS)
                    for u in range(STEPS):
                        t, k = (i4, u), u % RING
                        sp.wait_ge(S[last_rows], i4 + (u + L[last_rows] + 1 + PRIME - RING))
                        sp.nop(nofuse=True)
                        if kind != "mix":
                            sp.dma_start(idx[k][:], index_d[bass.ds(grp[u], 1), :, :].rearrange("g p c -> (g p) c")).then_inc(s_idx[k], 16)
                        else:
                            sp.dma_start(rowv(k), stash_d[bass.ds(grp[u], 1), :, :].rearrange("g p (c f) -> (g p) c f", c=C)).then_inc(s_rows[k], 16)
                        if kind == "sum_attr":
                            sp.reg_alu(attr_reg, grp[u] * GE, TAIL, ALU.min)
                            e = sp.snap(attr_reg, min_val=0, max_val=TAIL)
                            sp.dma_start(rows[k][:, :, F:2 * F],
                                         io["edge_attr_64"][bass.ds(e, GE), :].rearrange("(p c) f -> p c f", c=C)).then_inc(s_attr[k], 16)
                        if expand:
                            w(sp, t, "expanded", "expanded", RING)
                            sp.nop(nofuse=True)
                            sp.dma_start(dwin[k][:, 0:3 * dw], by_target[bass.ds(off[u], P), :]).then_inc(s_dwin[k], 16)
                        if kind == "gat":
                            j = (u - 3) % RING
                            landed(sp, s_rows[j], i, u, 3, 64)
                            sp.nop(nofuse=True)
                            landed(sp, s_stash[k], i, u, 1)
                            sp.nop(nofuse=True)
                            sp.dma_start(stash_d[bass.ds(grp[u - 3], 1), :, :].rearrange("g p (c f) -> (g p) c f", c=C),
                                         rowv(j)).then_inc(s_stash[j], 16)
                    carry_round(sp, 0, lag_g)
                if kind == "gat":
                    for k in range(RING):
                        sp.wait_ge(s_stash[k], n * (16 * (STEPS // RING)) + 16)
                        sp.nop(nofuse=True)

            @block.gpsimd
            def _(pool):
                if online:
                    nc.gpsimd.memset(top[0:R, :], -BIG)
                if expand:
                    for k in range(RING):
                        nc.gpsimd.memset(pay[k][:], 0.0)
                        nc.gpsimd.memset(gmax[k][:], 0.0)
                        nc.gpsimd.memset(gpart[k][:], 0.0)
                        nc.gpsimd.memset(factor[k][:], 1.0)
                nc.gpsimd.memset(small[:], 0.0).then_inc(pool_cleared, 1)
                if kind == "mix":
                    return
                pool.wait_ge(pool_cleared, 1)
                pool.wait_ge(dve_cleared, 1)
                for k in range(RING):
                    nc.gpsimd.dma_start(rowv(k), table[0:P * C, :].rearrange("(p c) f -> p c f", c=C)).then_inc(s_rows[k], 16)
                n = rounds(pool)
                with pool.Fori(0, n) as i:
                    i4 = pool.snap(i * STEPS)
                    for u in range(STEPS):
                        k = u % RING
                        pool.wait_ge(s_idx[k], i * (16 * (STEPS // RING)) + (u // RING + 1) * 16)
                        pool.wait_ge(S[last_rows], i4 + (u + L[last_rows] + 1 + PRIME - RING))
                        if kind == "gat":
                            landed(pool, s_stash[k], i, u, 1)
                        landed(pool, s_rows[k], i, u, RING, 64)
                        pool.nop(nofuse=True)
                        for c in range(C):
                            nc.gpsimd.indirect_dma_start(
                                out=rowv(k)[:, c, :], out_offset=None, in_=table,
                                in_offset=bass.IndirectOffsetOnAxis(ap=idx[k][:, c:c + 1].bitcast(U32), axis=0)).then_inc(s_rows[k], 16)

            def rows_in(eng, i, u, lag):
                landed(eng, s_rows[(u - lag) % RING], i, u, lag, 16 if kind == "mix" else 64)

            @block.tensor
            def _(pe):
                prime(pe, "turned", "expanded", "spread", "max_row", "max_edge", "summed_")
                pe.wait_ge(pool_cleared, 1)
                pe.wait_ge(dve_cleared, 1)
                n = rounds(pe)
                with pe.Fori(0, n) as i:
                    i4 = pe.snap(i * STEPS)
                    for u in range(STEPS):
                        t, k = (i4, u), u % RING
                        if expand:
                            w(pe, t, "turned", "onehot")
                            w(pe, t, "turned", "turn_copied", 2)
                            if online:
                                w(pe, t, "turned", "blocked", 2)
                            for c in range(C):
                                mm = pe.transpose(turn_b[u % 2][:, c * P:(c + 1) * P], onehot[k][:, c, :], ident[:])
                            mm.then_inc(S["turned"], 1)
                        if online:
                            j = (u - 2) % RING
                            w(pe, t, "max_row", "max_found")
                            w(pe, t, "max_row", "top_moved", 1)
                            w(pe, t, "max_row", "shifted", 1)
                            src = gmax[j][:, 0:2] if kind == "gat" else gmax[j][:, 0:1].to_broadcast([P, R])
                            pe.transpose(max_b[0:R, 0:P], src, ident[:]).then_inc(S["max_row"], 1)
                            w(pe, t, "max_edge", "max_split")
                            for c in range(C):
                                for q in range(3):
                                    mm = pe.matmul(max_b[:, 128 + c:129 + c], turned[j][:, c * P:(c + 1) * P], gpart[j][:, q:q + 1],
                                                   start=q == 0, stop=q == 2)
                            mm.then_inc(S["max_edge"], 1)
                        def expand_rows():
                            if expand:
                                w(pe, t, "expanded", "turn_copied")
                                landed(pe, s_dwin[k], i, u, 0)
                                w(pe, t, "expanded", "scored" if online else "gat_part", 2)
                                for c in range(C):
                                    for q in range(3):
                                        mm = pe.matmul(exp_b[u % 2][:, c * dw:(c + 1) * dw], turned[k][:, c * P:(c + 1) * P],
                                                       dwin[k][:, q * dw:(q + 1) * dw], start=q == 0, stop=q == 2)
                                mm.then_inc(S["expanded"], 1)

                        def sum_rows():
                            j = (u - L["summed_"]) % RING
                            w(pe, t, "summed_", {"gat": "exped", "mix": "paid", "hgt": "paid"}.get(kind, "onehot"))
                            w(pe, t, "summed_", "added", 2)
                            if not expand:
                                rows_in(pe, i, u, 0)
                            if kind == "sum_attr":
                                pe.wait_ge(s_attr[k], i * (16 * (STEPS // RING)) + (u // RING + 1) * 16)
                            for c in range(C):
                                if kind == "sum":
                                    lhs = rows[j][:, c, 0:F]
                                elif kind == "sum_attr":
                                    lhs = rows[j][:, c, :]
                                else:
                                    lhs = pay[j][:, c, 0:R]
                                mm = pe.matmul(sum_b[j % 2][0:R, 0:P], lhs, onehot[j][:, c, :], start=c == 0, stop=c == C - 1)
                            mm.then_inc(S["summed_"], 1)

                        if kind == "mix":
                            sum_rows()
                        expand_rows()
                        if online:
                            j = (u - 1) % RING
                            w(pe, t, "spread", "scored")
                            w(pe, t, "spread", "max_found", 1)
                            for c in range(C):
                                mm = pe.transpose(spread_b[:, c * P:(c + 1) * P], score[j][:, c:c + 1].to_broadcast([P, P]), ident[:])
                            mm.then_inc(S["spread"], 1)
                        if kind != "mix":
                            sum_rows()

            @block.scalar
            def _(act):
                prime(act, "turn_copied", "blocked", "exped", "relus", "factors", "gated")
                if not expand:
                    return
                act.wait_ge(pool_cleared, 1)
                act.wait_ge(dve_cleared, 1)
                nc.scalar.activation(warm, warm, ACT.Exp)
                n = rounds(act)
                with act.Fori(0, n) as i:
                    i4 = act.snap(i * STEPS)
                    for u in range(STEPS):
                        t, k = (i4, u), u % RING
                        w(act, t, "turn_copied", "turned")
                        w(act, t, "turn_copied", "summed_" if kind == "mix" else "max_edge", RING)
                        nc.scalar.copy(turned[k], turn_b[u % 2][:, :]).then_inc(S["turn_copied"], 1)
                        if online:
                            w(act, t, "blocked", "max_found", RING)
                            nc.scalar.activation(block_[k], turn_b[u % 2][:, :], ACT.Copy, bias=-BIG, scale=BIG).then_inc(S["blocked"], 1)
                            k = (u - 2) % RING
                            w(act, t, "exped", "shifted")
                            w(act, t, "exped", "summed_", RING)
                            if kind == "gat":
                                nc.scalar.activation(pay[k][:, :, 0], shift[k], ACT.Exp)
                                nc.scalar.activation(pay[k][:, :, 1], cosine[k], ACT.Exp).then_inc(S["exped"], 1)
                            else:
                                nc.scalar.activation(pay[k][:, :, F], shift[k], ACT.Exp).then_inc(S["exped"], 1)
                            w(act, t, "relus", "fall")
                            nc.scalar.activation(relu2[k % 2][0:R, 0:P], drop[k % 2][0:R, :], ACT.Relu, scale=-1.0)
                            nc.scalar.activation(relu2[k % 2][0:R, P:2 * P], drop[k % 2][0:R, :], ACT.Relu).then_inc(S["relus"], 1)
                            w(act, t, "factors", "relus")
                            w(act, t, "factors", "added", RING)
                            nc.scalar.activation(factor[k][0:R, :], relu2[k % 2][0:R, :], ACT.Exp, scale=-1.0).then_inc(S["factors"], 1)
                        else:
                            k = (u - 1) % RING
                            w(act, t, "exped", "shifted")
                            nc.scalar.activation(shift[k], shift[k], ACT.Exp).then_inc(S["exped"], 1)
                            k = (u - 2) % RING
                            w(act, t, "gated", "weighed")
                            w(act, t, "gated", "summed_", RING)
                            nc.scalar.activation(pay[k][:, :, F], score[k], ACT.Exp).then_inc(S["gated"], 1)

            @block.vector
            def _(dve):
                prime(dve, *[x for x in L if x not in ("turned", "expanded", "spread", "max_row", "max_edge", "summed_",
                                                       "turn_copied", "blocked", "exped", "relus", "factors", "gated")])
                V = nc.vector
                for b in bank:
                    V.memset(b[:], 0.0)
                V.memset(acc[0:R, :], 0.0)
                if kind == "gat":
                    V.memset(logit[:], 0.0)
                    V.memset(ecos[:], 0.0)
                V.memset(work[:], 0.0).then_inc(dve_cleared, 1)
                dve.wait_ge(pool_cleared, 1)
                dve.wait_ge(dve_cleared, 1)
                n = rounds(dve)
                back = L["added"]
                gback = 1 if expand else 0
                idle_before(dve, back, gback)
                with dve.Fori(0, n) as i:
                    off, grp = load_round(dve, i, back, gback)
                    i4 = dve.snap(i * STEPS)
                    col = {u: dve.snap(grp[u] * C) for u in grp}
                    for u in range(STEPS):
                        t, k = (i4, u), u % RING
                        k1, k2, k3 = (u - 1) % RING, (u - 2) % RING, (u - 3) % RING

                        def signal(ins, name):
                            ins.then_inc(S[name], 1)

                        if online:
                            w(dve, t, "max_found", "spread")
                            w(dve, t, "max_found", "blocked")
                            w(dve, t, "max_found", "max_row", RING)
                            dve.nop(nofuse=True)
                            signal(V.tensor_tensor_reduce(out=block_[k2], in0=spread_b[:, :], in1=block_[k2], scale=1.0, scalar=-BIG,
                                                          op0=ALU.add, op1=ALU.max, accum_out=gmax[k2][:, 0:1]), "max_found")
                        w(dve, t, "onehot", "summed_", RING)
                        signal(V.tensor_tensor(onehot[k], iota16[:, bass.ds(off[u], P)].unsqueeze(1).to_broadcast([P, C, P]),
                                               dstf[:, bass.ds(col[u], C)].unsqueeze(2).to_broadcast([P, C, P]),
                                               ALU.is_equal), "onehot")
                        if online:
                            w(dve, t, "max_hi", "max_found")
                            w(dve, t, "max_hi", "max_edge", RING)
                            signal(V.tensor_copy(gpart[k2][:, 0:1], gmax[k2][:, 0:1]), "max_hi")
                            ex = exp_b[k1 % 2][:, 0:C * dw].rearrange("p (c f) -> p c f", c=C)
                            w(dve, t, "products", "expanded")
                            rows_in(dve, i, u, 1)
                            signal(V.tensor_tensor(prod[:], rowv(k1)[:, :, 0:F], ex[:, :, 0:F], ALU.mult), "products")
                            w(dve, t, "max_rest", "max_hi")
                            signal(V.tensor_tensor(grest[:], gmax[k2][:, 0:1], gpart[k2][:, 0:1], ALU.subtract), "max_rest")
                            w(dve, t, "scored", "products")
                            w(dve, t, "scored", "exped", RING)
                            if kind == "hgt":
                                signal(V.tensor_reduce(score[k1], prod[:], AX.X, ALU.add), "scored")
                            else:
                                signal(V.tensor_reduce(cosine[k1], prod[:], AX.X, ALU.add), "cos_summed")
                                signal(V.tensor_tensor(score[k1], rowv(k1)[:, :, F], ex[:, :, F], ALU.add), "logit_summed")
                            w(dve, t, "max_mid", "max_rest")
                            signal(V.tensor_copy(gpart[k2][:, 1:2], grest[:]), "max_mid")
                            if kind == "gat":
                                w(dve, t, "leaky", "logit_summed")
                                signal(V.scalar_tensor_tensor(score[k1], score[k1], SLOPE, score[k1], ALU.mult, ALU.max), "leaky")
                                signal(V.tensor_tensor(cosine[k1], cosine[k1], rowv(k1)[:, :, F + 1], ALU.mult), "cos_scaled")
                            w(dve, t, "max_split", "max_mid")
                            signal(V.tensor_tensor(gpart[k2][:, 2:3], grest[:], gpart[k2][:, 1:2], ALU.subtract), "max_split")
                            if kind == "gat":
                                w(dve, t, "masked", "leaky")
                                signal(V.tensor_tensor(score[k1], score[k1], ex[:, :, F + 1], ALU.mult), "masked")
                                w(dve, t, "cos_kept", "cos_scaled")
                                signal(V.tensor_tensor(ecos[:, bass.ds(col[u - 1], C)], ecos[:, bass.ds(col[u - 1], C)], cosine[k1], ALU.add), "cos_kept")
                                w(dve, t, "scored", "masked")
                                signal(V.tensor_tensor(logit[:, bass.ds(col[u - 1], C)], logit[:, bass.ds(col[u - 1], C)], score[k1], ALU.add), "scored")
                            w(dve, t, "shifted", "max_edge")
                            w(dve, t, "shifted", "exped", RING)
                            signal(V.tensor_tensor(shift[k2], score[k2], max_b[:, 128:128 + C], ALU.subtract), "shifted")
                            now = top[0:R, bass.ds(off[u - 2], P)]
                            w(dve, t, "fall", "relus", 2)
                            w(dve, t, "fall", "top_moved", 1)
                            signal(V.tensor_tensor(drop[k2 % 2][0:R, :], now, max_b[0:R, 0:P], ALU.subtract), "fall")
                            signal(V.tensor_tensor(now, now, max_b[0:R, 0:P], ALU.max), "top_moved")
                        if kind == "mix":
                            ex = exp_b[k1 % 2][:, 0:C * dw].rearrange("p (c f) -> p c f", c=C)
                            w(dve, t, "below", "expanded")
                            w(dve, t, "below", "gat_part", RING)
                            signal(V.tensor_tensor(shift[k1], logit[:, bass.ds(col[u - 1], C)], ex[:, :, 0], ALU.subtract), "below")
                            signal(V.tensor_tensor(ccol[k1], ecos[:, bass.ds(col[u - 1], C)], ex[:, :, 2], ALU.mult), "cos_part")
                            signal(V.tensor_copy(gcol[k1], gate[:, bass.ds(col[u - 1], C)]), "gate_kept")
                            w(dve, t, "shifted", "below")
                            signal(V.tensor_tensor(shift[k1], shift[k1], ex[:, :, 3], ALU.mult), "shifted")
                            rows_in(dve, i, u, 3)
                            w(dve, t, "paid", "gated")
                            w(dve, t, "paid", "summed_", RING)
                            signal(V.tensor_tensor(pay[k3][:, :, 0:F], rowv(k3)[:, :, 0:F], pay[k3][:, :, F:F + 1].to_broadcast([P, C, F]),
                                                   ALU.mult), "paid")
                            exk = exp_b[k2 % 2][:, 0:C * dw].rearrange("p (c f) -> p c f", c=C)
                            w(dve, t, "gat_part", "exped")
                            w(dve, t, "gat_part", "gated", RING)
                            signal(V.tensor_tensor(score[k2], shift[k2], exk[:, :, 1], ALU.mult), "gat_part")
                            w(dve, t, "fused", "gat_part")
                            w(dve, t, "fused", "cos_part")
                            signal(V.tensor_tensor(score[k2], score[k2], ccol[k2], ALU.add), "fused")
                            w(dve, t, "weighed", "fused")
                            w(dve, t, "weighed", "gate_kept")
                            signal(V.tensor_tensor(score[k2], score[k2], gcol[k2], ALU.mult), "weighed")
                        k = (u - L["added"]) % RING
                        total_ = acc[0:R, bass.ds(off[u - L["added"]], P)]
                        if online:
                            w(dve, t, "old_scaled", "factors")
                            w(dve, t, "old_scaled", "added", 1)
                            signal(V.tensor_tensor(scaled[0:R, P:2 * P], total_, factor[k][0:R, 0:P], ALU.mult), "old_scaled")
                            w(dve, t, "new_scaled", "summed_")
                            signal(V.tensor_tensor(scaled[0:R, 0:P], sum_b[k % 2][0:R, 0:P], factor[k][0:R, P:2 * P], ALU.mult), "new_scaled")
                            if kind == "hgt":
                                w(dve, t, "paid", "exped")
                                w(dve, t, "paid", "summed_", RING)
                                signal(V.tensor_tensor(pay[k2][:, :, 0:F], rowv(k2)[:, :, F:2 * F], pay[k2][:, :, F:F + 1].to_broadcast([P, C, F]),
                                                       ALU.mult), "paid")
                            w(dve, t, "added", "new_scaled")
                            w(dve, t, "added", "old_scaled")
                            signal(V.tensor_tensor(total_, scaled[0:R, 0:P], scaled[0:R, P:2 * P], ALU.add), "added")
                        else:
                            w(dve, t, "added", "summed_")
                            w(dve, t, "added", "added", 1)
                            signal(V.tensor_tensor(total_, total_, sum_b[k % 2][0:R, 0:P], ALU.add), "added")
                    carry_round(dve, back, gback)

        carried = {}

        warm = small[:, 240:241]
        gmax = [sb(f"gmax{k}", [P, 2]) for k in range(RING)]
        gpart = [sb(f"gpart{k}", [P, 4], BF16) for k in range(RING)]
        grest = sb("grest", [P, 1])
        score = [small[:, 64 + 4 * k:68 + 4 * k] for k in range(RING)]
        cosine = [small[:, 96 + 4 * k:100 + 4 * k] for k in range(RING)]
        shift = [small[:, 128 + 4 * k:132 + 4 * k] for k in range(RING)]
        gcol = [small[:, 160 + 4 * k:164 + 4 * k] for k in range(RING)]
        ccol = [small[:, 192 + 4 * k:196 + 4 * k] for k in range(RING)]
        prod = sb("prod", [P, C, F])
        drop = [sb(f"drop{k}", [P, P]) for k in range(2)]
        relu2 = [sb(f"relu2{k}", [P, 2 * P]) for k in range(2)]
        factor = [sb(f"factor{k}", [P, 2 * P]) for k in range(RING)]
        scaled = sb("scaled", [P, 2 * P])
        ctx2 = ExitStack()

        def run_sweep(*a, **kw):
            nonlocal ctx2
            with ExitStack() as c2:
                ctx2 = c2
                sweep(*a, **kw)
            next_phase()

        def chunk(x, it):
            return x[bass.ds(it * CH, CH), :].rearrange("(p j) f -> p j f", j=J)

        def by_j(x, rows_, it):
            return x[0:rows_, bass.ds(it * CH, CH)].rearrange("r (p j) -> r j p", j=J)

        def area(k, at_, size):
            return work[0:k, at_:at_ + size]

        def jf(ap, f=F):
            return ap.rearrange("p (j f) -> p j f", j=J)

        def jp(ap):
            return ap.rearrange("r (j p) -> r j p", j=J)

        x_t, more_t, y_t, sq_t = (jf(area(Q, k * 256, 256)) for k in range(4))
        m1, m2, m3 = (area(Q, 1024 + 4 * k, 4) for k in range(3))
        t_a, t_b, t_c = (area(P, 1100 + 500 * k, 500) for k in range(3))
        s_row, d_row = (jf(area(Q, 2600 + 264 * k, 264), F + 2) for k in range(2))
        typed_t = area(Q, 3200, 1024).rearrange("p (j t f) -> p j t f", j=J, t=NT)
        typ_i, typ_f = area(Q, 4300, 4).bitcast(I32), area(Q, 4304, 4)
        masks = [area(Q, 4308 + 4 * t, 4) for t in range(NT)]

        def wide(v, f=F):
            return v.unsqueeze(2).to_broadcast([Q, J, f])

        def linker(dve, signal, it, per):
            count = [0]

            def link(ins):
                count[0] += 1
                ins.then_inc(signal, 1)
                dve.wait_ge(signal, it * per + count[0])
                assert count[0] <= per

            link.count = count
            return link

        def layernorm(dve, link, y, S, it):
            V = nc.vector
            link(V.tensor_reduce(m1, y, AX.X, ALU.add))
            link(V.tensor_scalar(m1, m1, 1.0 / F, None, ALU.mult))
            link(V.tensor_tensor(y, y, wide(m1), ALU.subtract))
            link(V.tensor_tensor(sq_t, y, y, ALU.mult))
            link(V.tensor_reduce(m2, sq_t, AX.X, ALU.add))
            V.tensor_scalar(m2, m2, 1.0 / F, LN_EPS, ALU.mult, ALU.add).then_inc(S["var_ready"], 1)
            dve.wait_ge(S["std_ready"], it + 1)
            link(V.reciprocal(m2, m3))
            V.tensor_tensor(y, y, wide(m2), ALU.mult).then_inc(S["y_ready"], 1)

        LN_LINKS = 6

        def deviation(act, S, it):
            act.wait_ge(S["var_ready"], it + 1)
            nc.scalar.activation(m3, m2, ACT.Sqrt).then_inc(S["std_ready"], 1)

        def node_mlp(tag, x_in, x_out, w1, b1, w2, b2, k1, m1_, source, extra=None):
            names = ["x_in", "x_turned", "h_ready", "hidden", "relu_ready", "mlp_out", "x_used", "y_ready", "y_stored", "var_ready", "std_ready", "link"]
            S = {n: psem(f"{tag}_{n}") for n in names}
            per = 1 + (1 if extra is not None else 0) + 1 + LN_LINKS - 1
            loads_n = 32 if extra is not None else 16
            with nc.Block() as block:
                @block.sync
                def _(sp):
                    def load(at_it):
                        sp.dma_start(x_t, chunk(x_in, at_it)).then_inc(S["x_in"], 16)
                        if extra is not None:
                            sp.dma_start(more_t, chunk(extra, at_it)).then_inc(S["x_in"], 16)

                    load(0)
                    sp.dma_start(trash_d[0:Q, 0:256].rearrange("p (j f) -> p j f", j=J), y_t).then_inc(S["y_stored"], 16)
                    with sp.Fori(0, CHUNKS) as it:
                        sp.wait_ge(S["x_used"], it + 1)
                        sp.nop(nofuse=True)
                        nxt = ahead(sp, it)
                        load(nxt)
                        sp.wait_ge(S["y_ready"], it + 1)
                        sp.nop(nofuse=True)
                        sp.dma_start(chunk(x_out, it), y_t).then_inc(S["y_stored"], 16)
                    sp.wait_ge(S["y_stored"], 16 * (CHUNKS + 1))
                    sp.wait_ge(S["x_in"], loads_n * (CHUNKS + 1))

                @block.tensor
                def _(pe):
                    with pe.Fori(0, CHUNKS) as it:
                        if source != "sums":
                            pe.wait_ge(S["x_in"], it * loads_n + loads_n)
                            for j in range(J):
                                mm = pe.matmul(bank[0][0:F, j * Q:(j + 1) * Q], x_t[:, j, :], ident[0:Q, 0:Q], start=True, stop=True)
                            mm.then_inc(S["x_turned"], 1)
                        pe.wait_ge(S["h_ready"], it + 1)
                        pe.nop(nofuse=True)
                        pe.matmul(bank[1][0:m1_, 0:CH], wt(w1, k1), t_a[0:k1, :], start=True, stop=True).then_inc(S["hidden"], 1)
                        pe.wait_ge(S["relu_ready"], it + 1)
                        for j in range(J):
                            mm = pe.matmul(bank[2][0:Q, j * F:(j + 1) * F], t_b[0:m1_, j * Q:(j + 1) * Q], wt(w2, m1_), start=True, stop=True)
                        mm.then_inc(S["mlp_out"], 1)

                @block.scalar
                def _(act):
                    nc.scalar.activation(warm, warm, ACT.Sqrt)
                    with act.Fori(0, CHUNKS) as it:
                        act.wait_ge(S["hidden"], it + 1)
                        nc.scalar.activation(t_b[0:m1_, :], bank[1][0:m1_, 0:CH], ACT.Relu, bias=bs(b1, m1_)).then_inc(S["relu_ready"], 1)
                        deviation(act, S, it)

                @block.vector
                def _(dve):
                    V = nc.vector
                    with dve.Fori(0, CHUNKS) as it:
                        link = linker(dve, S["link"], it, per)
                        if source == "x_and_sums":
                            dve.wait_ge(S["x_turned"], it + 1)
                            V.tensor_tensor(jp(t_a[0:F, :]), jp(bank[0][0:F, 0:CH]), by_j(acc, F, it), ALU.add).then_inc(S["h_ready"], 1)
                        elif source == "sums":
                            V.tensor_copy(jp(t_a[0:k1, :]), by_j(acc, k1, it)).then_inc(S["h_ready"], 1)
                        else:
                            dve.wait_ge(S["x_turned"], it + 1)
                            V.tensor_copy(t_a[0:F, :], bank[0][0:F, 0:CH]).then_inc(S["h_ready"], 1)
                        dve.wait_ge(S["mlp_out"], it + 1)
                        dve.wait_ge(S["y_stored"], it * 16 + 16)
                        dve.wait_ge(S["x_in"], it * loads_n + loads_n)
                        link(V.tensor_tensor(y_t, jf(bank[2][0:Q, 0:256]), bs(b2, Q).unsqueeze(1).to_broadcast([Q, J, F]), ALU.add))
                        if extra is not None:
                            link(V.tensor_tensor(y_t, y_t, more_t, ALU.add))
                        V.tensor_tensor(y_t, y_t, x_t, ALU.add).then_inc(S["x_used"], 1)
                        dve.wait_ge(S["x_used"], it + 1)
                        layernorm(dve, link, y_t, S, it)
                        dve.wait_ge(S["y_ready"], it + 1)
                        assert link.count[0] == per

        def ahead(eng, it):
            key = str(eng.engine)
            if key not in next_reg:
                next_reg[key] = eng.alloc_register("next_chunk")
            eng.reg_alu(next_reg[key], it + 1, CHUNKS - 1, ALU.min)
            return eng.snap(next_reg[key], min_val=0, max_val=CHUNKS - 1)

        next_reg = {}

        def in_parts(dve, link, parts, x, last):
            V = nc.vector
            link(V.tensor_copy(parts[:, :, 0, :], x))
            link(V.tensor_tensor(x, x, parts[:, :, 0, :], ALU.subtract))
            link(V.tensor_copy(parts[:, :, 1, :], x))
            V.tensor_tensor(parts[:, :, 2, :], x, parts[:, :, 1, :], ALU.subtract).then_inc(last, 1)

        parts_t = area(Q, 5000, 396).bitcast(BF16).rearrange("p (j q f) -> p j q f", j=J, q=3)
        stat_parts = area(Q, 5400, 24).bitcast(BF16).rearrange("p (j q f) -> p j q f", j=J, q=3)

        def flat_parts(parts):
            return parts.rearrange("p j q f -> p j (q f)")

        def node_gat_tables(tag, x_in, layer):
            S = {n: psem(f"{tag}_{n}") for n in ("x_in", "x_turned", "h_ready", "logits", "x_used", "rows_ready", "rows_stored", "var_ready", "std_ready", "link")}
            per = 6 + 4
            with nc.Block() as block:
                @block.sync
                def _(sp):
                    sp.dma_start(x_t, chunk(x_in, 0)).then_inc(S["x_in"], 16)
                    sp.wait_ge(S["rows_ready"], 1)
                    sp.dma_start(trash_d[0:Q, :].rearrange("p (j f) -> p j f", j=J), s_row).then_inc(S["rows_stored"], 16)
                    with sp.Fori(0, CHUNKS) as it:
                        sp.wait_ge(S["x_used"], it + 1)
                        sp.nop(nofuse=True)
                        sp.dma_start(x_t, chunk(x_in, ahead(sp, it))).then_inc(S["x_in"], 16)
                        sp.wait_ge(S["rows_ready"], it + 2)
                        sp.nop(nofuse=True)
                        sp.dma_start(chunk(srctab_d, it), s_row).then_inc(S["rows_stored"], 16)
                        sp.dma_start(chunk(dsttab_d, it), flat_parts(parts_t)).then_inc(S["rows_stored"], 16)
                    sp.wait_ge(S["rows_stored"], 32 * CHUNKS + 16)
                    sp.wait_ge(S["x_in"], 16 * (CHUNKS + 1))

                @block.tensor
                def _(pe):
                    with pe.Fori(0, CHUNKS) as it:
                        pe.wait_ge(S["x_in"], it * 16 + 16)
                        for j in range(J):
                            mm = pe.matmul(bank[0][0:F, j * Q:(j + 1) * Q], x_t[:, j, :], ident[0:Q, 0:Q], start=True, stop=True)
                        mm.then_inc(S["x_turned"], 1)
                        pe.wait_ge(S["h_ready"], it + 1)
                        for j in range(J):
                            mm = pe.matmul(bank[1][0:Q, 2 * j:2 * j + 2], t_a[0:F, j * Q:(j + 1) * Q], wt(f"U{layer}"), start=True, stop=True)
                        mm.then_inc(S["logits"], 1)

                @block.scalar
                def _(act):
                    nc.scalar.activation(warm, warm, ACT.Sqrt)
                    with act.Fori(0, CHUNKS) as it:
                        deviation(act, S, it)

                @block.vector
                def _(dve):
                    V = nc.vector
                    V.memset(work[0:Q, 2600:2600 + 528], 1.0).then_inc(S["rows_ready"], 1)
                    dve.wait_ge(S["rows_ready"], 1)
                    with dve.Fori(0, CHUNKS) as it:
                        link = linker(dve, S["link"], it, per)
                        dve.wait_ge(S["x_turned"], it + 1)
                        V.tensor_copy(t_a[0:F, :], bank[0][0:F, 0:CH]).then_inc(S["h_ready"], 1)
                        link(V.tensor_tensor(sq_t, x_t, x_t, ALU.mult))
                        link(V.tensor_reduce(m1, sq_t, AX.X, ALU.add))
                        V.tensor_scalar(m2, m1, COS_EPS2, None, ALU.max).then_inc(S["var_ready"], 1)
                        dve.wait_ge(S["std_ready"], it + 1)
                        link(V.reciprocal(m1, m3))
                        dve.wait_ge(S["rows_stored"], it * 32 + 16)
                        link(V.tensor_copy(s_row[:, :, 0:F], x_t))
                        link(V.tensor_copy(s_row[:, :, F + 1], m1))
                        V.memset(d_row[:, :, F + 1], 1.0)
                        V.tensor_tensor(d_row[:, :, 0:F], x_t, wide(m1), ALU.mult).then_inc(S["x_used"], 1)
                        dve.wait_ge(S["logits"], it + 1)
                        lg = jf(bank[1][0:Q, 0:2 * J], 2)
                        link(V.tensor_copy(s_row[:, :, F], lg[:, :, 1]))
                        link(V.tensor_copy(d_row[:, :, F], lg[:, :, 0]))
                        in_parts(dve, link, parts_t, d_row, S["rows_ready"])
                        dve.wait_ge(S["rows_ready"], it + 2)
                        assert link.count[0] == per

        def node_stats(tag, layer):
            S = {n: psem(f"{tag}_{n}") for n in ("rows_copied", "stats_turned", "stats_ready", "stats_stored", "link", "cos_exped")}
            stat_t = jf(area(Q, 2600, 16), 4)
            mix = wts[0:Q, wcols["mix"][0] + 2 * layer:wcols["mix"][0] + 2 * layer + 2]
            per = 4 + 4
            with nc.Block() as block:
                @block.sync
                def _(sp):
                    sp.wait_ge(S["stats_ready"], 1)
                    sp.dma_start(trash_d[0:Q, 0:16].rearrange("p (j f) -> p j f", j=J), stat_t).then_inc(S["stats_stored"], 16)
                    with sp.Fori(0, CHUNKS) as it:
                        sp.wait_ge(S["stats_ready"], it + 2)
                        sp.nop(nofuse=True)
                        sp.dma_start(chunk(stat_d, it), flat_parts(stat_parts)).then_inc(S["stats_stored"], 16)
                    sp.wait_ge(S["stats_stored"], 16 * CHUNKS + 16)

                @block.scalar
                def _(act):
                    nc.scalar.activation(ecos[:], ecos[:], ACT.Exp).then_inc(S["cos_exped"], 1)
                    act.wait_ge(S["cos_exped"], 1)

                @block.tensor
                def _(pe):
                    with pe.Fori(0, CHUNKS) as it:
                        pe.wait_ge(S["rows_copied"], it + 1)
                        for j in range(J):
                            pe.matmul(bank[0][0:Q, 4 * j:4 * j + 1], t_a[0:1, j * Q:(j + 1) * Q], ident[0:1, 0:1], start=True, stop=True)
                            mm = pe.matmul(bank[0][0:Q, 4 * j + 1:4 * j + 3], t_b[0:2, j * Q:(j + 1) * Q], ident[0:2, 0:2], start=True, stop=True)
                        mm.then_inc(S["stats_turned"], 1)

                @block.vector
                def _(dve):
                    V = nc.vector
                    V.memset(stat_t, 1.0).then_inc(S["stats_ready"], 1)
                    dve.wait_ge(S["stats_ready"], 1)
                    with dve.Fori(0, CHUNKS) as it:
                        link = linker(dve, S["link"], it, per)
                        link(V.tensor_copy(jp(t_a[0:1, :]), by_j(top, 1, it)))
                        V.tensor_copy(jp(t_b[0:2, :]), by_j(acc, 2, it)).then_inc(S["rows_copied"], 1)
                        dve.wait_ge(S["stats_turned"], it + 1)
                        dve.wait_ge(S["stats_stored"], it * 16 + 16)
                        ps = jf(bank[0][0:Q, 0:16], 4)
                        link(V.tensor_copy(stat_t[:, :, 0], ps[:, :, 0]))
                        link(V.tensor_scalar(stat_t[:, :, 1:3], ps[:, :, 1:3], SM_EPS, None, ALU.add))
                        link(V.reciprocal(stat_t[:, :, 1:3], stat_t[:, :, 1:3]))
                        V.memset(stat_t[:, :, 3], 1.0)
                        link(V.tensor_tensor(stat_t[:, :, 1:3], stat_t[:, :, 1:3], mix.unsqueeze(1).to_broadcast([Q, J, 2]), ALU.mult))
                        in_parts(dve, link, stat_parts, stat_t, S["stats_ready"])
                        dve.wait_ge(S["stats_ready"], it + 2)
                        assert link.count[0] == per

        def node_gat_out(tag, layer, h_out, twice):
            S = {n: psem(f"{tag}_{n}") for n in ("h_ready", "out_ready", "low", "exped", "h_made", "h_stored", "link")}
            rounds = 2 if twice else 1
            per = 4 + 1 + (rounds - 1) * 2
            with nc.Block() as block:
                @block.sync
                def _(sp):
                    sp.dma_start(trash_d[0:Q, 0:256].rearrange("p (j f) -> p j f", j=J), y_t).then_inc(S["h_stored"], 16)
                    with sp.Fori(0, CHUNKS) as it:
                        sp.wait_ge(S["h_made"], it + 1)
                        sp.nop(nofuse=True)
                        sp.dma_start(chunk(h_out, it), y_t).then_inc(S["h_stored"], 16)
                    sp.wait_ge(S["h_stored"], 16 * CHUNKS + 16)

                @block.tensor
                def _(pe):
                    with pe.Fori(0, CHUNKS) as it:
                        pe.wait_ge(S["h_ready"], it + 1)
                        for j in range(J):
                            mm = pe.matmul(bank[0][0:Q, j * (F + 1):(j + 1) * (F + 1)], t_a[0:F + 1, j * Q:(j + 1) * Q],
                                           wt(f"G{layer}", F + 1), start=True, stop=True)
                        mm.then_inc(S["out_ready"], 1)

                @block.scalar
                def _(act):
                    with act.Fori(0, CHUNKS) as it:
                        for r in range(rounds):
                            act.wait_ge(S["low"], it * rounds + r + 1)
                            nc.scalar.activation(sq_t, sq_t, ACT.Exp).then_inc(S["exped"], 1)

                @block.vector
                def _(dve):
                    V = nc.vector
                    with dve.Fori(0, CHUNKS) as it:
                        link = linker(dve, S["link"], it, per)
                        V.tensor_copy(jp(t_a[0:F + 1, :]), by_j(acc, F + 1, it)).then_inc(S["h_ready"], 1)
                        dve.wait_ge(S["out_ready"], it + 1)
                        ps = jf(bank[0][0:Q, 0:J * (F + 1)], F + 1)
                        link(V.tensor_scalar(m1, ps[:, :, F], SM_EPS, None, ALU.add))
                        link(V.reciprocal(m1, m1))
                        dve.wait_ge(S["h_stored"], it * 16 + 16)
                        link(V.tensor_tensor(y_t, ps[:, :, 0:F], wide(m1), ALU.mult))
                        link(V.tensor_tensor(y_t, y_t, bs(f"bg{layer}", Q).unsqueeze(1).to_broadcast([Q, J, F]), ALU.add))
                        for r in range(rounds):
                            V.tensor_scalar(sq_t, y_t, 0.0, None, ALU.min).then_inc(S["low"], 1)
                            link(V.tensor_scalar(y_t, y_t, 0.0, None, ALU.max))
                            dve.wait_ge(S["exped"], it * rounds + r + 1)
                            last = V.scalar_tensor_tensor(y_t, sq_t, -1.0, y_t, ALU.add, ALU.add)
                            if r < rounds - 1:
                                link(last)
                        last.then_inc(S["h_made"], 1)
                        dve.wait_ge(S["h_made"], it + 1)
                        assert link.count[0] == per

        def typed(link, last, x):
            V = nc.vector
            for t in range(NT):
                ins = V.tensor_tensor(typed_t[:, :, t, :], x, wide(masks[t]), ALU.mult)
                if t < NT - 1:
                    link(ins)
            ins.then_inc(last, 1)

        def make_masks(link):
            V = nc.vector
            link(V.tensor_copy(typ_f, typ_i))
            for t in range(NT):
                link(V.tensor_scalar(masks[t], typ_f, float(t), None, ALU.is_equal))

        def turn_typed(pe, signal):
            for h in range(2):
                for j in range(J):
                    mm = pe.matmul(bank[h][:, j * Q:(j + 1) * Q], typed_t[:, j, 2 * h:2 * h + 2, :].rearrange("p t f -> p (t f)"),
                                   ident[0:Q, 0:Q], start=True, stop=True)
            mm.then_inc(signal, 1)

        types = io["node_type_4"].rearrange("(n j) -> n j", j=J)
        rel_t = top[0:Q, 0:NR * J * 2 * F].rearrange("p (r j f) -> p r j f", r=NR, j=J)

        def node_relations(tag, x_in):
            S = {n: psem(f"{tag}_{n}") for n in ("x_in", "typed", "turned", "half0", "half1", "kv", "k_copied", "v_copied", "q_ready",
                                                "rel_out", "att_copied", "msg_copied", "q_copied", "q_set", "stored", "link")}
            per = 5 + NT - 1 + 4
            wk, wq, wv = (wt(n, P).rearrange("p (h e) -> p h e", h=2) for n in ("K", "Qw", "V"))
            with nc.Block() as block:
                @block.sync
                def _(sp):
                    def load(at_it):
                        sp.dma_start(x_t, chunk(x_in, at_it)).then_inc(S["x_in"], 16)
                        sp.dma_start(typ_i, types[bass.ds(at_it * Q, Q), :]).then_inc(S["x_in"], 16)

                    load(0)
                    sp.wait_ge(S["q_set"], 1)
                    sp.dma_start(trash_d[0:Q, :].rearrange("p (j f) -> p j f", j=J), d_row).then_inc(S["stored"], 16)
                    with sp.Fori(0, CHUNKS) as it:
                        sp.wait_ge(S["typed"], it + 1)
                        sp.nop(nofuse=True)
                        load(ahead(sp, it))
                        sp.wait_ge(S["q_copied"], it + 1)
                        sp.nop(nofuse=True)
                        sp.dma_start(chunk(dsttab_d, it), flat_parts(parts_t)).then_inc(S["stored"], 16)
                        sp.wait_ge(S["att_copied"], it * J + J)
                        sp.wait_ge(S["msg_copied"], it * J + J)
                        sp.nop(nofuse=True)
                        for r in range(NR):
                            sp.dma_start(reltab_d[r * N:(r + 1) * N, :][bass.ds(it * CH, CH), :].rearrange("(p j) f -> p j f", j=J),
                                         rel_t[:, r, :, :]).then_inc(S["stored"], 16)
                    sp.wait_ge(S["stored"], 16 + (NR + 1) * 16 * CHUNKS)
                    sp.wait_ge(S["x_in"], 32 * (CHUNKS + 1))

                @block.tensor
                def _(pe):
                    with pe.Fori(0, CHUNKS) as it:
                        pe.wait_ge(S["typed"], it + 1)
                        turn_typed(pe, S["turned"])
                        pe.wait_ge(S["half0"], it + 1)
                        pe.wait_ge(S["half1"], it + 1)
                        for b, w_ in ((2, wk), (3, wv)):
                            for h in range(2):
                                mm = pe.matmul(bank[b][0:F, 0:CH], w_[:, h, :], (t_a, t_b)[h], start=h == 0, stop=h == 1)
                        mm.then_inc(S["kv"], 1)
                        for j in range(J):
                            for h in range(2):
                                mm = pe.matmul(bank[4][0:Q, j * F:(j + 1) * F], (t_a, t_b)[h][:, j * Q:(j + 1) * Q], wq[:, h, :],
                                               start=h == 0, stop=h == 1)
                        mm.then_inc(S["q_ready"], 1)
                        pe.wait_ge(S["k_copied"], it + 1)
                        pe.wait_ge(S["v_copied"], it + 1)
                        for j in range(J):
                            if j >= 2:
                                pe.wait_ge(S["att_copied"], it * J + j - 1)
                                pe.wait_ge(S["msg_copied"], it * J + j - 1)
                            pe.matmul(bank[5 + j % 2][0:Q, :], t_c[0:F, j * Q:(j + 1) * Q], wt("RA"), start=True, stop=True)
                            pe.matmul(bank[7 * (1 - j % 2)][0:Q, :], vT[0:F, j * Q:(j + 1) * Q], wt("RM"), start=True, stop=True).then_inc(S["rel_out"], 1)
                        pe.wait_ge(S["msg_copied"], it * J + J)

                @block.scalar
                def _(act):
                    with act.Fori(0, CHUNKS) as it:
                        act.wait_ge(S["turned"], it + 1)
                        nc.scalar.copy(t_a, bank[0][:, 0:CH]).then_inc(S["half0"], 1)
                        act.wait_ge(S["kv"], it + 1)
                        nc.scalar.copy(t_c[0:F, :], bank[2][0:F, 0:CH]).then_inc(S["k_copied"], 1)
                        act.wait_ge(S["stored"], it * (NR + 1) * 16 + 16)
                        for j in range(J):
                            act.wait_ge(S["rel_out"], it * J + j + 1)
                            nc.scalar.copy(rel_t[:, :, j, 0:F], bank[5 + j % 2][0:Q, :].rearrange("p (r d) -> p r d", r=NR)).then_inc(S["att_copied"], 1)

                @block.vector
                def _(dve):
                    V = nc.vector
                    V.memset(d_row, 1.0).then_inc(S["q_set"], 1)
                    dve.wait_ge(S["q_set"], 1)
                    with dve.Fori(0, CHUNKS) as it:
                        link = linker(dve, S["link"], it, per)
                        dve.wait_ge(S["x_in"], it * 32 + 32)
                        make_masks(link)
                        typed(link, S["typed"], x_t)
                        dve.wait_ge(S["turned"], it + 1)
                        V.tensor_copy(t_b, bank[1][:, 0:CH]).then_inc(S["half1"], 1)
                        dve.wait_ge(S["kv"], it + 1)
                        V.tensor_copy(vT[0:F, :], bank[3][0:F, 0:CH]).then_inc(S["v_copied"], 1)
                        dve.wait_ge(S["stored"], it * (NR + 1) * 16 + 16)
                        dve.wait_ge(S["q_ready"], it + 1)
                        V.memset(d_row[:, :, F:], 1.0)
                        link(V.tensor_copy(d_row[:, :, 0:F], jf(bank[4][0:Q, 0:256])))
                        in_parts(dve, link, parts_t, d_row, S["q_copied"])
                        for j in range(J):
                            dve.wait_ge(S["rel_out"], it * J + j + 1)
                            V.tensor_copy(rel_t[:, :, j, F:2 * F], bank[7 * (1 - j % 2)][0:Q, :].rearrange("p (r d) -> p r d", r=NR)).then_inc(S["msg_copied"], 1)
                        assert link.count[0] == per

        vT = area(P, 4400, 500)

        def node_last(tag, x_in):
            S = {n: psem(f"{tag}_{n}") for n in ("x_in", "h_ready", "sums_turned", "typed", "turned", "half0", "half1", "mapped", "x_used",
                                                "y_ready", "y_stored", "var_ready", "std_ready", "link")}
            per = 5 + 4 + NT - 1 + LN_LINKS
            wa = wt("A", P).rearrange("p (h e) -> p h e", h=2)
            with nc.Block() as block:
                @block.sync
                def _(sp):
                    def load(at_it):
                        sp.dma_start(x_t, chunk(x_in, at_it)).then_inc(S["x_in"], 16)
                        sp.dma_start(typ_i, types[bass.ds(at_it * Q, Q), :]).then_inc(S["x_in"], 16)

                    load(0)
                    sp.dma_start(trash_d[0:Q, 0:256].rearrange("p (j f) -> p j f", j=J), y_t).then_inc(S["y_stored"], 16)
                    with sp.Fori(0, CHUNKS) as it:
                        sp.wait_ge(S["x_used"], it + 1)
                        sp.nop(nofuse=True)
                        load(ahead(sp, it))
                        sp.wait_ge(S["y_ready"], it + 1)
                        sp.nop(nofuse=True)
                        sp.dma_start(chunk(out, it), y_t).then_inc(S["y_stored"], 16)
                    sp.wait_ge(S["y_stored"], 16 * (CHUNKS + 1))
                    sp.wait_ge(S["x_in"], 32 * (CHUNKS + 1))

                @block.tensor
                def _(pe):
                    with pe.Fori(0, CHUNKS) as it:
                        pe.wait_ge(S["h_ready"], it + 1)
                        for j in range(J):
                            mm = pe.matmul(bank[2][0:Q, j * (F + 1):(j + 1) * (F + 1)], t_c[0:F + 1, j * Q:(j + 1) * Q],
                                           ident[0:F + 1, 0:F + 1], start=True, stop=True)
                        mm.then_inc(S["sums_turned"], 1)
                        pe.wait_ge(S["typed"], it + 1)
                        turn_typed(pe, S["turned"])
                        pe.wait_ge(S["half0"], it + 1)
                        pe.wait_ge(S["half1"], it + 1)
                        for j in range(J):
                            for h in range(2):
                                mm = pe.matmul(bank[3][0:Q, j * F:(j + 1) * F], (t_a, t_b)[h][:, j * Q:(j + 1) * Q], wa[:, h, :],
                                               start=h == 0, stop=h == 1)
                        mm.then_inc(S["mapped"], 1)

                @block.scalar
                def _(act):
                    nc.scalar.activation(warm, warm, ACT.Sqrt)
                    with act.Fori(0, CHUNKS) as it:
                        act.wait_ge(S["turned"], it + 1)
                        nc.scalar.copy(t_a, bank[0][:, 0:CH]).then_inc(S["half0"], 1)
                        deviation(act, S, it)

                @block.vector
                def _(dve):
                    V = nc.vector
                    with dve.Fori(0, CHUNKS) as it:
                        link = linker(dve, S["link"], it, per)
                        V.tensor_copy(jp(t_c[0:F + 1, :]), by_j(acc, F + 1, it)).then_inc(S["h_ready"], 1)
                        dve.wait_ge(S["x_in"], it * 32 + 32)
                        make_masks(link)
                        dve.wait_ge(S["sums_turned"], it + 1)
                        ps = jf(bank[2][0:Q, 0:J * (F + 1)], F + 1)
                        link(V.tensor_scalar(m1, ps[:, :, F], 0.0, None, ALU.is_equal))
                        link(V.tensor_tensor(m1, m1, ps[:, :, F], ALU.add))
                        link(V.reciprocal(m1, m1))
                        link(V.tensor_tensor(more_t, ps[:, :, 0:F], wide(m1), ALU.mult))
                        typed(link, S["typed"], more_t)
                        dve.wait_ge(S["turned"], it + 1)
                        V.tensor_copy(t_b, bank[1][:, 0:CH]).then_inc(S["half1"], 1)
                        dve.wait_ge(S["mapped"], it + 1)
                        dve.wait_ge(S["y_stored"], it * 16 + 16)
                        V.tensor_tensor(y_t, jf(bank[3][0:Q, 0:256]), x_t, ALU.add).then_inc(S["x_used"], 1)
                        dve.wait_ge(S["x_used"], it + 1)
                        layernorm(dve, link, y_t, S, it)
                        dve.wait_ge(S["y_ready"], it + 1)
                        assert link.count[0] == per

        run_sweep("s0", "sum_attr", io["x"], src_d)
        node_mlp("n0", io["x"], x1_d, "W01", "b01", "W02", "b02", F, F, "x_and_sums")
        next_phase()
        run_sweep("s1", "sum", x1_d, src_d)
        node_mlp("n1", x1_d, x2_d, "W11", "b11", "W12", "b12", P, P, "sums")
        next_phase()
        for layer, x_l, h_l in ((0, x2_d, h1_d), (1, h1_d, h2_d)):
            node_gat_tables(f"t{layer}", x_l, layer)
            next_phase()
            run_sweep(f"a{layer}", "gat", srctab_d, src_d)
            node_stats(f"st{layer}", layer)
            next_phase()
            run_sweep(f"b{layer}", "mix")
            node_gat_out(f"h{layer}", layer, h_l, layer == 0)
            next_phase()
        node_mlp("n2", x2_d, x3_d, "R1", "rb1", "R2", "rb2", F, F, "x", extra=h2_d)
        next_phase()
        node_relations("r", x3_d)
        next_phase()
        run_sweep("s3", "hgt", reltab_d, rel_d)
        node_last("last", x3_d)
        next_phase()


_INS = ['x', 'src', 'dst', 'edge_attr_64', 'edge_type_8', 'edge_weight', 'node_type_4', 'L0_gnn_W1', 'L0_gnn_b1',
        'L0_gnn_W2', 'L0_gnn_b2', 'L1_gnn_W1', 'L1_gnn_b1', 'L1_gnn_W2', 'L1_gnn_b2', 'L2_gnn_W0', 'L2_gnn_att0',
        'L2_gnn_beta0', 'L2_gnn_b0', 'L2_gnn_W1', 'L2_gnn_att1', 'L2_gnn_beta1', 'L2_gnn_b1', 'L2_gnn_rW1',
        'L2_gnn_rb1', 'L2_gnn_rW2', 'L2_gnn_rb2', 'L3_gnn_k_lin', 'L3_gnn_q_lin', 'L3_gnn_v_lin', 'L3_gnn_a_lin',
        'L3_gnn_rel_att', 'L3_gnn_rel_msg', 'L3_gnn_rel_pri', 'L3_gnn_skip']


def kernel(**inputs):
    import numpy as _np
    import concourse.bacc as _bacc
    from concourse import mybir as _mybir
    from concourse.bass_utils import run_bass_kernel_spmd as _run

    nc = _bacc.Bacc("TRN2", target_bir_lowering=False, num_devices=1)
    arrays, io = {}, {}
    for name in _INS:
        a = _np.asarray(inputs[name])
        if name == "L3_gnn_rel_att":
            a = a.transpose(2, 0, 1).reshape(64, -1)
        elif name == "L3_gnn_rel_msg":
            a = a.transpose(1, 0, 2).reshape(64, -1)
        elif name.endswith("_lin"):
            a = a.reshape(-1, a.shape[-1])
        a = _np.ascontiguousarray(a)
        arrays[f"in_{name}_dram"] = a
        io[name] = nc.dram_tensor(f"in_{name}_dram", a.shape, _mybir.dt.from_np(a.dtype), kind="ExternalInput").ap()
    out = nc.dram_tensor("out_0_dram", (12500, 64), _mybir.dt.float32, kind="ExternalOutput").ap()
    build(nc, io, out)
    r = _run(nc, [arrays], core_ids=[0])
    return r.results[0]["out_0_dram"]
```

```python
from contextlib import ExitStack

import concourse.bass as bass
from concourse import mybir

ALU = mybir.AluOpType
ACT = mybir.ActivationFunctionType
AX = mybir.AxisListType
F32 = mybir.dt.float32
BF16 = mybir.dt.bfloat16
I16 = mybir.dt.int16
I32 = mybir.dt.int32
U32 = mybir.dt.uint32

P = 128
C = 4
GE = P * C
N, E, F = 12500, 200000, 64
NT, NR = 4, 8
FULL = E // GE
STEPS = 8
GROUPS = -(-(FULL + 1) // STEPS) * STEPS
TAIL = E - GE
OVER = (FULL + 1) * GE - E
WIN = -(-N // P)
ND = -(-(N + P) // P) * P
OFF_IDLE = N
RING = 4
LAG = 4
ROUNDS = -(-(GROUPS * WIN + LAG + STEPS) // (STEPS * P)) * P
HALVES = 2 * ROUNDS + P
PRIME = 8
Q, J = 125, 4
CH = Q * J
CHUNKS = N // CH
BIG = 2.0 ** 99
LN_EPS = 1e-5
SM_EPS = 1e-16
COS_EPS2 = 1e-16
SLOPE = 0.2


def build(nc, io, out):
    with ExitStack() as ctx:
        def sb(name, shape, dt=F32):
            return ctx.enter_context(nc.sbuf_tensor(name, shape, dt))

        def sem(name):
            return ctx.enter_context(nc.semaphore(name))

        phase_sems = []

        def psem(name):
            phase_sems.append(nc.alloc_semaphore(name))
            return phase_sems[-1]

        def next_phase():
            nc.clear_and_free_semaphores(list(phase_sems))
            nc.all_engine_barrier()
            phase_sems.clear()

        def dram(name, shape, dt=F32):
            return nc.dram_tensor(name, shape, dt).ap()

        x1_d, x2_d, x3_d, h1_d, h2_d = (dram(f"{n}_d", (N, F)) for n in ("x1", "x2", "x3", "h1", "h2"))
        src_d = dram("src_d", (GROUPS + 1, P, C), I32)
        rel_d = dram("rel_d", (GROUPS + 1, P, C), I32)
        iota_d = dram("iota_d", (ND, 1), I32)
        base_d = dram("base_d", (GROUPS, 1), I32)
        nwin_d = dram("nwin_d", (GROUPS, 1), I32)
        sched_d = dram("sched_d", (HALVES, 2 * RING), I32)
        iters_d = dram("iters_d", (1, 2), I32)
        srctab_d = dram("srctab_d", (N, F + 2))
        dsttab_d = dram("dsttab_d", (ND, 3 * (F + 2)), BF16)
        stat_d = dram("stat_d", (ND, 3 * 4), BF16)
        stash_d = dram("stash_d", (GROUPS + 1, P, C * (F + 2)))
        reltab_d = dram("reltab_d", (NR * N, 2 * F))
        trash_d = dram("trash_d", (P, C * (F + 2)))

        acc = sb("acc", [P, ND])
        top = sb("top", [P, ND])
        iota16 = sb("iota16", [P, ND], I16)
        dstf = sb("dstf", [P, GROUPS * C + C])
        gate = sb("gate", [P, GROUPS * C + C])
        logit = sb("logit", [P, GROUPS * C + C])
        ecos = sb("ecos", [P, GROUPS * C + C])
        ident = sb("ident", [P, P])
        work = sb("work", [P, 5440])
        rows = [sb(f"rows{k}", [P, C, 2 * F]) for k in range(RING)]
        pay = [sb(f"pay{k}", [P, C, F + 1]) for k in range(RING)]
        dwin = [sb(f"dwin{k}", [P, 3 * (F + 2)], BF16) for k in range(RING)]
        idx = [sb(f"idx{k}", [P, C], I32) for k in range(RING)]
        small = sb("small", [P, 256])
        wts = sb("wts", [P, 2400])
        bias = sb("bias", [P, 640])
        bank = [ctx.enter_context(nc.psum_tensor(f"bank{b}", [P, 512], F32)) for b in range(8)]

        onehot = [work[:, k * 512:(k + 1) * 512].rearrange("p (c n) -> p c n", c=C) for k in range(RING)]
        turned = [work[:, 2048 + k * 256:2048 + (k + 1) * 256].bitcast(BF16) for k in range(RING)]
        block_ = [work[:, 3072 + k * 256:3072 + (k + 1) * 256].bitcast(BF16) for k in range(RING)]

        at, wcols, bcols = 0, {}, {}
        for name, w in (("W01", 64), ("W02", 64), ("W11", 128), ("W12", 64), ("G0", 65), ("G1", 65), ("R1", 64),
                        ("R2", 64), ("K", 128), ("Qw", 128), ("V", 128), ("A", 128), ("RA", 512), ("RM", 512),
                        ("U0", 2), ("U1", 2), ("pri", 8), ("skip", 2), ("beta", 2), ("mix", 4)):
            wcols[name] = (at, at + w)
            at += w
        at = 0
        for name, w in (("b02", 64), ("b12", 64), ("bg0", 64), ("bg1", 64), ("rb2", 64), ("att0", 128), ("att1", 128),
                        ("b01", 1), ("b11", 1), ("rb1", 1)):
            bcols[name] = (at, at + w)
            at += w

        def wt(name, k=64):
            a, b = wcols[name]
            return wts[0:k, a:b]

        def bs(name, k=P):
            a, b = bcols[name]
            return bias[0:k, a:b]

        def grouped(x):
            return x[0:FULL * GE].rearrange("(g p c) -> p g c", p=P, c=C)

        def tail(x):
            return x[TAIL:E].rearrange("(p c) -> p c", c=C)

        loaded, made, stored, sched = (sem(n) for n in ("loaded", "made", "prep_stored", "sched_stored"))
        acted, pooled, summed = sem("prep_acted"), sem("prep_pooled"), sem("steps_summed")
        cols = C * GROUPS
        raw_i = [top[:, k * 2048:k * 2048 + cols].bitcast(I32) for k in range(4)]
        raw_f = [acc[:, k * 2048:k * 2048 + cols] for k in range(6)]
        QP = GROUPS // 4
        spans = top[0:QP, 8192:8192 + 2048].bitcast(I32).rearrange("p (g e) -> p g e", g=4)
        spansf = acc[0:QP, 10240:10240 + 2048].rearrange("p (g e) -> p g e", g=4)
        lo, hi, nwin = small[0:QP, 0:4], small[0:QP, 4:8], small[0:QP, 8:12]
        lo_i, hi_i = small[0:QP, 16:20].bitcast(I32), small[0:QP, 20:24].bitcast(I32)
        nsum = small[0:QP, 24:25]
        total, total_i = small[0:1, 32:34], small[0:1, 36:38].bitcast(I32)
        idle = work[:, 0:HALVES // P * 2 * RING].bitcast(I32).rearrange("p (a b) -> p a b", b=2 * RING)
        iota_i = work[:, 1024:1024 + ND // P].bitcast(I32)
        dpad = work[:, 1200:1200 + 3 * (F + 2)].bitcast(BF16).rearrange("p (a b) -> p a b", a=2)
        zero_i = work[:, 2048:2048 + C].bitcast(I32)
        ones = small[:, 40:41]
        prod64 = work[0:64, 3072:3136]
        sg = wts[:, wcols["skip"][0]:wcols["beta"][1]]
        rel_made, windows_made, counts_made, total_made = (sem(n) for n in ("rel_made", "windows_made", "counts_made", "total_made"))

        with nc.Block() as block:
            loads = []

            @block.sync
            def _(sp):
                def load(dst, src):
                    loads.append(1)
                    sp.dma_start(dst, src).then_inc(loaded, 16)

                for k, name in enumerate(("dst", "src", "edge_weight", "edge_type_8")):
                    t = raw_i[k] if name != "edge_weight" else raw_f[5]
                    load(t[:, 0:C * FULL].rearrange("p (g c) -> p g c", c=C), grouped(io[name]))
                    for g in range(FULL, GROUPS):
                        load(t[:, C * g:C * g + C], tail(io[name]))
                full4 = FULL // 4
                load(spans[0:full4, :, :], io["dst"][0:full4 * 4 * GE].rearrange("(p g e) -> p g e", g=4, e=GE))
                for g in range(full4 * 4, GROUPS):
                    a = min(g * GE, TAIL)
                    load(spans[g // 4:g // 4 + 1, g % 4, :], io["dst"][a:a + GE].rearrange("(p e) -> p e", p=1))
                sp.wait_ge(pooled, 1)
                for name, key, k in (("W01", "L0_gnn_W1", 64), ("W02", "L0_gnn_W2", 64), ("W12", "L1_gnn_W2", 128),
                                     ("R1", "L2_gnn_rW1", 64), ("R2", "L2_gnn_rW2", 64)):
                    load(wt(name, k), io[key])
                load(wts[0:64, wcols["W11"][0]:wcols["W11"][1]], io["L1_gnn_W1"])
                load(wts[64:128, wcols["W11"][0]:wcols["W11"][1]], io["L1_gnn_W1"])
                for name, key in (("G0", "L2_gnn_W0"), ("G1", "L2_gnn_W1")):
                    a = wcols[name][0]
                    load(wts[0:64, a:a + 64], io[key])
                for name, key in (("K", "L3_gnn_k_lin"), ("Qw", "L3_gnn_q_lin"), ("V", "L3_gnn_v_lin"), ("A", "L3_gnn_a_lin")):
                    load(wt(name, 128).rearrange("p (h e) -> p h e", h=2), io[key].rearrange("(h p) e -> p h e", h=2))
                load(wt("RA"), io["L3_gnn_rel_att"])
                load(wt("RM"), io["L3_gnn_rel_msg"])
                load(wt("pri"), io["L3_gnn_rel_pri"].partition_broadcast(64))
                for t in range(NT):
                    a = wcols["skip"][0] + t // 2
                    load(wts[64 * (t % 2):64 * (t % 2) + 64, a:a + 1], io["L3_gnn_skip"][t:t + 1].partition_broadcast(64))
                for i, key in enumerate(("L2_gnn_beta0", "L2_gnn_beta1")):
                    a = wcols["beta"][0] + i
                    load(wts[:, a:a + 1], io[key].partition_broadcast(P))
                for name, key in (("b02", "L0_gnn_b2"), ("b12", "L1_gnn_b2"), ("bg0", "L2_gnn_b0"), ("bg1", "L2_gnn_b1"),
                                  ("rb2", "L2_gnn_rb2")):
                    load(bs(name), io[key].partition_broadcast(P))
                for name, key in (("att0", "L2_gnn_att0"), ("att1", "L2_gnn_att1")):
                    load(bs(name, 64), io[key].rearrange("a b -> (a b)").partition_broadcast(64))
                for name, key, k in (("b01", "L0_gnn_b1", 64), ("b11", "L1_gnn_b1", 128), ("rb1", "L2_gnn_rb1", 64)):
                    load(bs(name, k), io[key].rearrange("(a b) -> a b", b=1))
                sp.wait_ge(rel_made, 1)
                sp.dma_start(src_d[0:GROUPS].rearrange("g p c -> p g c"), raw_i[1].rearrange("p (g c) -> p g c", c=C)).then_inc(stored, 16)
                sp.dma_start(rel_d[0:GROUPS].rearrange("g p c -> p g c"), raw_i[2].rearrange("p (g c) -> p g c", c=C)).then_inc(stored, 16)
                sp.wait_ge(pooled, 2)
                sp.dma_start(iota_d.rearrange("(p a) b -> p (a b)", p=P), iota_i).then_inc(stored, 16)
                for d in (src_d, rel_d):
                    sp.dma_start(d[GROUPS], zero_i[:, 0:C]).then_inc(stored, 16)
                sp.dma_start(sched_d.rearrange("(p a) b -> p a b", p=P), idle).then_inc(stored, 16)
                sp.dma_start(dsttab_d[N:ND, :].rearrange("(p a) b -> p a b", p=(ND - N) // 2), dpad[0:(ND - N) // 2, :, :]).then_inc(stored, 16)
                sp.dma_start(stat_d[N:ND, :].rearrange("(p a) b -> p a b", p=(ND - N) // 2), dpad[0:(ND - N) // 2, :, 0:12]).then_inc(stored, 16)
                sp.wait_ge(windows_made, 1)
                sp.dma_start(base_d.rearrange("(p a) b -> p (a b)", p=QP), lo_i).then_inc(stored, 16)
                sp.dma_start(nwin_d.rearrange("(p a) b -> p (a b)", p=QP), hi_i).then_inc(stored, 16)
                sp.wait_ge(total_made, 1)
                sp.dma_start(iters_d, total_i).then_inc(stored, 16)
                sp.wait_ge(stored, 16 * 11)

            @block.gpsimd
            def _(pool):
                nc.gpsimd.memset(wts[:], 0.0).then_inc(pooled, 1)
                nc.gpsimd.memset(idle[:, :, 0:RING], OFF_IDLE)
                nc.gpsimd.memset(idle[:, :, RING:], GROUPS)
                nc.gpsimd.memset(zero_i, 0)
                nc.gpsimd.memset(dpad, 0.0)
                nc.gpsimd.memset(ones, 1.0)
                nc.gpsimd.iota(iota16[:], pattern=[[1, ND]], base=0, channel_multiplier=0)
                nc.gpsimd.memset(ident[:], 0.0)
                nc.gpsimd.iota(iota_i, pattern=[[1, ND // P]], base=0, channel_multiplier=ND // P).then_inc(pooled, 1)
                pool.wait_ge(pooled, 2)
                nc.gpsimd.affine_select(out=ident[:], in_=ident[:], compare_op=ALU.not_equal, fill=1.0, base=0,
                                        pattern=[[-1, P]], channel_multiplier=1).then_inc(pooled, 1)

            @block.vector
            def _(dve):
                V = nc.vector
                add, mul = ALU.add, ALU.mult
                chained = [0]

                def link(ins):
                    chained[0] += 1
                    ins.then_inc(made, 1)
                    dve.wait_ge(made, chained[0])

                def show(ins, signal):
                    ins.then_inc(signal, 1)
                    dve.wait_ge(signal, 1)

                dve.wait_ge(loaded, 16 * len(loads))
                dve.wait_ge(pooled, 3)
                link(V.tensor_copy(dstf[:, 0:cols], raw_i[0]))
                link(V.memset(dstf[0:OVER // C, C * FULL:C * FULL + C], -1.0))
                link(V.memset(dstf[:, C * (FULL + 1):], -1.0))
                link(V.tensor_copy(raw_f[1], raw_i[1]))
                link(V.tensor_copy(raw_f[2], raw_i[3]))
                link(V.scalar_tensor_tensor(raw_f[1], raw_f[2], float(N), raw_f[1], mul, add))
                show(V.tensor_copy(raw_i[2], raw_f[1]), rel_made)
                link(V.tensor_scalar(gate[:, 0:cols], raw_f[5], 4.0, -0.25, ALU.min, mul))
                link(V.memset(gate[:, cols:], 1.0))
                link(V.tensor_scalar(gate[:], gate[:], 1.0, 0.0, add, ALU.max))
                link(V.tensor_scalar(gate[:], gate[:], 1.0, None, ALU.min))
                link(V.tensor_copy(spansf, spans))
                link(V.tensor_reduce(lo, spansf, AX.X, ALU.min))
                link(V.tensor_reduce(hi, spansf, AX.X, ALU.max))
                link(V.tensor_copy(lo_i, lo))
                link(V.tensor_tensor(hi, hi, lo, ALU.subtract))
                link(V.tensor_scalar(hi, hi, float(P), None, add))
                link(V.tensor_copy(hi_i, hi))
                link(V.tensor_scalar(hi_i, hi_i, 7, None, ALU.arith_shift_right))
                show(V.tensor_copy(nwin, hi_i), windows_made)
                show(V.tensor_reduce(nsum, nwin, AX.X, add), counts_made)
                dve.wait_ge(summed, 1)
                link(V.tensor_scalar(total[:, 0:1], bank[0][0:1, 0:1], float(LAG + STEPS - 1), None, add))
                link(V.tensor_copy(total[:, 1:2], bank[0][0:1, 0:1]))
                link(V.tensor_copy(total_i, total))
                show(V.tensor_scalar(total_i[:, 0:1], total_i[:, 0:1], STEPS.bit_length() - 1, None, ALU.arith_shift_right), total_made)
                for i in range(2):
                    g, a = wcols[f"G{i}"][0], wcols[f"U{i}"][0]
                    att = bs(f"att{i}", 64)
                    for h in range(2):
                        link(V.tensor_tensor(prod64, wts[0:64, g:g + 64], att[:, 64 * h:64 * h + 64], mul))
                        link(V.tensor_reduce(wts[0:64, a + h:a + h + 1], prod64, AX.X, add))
                    link(V.memset(wts[64:65, g + 64:g + 65], 1.0))
                link(V.tensor_scalar(wt("pri"), wt("pri"), 1.0 / 8.0, None, mul))
                ra = wt("RA").rearrange("p (r d) -> p r d", r=NR)
                link(V.tensor_tensor(ra, ra, wt("pri").unsqueeze(2).to_broadcast([64, NR, F]), mul))
                dve.wait_ge(acted, 1)
                link(V.tensor_scalar(sg, sg, 1.0, None, add))
                link(V.reciprocal(sg, sg))
                for i in range(2):
                    m, b = wcols["mix"][0] + 2 * i, wcols["beta"][0] + i
                    link(V.tensor_copy(wts[:, m + 1:m + 2], wts[:, b:b + 1]))
                    link(V.tensor_scalar(wts[:, m:m + 1], wts[:, b:b + 1], -1.0, 1.0, mul, add))
                    a, s = wcols["A"][0] + 64 * i, wcols["skip"][0] + i
                    link(V.tensor_scalar(wts[:, a:a + 64], wts[:, a:a + 64], wts[:, s:s + 1], None, mul))

            @block.tensor
            def _(pe):
                pe.wait_ge(counts_made, 1)
                pe.matmul(bank[0][0:1, 0:1], nsum, ones[0:QP, :], start=True, stop=True).then_inc(summed, 1)

            @block.scalar
            def _(act):
                act.wait_ge(loaded, 16 * len(loads))
                nc.scalar.activation(sg, sg, ACT.Exp, scale=-1.0).then_inc(acted, 1)

        with nc.Block() as block:
            @block.sync
            def _(sp):
                steps_n = sp.value_load(iters_d[0:1, 1:2], min_val=GROUPS, max_val=GROUPS * WIN)
                at_reg, off_reg, place_reg = (sp.alloc_register(n) for n in ("step_at", "step_off", "step_place"))
                cells = sched_d.rearrange("r (q b) -> (r q) b", b=1)
                with sp.If(steps_n == GROUPS):
                    sp.dma_start(sched_d[0:GROUPS // RING, 0:RING], base_d.rearrange("(r q) b -> r (q b)", q=RING)).then_inc(sched, 16)
                    sp.dma_start(sched_d[0:GROUPS // RING, RING:2 * RING],
                                 iota_d[0:GROUPS, :].rearrange("(r q) b -> r (q b)", q=RING)).then_inc(sched, 16)
                    sp.wait_ge(sched, 32)
                with sp.Else():
                    sp.reg_mov(at_reg, 0)
                    with sp.Fori(0, GROUPS) as g:
                        first = sp.value_load(base_d[bass.ds(g, 1), :], min_val=0, max_val=N - 1)
                        count = sp.value_load(nwin_d[bass.ds(g, 1), :], min_val=1, max_val=WIN)
                        with sp.Fori(0, count) as w:
                            s = sp.snap(at_reg, min_val=0, max_val=GROUPS * WIN - 1)
                            sp.reg_mov(off_reg, first + w * P)
                            o = sp.snap(off_reg, min_val=0, max_val=N - 1)
                            place = s * 2 - s % RING
                            sp.reg_mov(place_reg, place)
                            place = sp.snap(place_reg, min_val=0, max_val=2 * RING * HALVES - RING - 1)
                            sp.dma_start(cells[bass.ds(place, 1), :], iota_d[bass.ds(o, 1), :]).then_inc(sched, 16)
                            sp.dma_start(cells[bass.ds(place + RING, 1), :], iota_d[bass.ds(g, 1), :]).then_inc(sched, 16)
                            sp.reg_add(at_reg, at_reg, 1)
                            sp.wait_ge(sched, (s + 1) * 32)
                            sp.nop(nofuse=True)

        def sweep(tag, kind, table=None, index_d=None):
            expand = kind in ("gat", "mix", "hgt")
            online = kind in ("gat", "hgt")
            R = {"sum": F, "sum_attr": 2 * F, "gat": 2, "mix": F + 1, "hgt": F + 1}[kind]
            width = {"sum": F, "sum_attr": F, "gat": F + 2, "mix": F + 2, "hgt": 2 * F}[kind]
            dw = 4 if kind == "mix" else F + 2
            L = dict(onehot=0, turned=0, turn_copied=0, blocked=0, expanded=0,
                     products=1, cos_summed=1, logit_summed=1, cos_scaled=1, leaky=1, cos_kept=1, masked=1, scored=1, spread=1,
                     max_found=2, max_hi=2, max_rest=2, max_mid=2, max_split=2, max_row=2, max_edge=2, fall=2, top_moved=2,
                     shifted=2, exped=2, relus=2, factors=2, paid=2, summed_=2, new_scaled=3, old_scaled=3, added=3)
            if kind in ("sum", "sum_attr"):
                L = dict(onehot=0, summed_=0, added=1)
            if kind == "mix":
                L = dict(onehot=0, turned=0, turn_copied=0, expanded=0, below=1, cos_part=1, gate_kept=1, shifted=1, exped=1,
                         gat_part=2, fused=2, weighed=2, gated=2, paid=3, summed_=3, added=4)
            S = {n: psem(f"{tag}_{n}") for n in L}
            s_idx = [psem(f"{tag}_idx{k}") for k in range(RING)]
            s_rows = [psem(f"{tag}_rows{k}") for k in range(RING)]
            s_dwin = [psem(f"{tag}_dwin{k}") for k in range(RING)] if expand else None
            s_attr = [psem(f"{tag}_attr{k}") for k in range(RING)] if kind == "sum_attr" else None
            s_stash = [psem(f"{tag}_stash{k}") for k in range(RING)] if kind == "gat" else None
            pool_cleared, dve_cleared = psem(f"{tag}_pool_cleared"), psem(f"{tag}_dve_cleared")
            last_rows = "scored" if kind == "gat" else "paid" if kind in ("mix", "hgt") else "summed_"
            by_target = stat_d if kind == "mix" else dsttab_d

            def rowv(k):
                if kind in ("sum", "sum_attr"):
                    return rows[k][:, :, 0:F]
                flat = rows[k][:].rearrange("p c f -> p (c f)")
                return flat[:, 0:C * width].rearrange("p (c f) -> p c f", c=C)

            turn_b, exp_b, sum_b = bank[0:2], bank[2:4], bank[6:8]
            spread_b, max_b = bank[4], bank[5]

            def w(eng, t, mine, name, ring=0):
                eng.wait_ge(S[name], t[0] + (t[1] - L[mine] + L[name] + 1 + PRIME - ring))

            def landed(eng, sem_, i, u, lag, per=16):
                eng.wait_ge(sem_, i * (per * (STEPS // RING)) + ((u - lag) // RING + 1) * per + 16)

            def prime(eng, *names):
                for n in names:
                    if n in S:
                        eng.sem_inc(S[n], PRIME)

            def start_schedule(eng):
                if eng.engine.name not in carried:
                    carried[eng.engine.name] = [[eng.alloc_register(f"{what}_{q}") for q in range(STEPS)] for what in ("window", "group")]
                offs, grps = carried[eng.engine.name]
                for q in range(RING, STEPS):
                    eng.reg_mov(offs[q], OFF_IDLE)
                    eng.reg_mov(grps[q], GROUPS)
                load_half(eng, 0, 0)
                return (lambda u: eng.snap(offs[u % STEPS], min_val=0, max_val=N),
                        lambda u: eng.snap(grps[u % STEPS], min_val=0, max_val=GROUPS))

            def load_half(eng, row, half):
                offs, grps = carried[eng.engine.name]
                eng.load(offs[half * RING:half * RING + RING] + grps[half * RING:half * RING + RING], sched_d[bass.ds(row, 1), :])

            def load_behind(eng, i, u):
                if u % RING == RING - 1:
                    load_half(eng, i * 2 + (1 if u < RING else 2), 1 if u < RING else 0)

            block = ctx2.enter_context(nc.Block())

            def rounds(eng):
                return eng.value_load(iters_d[0:1, 0:1], min_val=1, max_val=ROUNDS)

            @block.sync
            def _(sp):
                sp.wait_ge(pool_cleared, 1)
                sp.wait_ge(dve_cleared, 1)
                for k in range(RING):
                    if expand:
                        sp.dma_start(dwin[k][:, 0:3 * dw], by_target[0:P, :]).then_inc(s_dwin[k], 16)
                    if kind == "mix":
                        sp.dma_start(rowv(k), stash_d[k].rearrange("p (c f) -> p c f", c=C)).then_inc(s_rows[k], 16)
                    if kind == "gat":
                        sp.wait_ge(s_rows[k], 16)
                        sp.dma_start(stash_d[GROUPS].rearrange("p (c f) -> p c f", c=C), rowv(k)).then_inc(s_stash[k], 16)
                        sp.wait_ge(s_stash[k], 16)
                for k in range(RING):
                    if expand:
                        sp.wait_ge(s_dwin[k], 16)
                    if kind == "mix":
                        sp.wait_ge(s_rows[k], 16)
                n = rounds(sp)
                attr_reg = sp.alloc_register(f"{tag}_attr_at") if kind == "sum_attr" else None
                off, grp = start_schedule(sp)
                with sp.Fori(0, n) as i:
                    i4 = sp.snap(i * STEPS)
                    for u in range(STEPS):
                        t, k = (i4, u), u % RING
                        if kind != "mix":
                            landed(sp, s_rows[k], i, u, RING, 64)
                            sp.nop(nofuse=True)
                            sp.dma_start(idx[k][:], index_d[bass.ds(grp(u), 1), :, :].rearrange("g p c -> (g p) c")).then_inc(s_idx[k], 16)
                        if kind in ("mix", "sum_attr"):
                            sp.wait_ge(S[last_rows], i4 + (u + L[last_rows] + 1 + PRIME - RING))
                            sp.nop(nofuse=True)
                        if kind == "mix":
                            sp.dma_start(rowv(k), stash_d[bass.ds(grp(u), 1), :, :].rearrange("g p (c f) -> (g p) c f", c=C)).then_inc(s_rows[k], 16)
                        if kind == "sum_attr":
                            sp.reg_alu(attr_reg, grp(u) * GE, TAIL, ALU.min)
                            e = sp.snap(attr_reg, min_val=0, max_val=TAIL)
                            sp.dma_start(rows[k][:, :, F:2 * F],
                                         io["edge_attr_64"][bass.ds(e, GE), :].rearrange("(p c) f -> p c f", c=C)).then_inc(s_attr[k], 16)
                        if expand:
                            w(sp, t, "expanded", "expanded", RING)
                            sp.nop(nofuse=True)
                            sp.dma_start(dwin[k][:, 0:3 * dw], by_target[bass.ds(off(u), P), :]).then_inc(s_dwin[k], 16)
                        if kind == "gat":
                            j = (u - 3) % RING
                            landed(sp, s_rows[j], i, u, 3, 64)
                            sp.nop(nofuse=True)
                            landed(sp, s_stash[k], i, u, 1)
                            sp.nop(nofuse=True)
                            sp.dma_start(stash_d[bass.ds(grp(u - 3), 1), :, :].rearrange("g p (c f) -> (g p) c f", c=C),
                                         rowv(j)).then_inc(s_stash[j], 16)
                        load_behind(sp, i, u)
                if kind == "gat":
                    for k in range(RING):
                        sp.wait_ge(s_stash[k], n * (16 * (STEPS // RING)) + 16)
                        sp.nop(nofuse=True)

            @block.gpsimd
            def _(pool):
                if online:
                    nc.gpsimd.memset(top[0:R, :], -BIG)
                if expand:
                    for k in range(RING):
                        nc.gpsimd.memset(pay[k][:], 0.0)
                        nc.gpsimd.memset(gmax[k][:], 0.0)
                        nc.gpsimd.memset(gpart[k][:], 0.0)
                        nc.gpsimd.memset(factor[k][:], 1.0)
                nc.gpsimd.memset(small[:], 0.0).then_inc(pool_cleared, 1)
                if kind == "mix":
                    return
                pool.wait_ge(pool_cleared, 1)
                pool.wait_ge(dve_cleared, 1)
                for k in range(RING):
                    nc.gpsimd.dma_start(rowv(k), table[0:P * C, :].rearrange("(p c) f -> p c f", c=C)).then_inc(s_rows[k], 16)
                n = rounds(pool)
                with pool.Fori(0, n) as i:
                    i4 = pool.snap(i * STEPS)
                    for u in range(STEPS):
                        k = u % RING
                        pool.wait_ge(s_idx[k], i * (16 * (STEPS // RING)) + (u // RING + 1) * 16)
                        pool.wait_ge(S[last_rows], i4 + (u + L[last_rows] + 1 + PRIME - RING))
                        if kind == "gat":
                            landed(pool, s_stash[k], i, u, 1)
                        landed(pool, s_rows[k], i, u, RING, 64)
                        pool.nop(nofuse=True)
                        for c in range(C):
                            nc.gpsimd.indirect_dma_start(
                                out=rowv(k)[:, c, :], out_offset=None, in_=table,
                                in_offset=bass.IndirectOffsetOnAxis(ap=idx[k][:, c:c + 1].bitcast(U32), axis=0)).then_inc(s_rows[k], 16)

            def rows_in(eng, i, u, lag):
                landed(eng, s_rows[(u - lag) % RING], i, u, lag, 16 if kind == "mix" else 64)

            @block.tensor
            def _(pe):
                prime(pe, "turned", "expanded", "spread", "max_row", "max_edge", "summed_")
                pe.wait_ge(pool_cleared, 1)
                pe.wait_ge(dve_cleared, 1)
                n = rounds(pe)
                with pe.Fori(0, n) as i:
                    i4 = pe.snap(i * STEPS)
                    for u in range(STEPS):
                        t, k = (i4, u), u % RING
                        if expand:
                            w(pe, t, "turned", "onehot")
                            w(pe, t, "turned", "turn_copied", 2)
                            if online:
                                w(pe, t, "turned", "blocked", 2)
                            for c in range(C):
                                mm = pe.transpose(turn_b[u % 2][:, c * P:(c + 1) * P], onehot[k][:, c, :], ident[:])
                            mm.then_inc(S["turned"], 1)
                        if online:
                            j = (u - 2) % RING
                            w(pe, t, "max_row", "max_found")
                            w(pe, t, "max_row", "top_moved", 1)
                            w(pe, t, "max_row", "shifted", 1)
                            src = gmax[j][:, 0:2] if kind == "gat" else gmax[j][:, 0:1].to_broadcast([P, R])
                            pe.transpose(max_b[0:R, 0:P], src, ident[:]).then_inc(S["max_row"], 1)
                            w(pe, t, "max_edge", "max_split")
                            for c in range(C):
                                for q in range(3):
                                    mm = pe.matmul(max_b[:, 128 + c:129 + c], turned[j][:, c * P:(c + 1) * P], gpart[j][:, q:q + 1],
                                                   start=q == 0, stop=q == 2)
                            mm.then_inc(S["max_edge"], 1)
                        def expand_rows():
                            if expand:
                                w(pe, t, "expanded", "turn_copied")
                                landed(pe, s_dwin[k], i, u, 0)
                                w(pe, t, "expanded", "scored" if online else "gat_part", 2)
                                for c in range(C):
                                    for q in range(3):
                                        mm = pe.matmul(exp_b[u % 2][:, c * dw:(c + 1) * dw], turned[k][:, c * P:(c + 1) * P],
                                                       dwin[k][:, q * dw:(q + 1) * dw], start=q == 0, stop=q == 2)
                                mm.then_inc(S["expanded"], 1)

                        def sum_rows():
                            j = (u - L["summed_"]) % RING
                            w(pe, t, "summed_", {"gat": "exped", "mix": "paid", "hgt": "paid"}.get(kind, "onehot"))
                            w(pe, t, "summed_", "added", 2)
                            if not expand:
                                rows_in(pe, i, u, 0)
                            if kind == "sum_attr":
                                pe.wait_ge(s_attr[k], i * (16 * (STEPS // RING)) + (u // RING + 1) * 16)
                            for c in range(C):
                                if kind == "sum":
                                    lhs = rows[j][:, c, 0:F]
                                elif kind == "sum_attr":
                                    lhs = rows[j][:, c, :]
                                else:
                                    lhs = pay[j][:, c, 0:R]
                                mm = pe.matmul(sum_b[j % 2][0:R, 0:P], lhs, onehot[j][:, c, :], start=c == 0, stop=c == C - 1)
                            mm.then_inc(S["summed_"], 1)

                        if kind == "mix":
                            sum_rows()
                        expand_rows()
                        if online:
                            j = (u - 1) % RING
                            w(pe, t, "spread", "scored")
                            w(pe, t, "spread", "max_found", 1)
                            for c in range(C):
                                mm = pe.transpose(spread_b[:, c * P:(c + 1) * P], score[j][:, c:c + 1].to_broadcast([P, P]), ident[:])
                            mm.then_inc(S["spread"], 1)
                        if kind != "mix":
                            sum_rows()

            @block.scalar
            def _(act):
                prime(act, "turn_copied", "blocked", "exped", "relus", "factors", "gated")
                if not expand:
                    return
                act.wait_ge(pool_cleared, 1)
                act.wait_ge(dve_cleared, 1)
                nc.scalar.activation(warm, warm, ACT.Exp)
                n = rounds(act)
                with act.Fori(0, n) as i:
                    i4 = act.snap(i * STEPS)
                    for u in range(STEPS):
                        t, k = (i4, u), u % RING
                        w(act, t, "turn_copied", "turned")
                        w(act, t, "turn_copied", "summed_" if kind == "mix" else "max_edge", RING)
                        nc.scalar.copy(turned[k], turn_b[u % 2][:, :]).then_inc(S["turn_copied"], 1)
                        if online:
                            w(act, t, "blocked", "max_found", RING)
                            nc.scalar.activation(block_[k], turn_b[u % 2][:, :], ACT.Copy, bias=-BIG, scale=BIG).then_inc(S["blocked"], 1)
                            k = (u - 2) % RING
                            w(act, t, "exped", "shifted")
                            w(act, t, "exped", "summed_", RING)
                            if kind == "gat":
                                nc.scalar.activation(pay[k][:, :, 0], shift[k], ACT.Exp)
                                nc.scalar.activation(pay[k][:, :, 1], cosine[k], ACT.Exp).then_inc(S["exped"], 1)
                            else:
                                nc.scalar.activation(pay[k][:, :, F], shift[k], ACT.Exp).then_inc(S["exped"], 1)
                            w(act, t, "relus", "fall")
                            nc.scalar.activation(relu2[k % 2][0:R, 0:P], drop[k % 2][0:R, :], ACT.Relu, scale=-1.0)
                            nc.scalar.activation(relu2[k % 2][0:R, P:2 * P], drop[k % 2][0:R, :], ACT.Relu).then_inc(S["relus"], 1)
                            w(act, t, "factors", "relus")
                            w(act, t, "factors", "added", RING)
                            nc.scalar.activation(factor[k][0:R, :], relu2[k % 2][0:R, :], ACT.Exp, scale=-1.0).then_inc(S["factors"], 1)
                        else:
                            k = (u - 1) % RING
                            w(act, t, "exped", "shifted")
                            nc.scalar.activation(shift[k], shift[k], ACT.Exp).then_inc(S["exped"], 1)
                            k = (u - 2) % RING
                            w(act, t, "gated", "weighed")
                            w(act, t, "gated", "summed_", RING)
                            nc.scalar.activation(pay[k][:, :, F], score[k], ACT.Exp).then_inc(S["gated"], 1)

            @block.vector
            def _(dve):
                prime(dve, *[x for x in L if x not in ("turned", "expanded", "spread", "max_row", "max_edge", "summed_",
                                                       "turn_copied", "blocked", "exped", "relus", "factors", "gated")])
                V = nc.vector
                for b in bank:
                    V.memset(b[:], 0.0)
                V.memset(acc[0:R, :], 0.0)
                if kind == "gat":
                    V.memset(logit[:], 0.0)
                    V.memset(ecos[:], 0.0)
                V.memset(work[:], 0.0).then_inc(dve_cleared, 1)
                dve.wait_ge(pool_cleared, 1)
                dve.wait_ge(dve_cleared, 1)
                n = rounds(dve)
                back = L["added"]
                off, grp = start_schedule(dve)
                with dve.Fori(0, n) as i:
                    i4 = dve.snap(i * STEPS)
                    for u in range(STEPS):
                        t, k = (i4, u), u % RING
                        k1, k2, k3 = (u - 1) % RING, (u - 2) % RING, (u - 3) % RING

                        if expand:
                            last_col = dve.snap(grp(u - 1) * C)

                        def signal(ins, name):
                            ins.then_inc(S[name], 1)

                        if online:
                            w(dve, t, "max_found", "spread")
                            w(dve, t, "max_found", "blocked")
                            w(dve, t, "max_found", "max_row", RING)
                            dve.nop(nofuse=True)
                            signal(V.tensor_tensor_reduce(out=block_[k2], in0=spread_b[:, :], in1=block_[k2], scale=1.0, scalar=-BIG,
                                                          op0=ALU.add, op1=ALU.max, accum_out=gmax[k2][:, 0:1]), "max_found")
                        w(dve, t, "onehot", "summed_", RING)
                        signal(V.tensor_tensor(onehot[k], iota16[:, bass.ds(off(u), P)].unsqueeze(1).to_broadcast([P, C, P]),
                                               dstf[:, bass.ds(grp(u) * C, C)].unsqueeze(2).to_broadcast([P, C, P]),
                                               ALU.is_equal), "onehot")
                        if back < RING:
                            load_behind(dve, i, u)
                        if online:
                            w(dve, t, "max_hi", "max_found")
                            w(dve, t, "max_hi", "max_edge", RING)
                            signal(V.tensor_copy(gpart[k2][:, 0:1], gmax[k2][:, 0:1]), "max_hi")
                            ex = exp_b[k1 % 2][:, 0:C * dw].rearrange("p (c f) -> p c f", c=C)
                            w(dve, t, "products", "expanded")
                            rows_in(dve, i, u, 1)
                            signal(V.tensor_tensor(prod[:], rowv(k1)[:, :, 0:F], ex[:, :, 0:F], ALU.mult), "products")
                            w(dve, t, "max_rest", "max_hi")
                            signal(V.tensor_tensor(grest[:], gmax[k2][:, 0:1], gpart[k2][:, 0:1], ALU.subtract), "max_rest")
                            w(dve, t, "scored", "products")
                            w(dve, t, "scored", "exped", RING)
                            if kind == "hgt":
                                signal(V.tensor_reduce(score[k1], prod[:], AX.X, ALU.add), "scored")
                            else:
                                signal(V.tensor_reduce(cosine[k1], prod[:], AX.X, ALU.add), "cos_summed")
                                signal(V.tensor_tensor(score[k1], rowv(k1)[:, :, F], ex[:, :, F], ALU.add), "logit_summed")
                            w(dve, t, "max_mid", "max_rest")
                            signal(V.tensor_copy(gpart[k2][:, 1:2], grest[:]), "max_mid")
                            if kind == "gat":
                                w(dve, t, "leaky", "logit_summed")
                                signal(V.scalar_tensor_tensor(score[k1], score[k1], SLOPE, score[k1], ALU.mult, ALU.max), "leaky")
                                signal(V.tensor_tensor(cosine[k1], cosine[k1], rowv(k1)[:, :, F + 1], ALU.mult), "cos_scaled")
                            w(dve, t, "max_split", "max_mid")
                            signal(V.tensor_tensor(gpart[k2][:, 2:3], grest[:], gpart[k2][:, 1:2], ALU.subtract), "max_split")
                            if kind == "gat":
                                w(dve, t, "masked", "leaky")
                                signal(V.tensor_tensor(score[k1], score[k1], ex[:, :, F + 1], ALU.mult), "masked")
                                w(dve, t, "cos_kept", "cos_scaled")
                                signal(V.tensor_tensor(ecos[:, bass.ds(last_col, C)], ecos[:, bass.ds(last_col, C)], cosine[k1], ALU.add), "cos_kept")
                                w(dve, t, "scored", "masked")
                                signal(V.tensor_tensor(logit[:, bass.ds(last_col, C)], logit[:, bass.ds(last_col, C)], score[k1], ALU.add), "scored")
                            w(dve, t, "shifted", "max_edge")
                            w(dve, t, "shifted", "exped", RING)
                            signal(V.tensor_tensor(shift[k2], score[k2], max_b[:, 128:128 + C], ALU.subtract), "shifted")
                            now = top[0:R, bass.ds(off(u - 2), P)]
                            w(dve, t, "fall", "relus", 2)
                            w(dve, t, "fall", "top_moved", 1)
                            signal(V.tensor_tensor(drop[k2 % 2][0:R, :], now, max_b[0:R, 0:P], ALU.subtract), "fall")
                            signal(V.tensor_tensor(now, now, max_b[0:R, 0:P], ALU.max), "top_moved")
                        if kind == "mix":
                            ex = exp_b[k1 % 2][:, 0:C * dw].rearrange("p (c f) -> p c f", c=C)
                            w(dve, t, "below", "expanded")
                            w(dve, t, "below", "gat_part", RING)
                            signal(V.tensor_tensor(shift[k1], logit[:, bass.ds(last_col, C)], ex[:, :, 0], ALU.subtract), "below")
                            signal(V.tensor_tensor(ccol[k1], ecos[:, bass.ds(last_col, C)], ex[:, :, 2], ALU.mult), "cos_part")
                            signal(V.tensor_copy(gcol[k1], gate[:, bass.ds(last_col, C)]), "gate_kept")
                            w(dve, t, "shifted", "below")
                            signal(V.tensor_tensor(shift[k1], shift[k1], ex[:, :, 3], ALU.mult), "shifted")
                            rows_in(dve, i, u, 3)
                            w(dve, t, "paid", "gated")
                            w(dve, t, "paid", "summed_", RING)
                            signal(V.tensor_tensor(pay[k3][:, :, 0:F], rowv(k3)[:, :, 0:F], pay[k3][:, :, F:F + 1].to_broadcast([P, C, F]),
                                                   ALU.mult), "paid")
                            exk = exp_b[k2 % 2][:, 0:C * dw].rearrange("p (c f) -> p c f", c=C)
                            w(dve, t, "gat_part", "exped")
                            w(dve, t, "gat_part", "gated", RING)
                            signal(V.tensor_tensor(score[k2], shift[k2], exk[:, :, 1], ALU.mult), "gat_part")
                            w(dve, t, "fused", "gat_part")
                            w(dve, t, "fused", "cos_part")
                            signal(V.tensor_tensor(score[k2], score[k2], ccol[k2], ALU.add), "fused")
                            w(dve, t, "weighed", "fused")
                            w(dve, t, "weighed", "gate_kept")
                            signal(V.tensor_tensor(score[k2], score[k2], gcol[k2], ALU.mult), "weighed")
                        k = (u - L["added"]) % RING
                        total_ = acc[0:R, bass.ds(off(u - L["added"]), P)]
                        if online:
                            w(dve, t, "old_scaled", "factors")
                            w(dve, t, "old_scaled", "added", 1)
                            signal(V.tensor_tensor(scaled[0:R, P:2 * P], total_, factor[k][0:R, 0:P], ALU.mult), "old_scaled")
                            w(dve, t, "new_scaled", "summed_")
                            signal(V.tensor_tensor(scaled[0:R, 0:P], sum_b[k % 2][0:R, 0:P], factor[k][0:R, P:2 * P], ALU.mult), "new_scaled")
                            if kind == "hgt":
                                w(dve, t, "paid", "exped")
                                w(dve, t, "paid", "summed_", RING)
                                signal(V.tensor_tensor(pay[k2][:, :, 0:F], rowv(k2)[:, :, F:2 * F], pay[k2][:, :, F:F + 1].to_broadcast([P, C, F]),
                                                       ALU.mult), "paid")
                            w(dve, t, "added", "new_scaled")
                            w(dve, t, "added", "old_scaled")
                            signal(V.tensor_tensor(total_, scaled[0:R, 0:P], scaled[0:R, P:2 * P], ALU.add), "added")
                        else:
                            w(dve, t, "added", "summed_")
                            w(dve, t, "added", "added", 1)
                            signal(V.tensor_tensor(total_, total_, sum_b[k % 2][0:R, 0:P], ALU.add), "added")
                        if back >= RING:
                            load_behind(dve, i, u)

        carried = {}

        warm = small[:, 240:241]
        gmax = [sb(f"gmax{k}", [P, 2]) for k in range(RING)]
        gpart = [sb(f"gpart{k}", [P, 4], BF16) for k in range(RING)]
        grest = sb("grest", [P, 1])
        score = [small[:, 64 + 4 * k:68 + 4 * k] for k in range(RING)]
        cosine = [small[:, 96 + 4 * k:100 + 4 * k] for k in range(RING)]
        shift = [small[:, 128 + 4 * k:132 + 4 * k] for k in range(RING)]
        gcol = [small[:, 160 + 4 * k:164 + 4 * k] for k in range(RING)]
        ccol = [small[:, 192 + 4 * k:196 + 4 * k] for k in range(RING)]
        prod = sb("prod", [P, C, F])
        drop = [sb(f"drop{k}", [P, P]) for k in range(2)]
        relu2 = [sb(f"relu2{k}", [P, 2 * P]) for k in range(2)]
        factor = [sb(f"factor{k}", [P, 2 * P]) for k in range(RING)]
        scaled = sb("scaled", [P, 2 * P])
        ctx2 = ExitStack()

        def run_sweep(*a, **kw):
            nonlocal ctx2
            with ExitStack() as c2:
                ctx2 = c2
                sweep(*a, **kw)
            next_phase()

        def chunk(x, it):
            return x[bass.ds(it * CH, CH), :].rearrange("(p j) f -> p j f", j=J)

        def by_j(x, rows_, it):
            return x[0:rows_, bass.ds(it * CH, CH)].rearrange("r (p j) -> r j p", j=J)

        def area(k, at_, size):
            return work[0:k, at_:at_ + size]

        def jf(ap, f=F):
            return ap.rearrange("p (j f) -> p j f", j=J)

        def jp(ap):
            return ap.rearrange("r (j p) -> r j p", j=J)

        x_t, more_t, y_t, sq_t = (jf(area(Q, k * 256, 256)) for k in range(4))
        m1, m2, m3, m4 = (area(Q, 1024 + 4 * k, 4) for k in range(4))
        t_a, t_b, t_c = (area(P, 1100 + 500 * k, 500) for k in range(3))
        s_row, d_row = (jf(area(Q, 2600 + 264 * k, 264), F + 2) for k in range(2))
        typed_t = area(Q, 3200, 1024).rearrange("p (j t f) -> p j t f", j=J, t=NT)
        typ_i, typ_f = area(Q, 4300, 4).bitcast(I32), area(Q, 4304, 4)
        masks = [area(Q, 4308 + 4 * t, 4) for t in range(NT)]

        z_t, xh_t = (jf(area(Q, k * 256 + 3200, 256)) for k in range(2))

        def wide(v, f=F):
            return v.unsqueeze(2).to_broadcast([Q, J, f])

        def linker(dve, signal, it, per):
            count = [0]

            def link(ins):
                count[0] += 1
                ins.then_inc(signal, 1)
                dve.wait_ge(signal, it * per + count[0])
                assert count[0] <= per

            link.count = count
            return link

        def layernorm(dve, link, y, S, it, out_t=None, stored_=None):
            V = nc.vector
            link(V.tensor_reduce(m1, y, AX.X, ALU.add))
            link(V.tensor_scalar(m1, m1, 1.0 / F, None, ALU.mult))
            link(V.tensor_tensor(y, y, wide(m1), ALU.subtract))
            link(V.tensor_tensor(sq_t, y, y, ALU.mult))
            link(V.tensor_reduce(m2, sq_t, AX.X, ALU.add))
            V.tensor_scalar(m2, m2, 1.0 / F, LN_EPS, ALU.mult, ALU.add).then_inc(S["var_ready"], 1)
            dve.wait_ge(S["std_ready"], it + 1)
            link(V.reciprocal(m2, m3))
            if stored_ is not None:
                dve.wait_ge(stored_, it * 16 + 16)
            V.tensor_tensor(y if out_t is None else out_t, y, wide(m2), ALU.mult).then_inc(S["y_ready"], 1)

        LN_LINKS = 6

        def deviation(act, S, it):
            act.wait_ge(S["var_ready"], it + 1)
            nc.scalar.activation(m3, m2, ACT.Sqrt).then_inc(S["std_ready"], 1)

        def node_mlp(tag, x_in, x_out, w1, b1, w2, b2, k1, m1_, source, extra=None):
            S = {n: psem(f"{tag}_{n}") for n in ("x_for_h", "x_in", "x_turned", "h_ready", "hidden", "relu_ready", "mlp_out", "mlp_used",
                                                "x_used", "y_ready", "y_stored", "var_ready", "std_ready", "link")}
            per = (1 if extra is not None else 0) + LN_LINKS
            loads_n = 32 if extra is not None else 16
            with nc.Block() as block:
                @block.sync
                def _(sp):
                    def load_for_h(c):
                        if source != "sums":
                            sp.dma_start(xh_t, chunk(x_in, c)).then_inc(S["x_for_h"], 16)

                    def load(c):
                        sp.dma_start(x_t, chunk(x_in, c)).then_inc(S["x_in"], 16)
                        if extra is not None:
                            sp.dma_start(more_t, chunk(extra, c)).then_inc(S["x_in"], 16)

                    def store(c):
                        sp.wait_ge(S["y_ready"], c + 1)
                        sp.nop(nofuse=True)
                        sp.dma_start(chunk(x_out, c), z_t).then_inc(S["y_stored"], 16)

                    load_for_h(0)
                    load(0)
                    sp.dma_start(trash_d[0:Q, 0:256].rearrange("p (j f) -> p j f", j=J), z_t).then_inc(S["y_stored"], 16)
                    if source != "sums":
                        sp.wait_ge(S["x_turned"], 1)
                    load_for_h(1)
                    with sp.Fori(0, CHUNKS - 1) as it:
                        if source != "sums":
                            sp.wait_ge(S["x_turned"], it + 2)
                            sp.nop(nofuse=True)
                            load_for_h(ahead(sp, it, 2))
                        sp.wait_ge(S["x_used"], it + 1)
                        sp.nop(nofuse=True)
                        load(it + 1)
                        store(it)
                    store(CHUNKS - 1)
                    sp.wait_ge(S["y_stored"], 16 * (CHUNKS + 1))
                    if source != "sums":
                        sp.wait_ge(S["x_for_h"], 16 * (CHUNKS + 1))

                @block.tensor
                def _(pe):
                    def turn(c):
                        if source != "sums":
                            pe.wait_ge(S["x_for_h"], c * 16 + 16)
                            for j in range(J):
                                mm = pe.matmul(bank[0][0:F, j * Q:(j + 1) * Q], xh_t[:, j, :], ident[0:Q, 0:Q], start=True, stop=True)
                            mm.then_inc(S["x_turned"], 1)

                    def hidden(c):
                        pe.wait_ge(S["h_ready"], c + 1)
                        pe.nop(nofuse=True)
                        pe.matmul(bank[1][0:m1_, 0:CH], wt(w1, k1), t_a[0:k1, :], start=True, stop=True).then_inc(S["hidden"], 1)

                    def mlp(c):
                        pe.wait_ge(S["relu_ready"], c + 1)
                        for j in range(J):
                            mm = pe.matmul(bank[2][0:Q, j * F:(j + 1) * F], t_b[0:m1_, j * Q:(j + 1) * Q], wt(w2, m1_), start=True, stop=True)
                        mm.then_inc(S["mlp_out"], 1)

                    turn(0)
                    hidden(0)
                    turn(1)
                    mlp(0)
                    with pe.Fori(1, CHUNKS - 1) as it:
                        hidden(it)
                        turn(it + 1)
                        pe.wait_ge(S["mlp_used"], it)
                        mlp(it)
                    hidden(CHUNKS - 1)
                    pe.wait_ge(S["mlp_used"], CHUNKS - 1)
                    mlp(CHUNKS - 1)

                @block.scalar
                def _(act):
                    def relu(c):
                        act.wait_ge(S["hidden"], c + 1)
                        nc.scalar.activation(t_b[0:m1_, :], bank[1][0:m1_, 0:CH], ACT.Relu, bias=bs(b1, m1_)).then_inc(S["relu_ready"], 1)

                    nc.scalar.activation(warm, warm, ACT.Sqrt)
                    relu(0)
                    with act.Fori(0, CHUNKS - 1) as it:
                        act.wait_ge(S["mlp_out"], it + 1)
                        relu(it + 1)
                        deviation(act, S, it)
                    deviation(act, S, CHUNKS - 1)

                @block.vector
                def _(dve):
                    V = nc.vector

                    def make_h(c):
                        if source == "sums":
                            V.tensor_copy(jp(t_a[0:k1, :]), by_j(acc, k1, c)).then_inc(S["h_ready"], 1)
                            return
                        dve.wait_ge(S["x_turned"], c + 1)
                        if source == "x_and_sums":
                            V.tensor_tensor(jp(t_a[0:F, :]), jp(bank[0][0:F, 0:CH]), by_j(acc, F, c), ALU.add).then_inc(S["h_ready"], 1)
                        else:
                            V.tensor_copy(t_a[0:F, :], bank[0][0:F, 0:CH]).then_inc(S["h_ready"], 1)

                    def finish(c):
                        link = linker(dve, S["link"], c, per)
                        dve.wait_ge(S["mlp_out"], c + 1)
                        V.tensor_tensor(y_t, jf(bank[2][0:Q, 0:256]), bs(b2, Q).unsqueeze(1).to_broadcast([Q, J, F]), ALU.add).then_inc(S["mlp_used"], 1)
                        dve.wait_ge(S["mlp_used"], c + 1)
                        dve.wait_ge(S["x_in"], c * loads_n + loads_n)
                        if extra is not None:
                            link(V.tensor_tensor(y_t, y_t, more_t, ALU.add))
                        V.tensor_tensor(y_t, y_t, x_t, ALU.add).then_inc(S["x_used"], 1)
                        dve.wait_ge(S["x_used"], c + 1)
                        layernorm(dve, link, y_t, S, c, z_t, S["y_stored"])
                        dve.wait_ge(S["y_ready"], c + 1)
                        assert link.count[0] == per

                    make_h(0)
                    with dve.Fori(0, CHUNKS - 1) as it:
                        dve.wait_ge(S["hidden"], it + 1)
                        make_h(it + 1)
                        finish(it)
                    finish(CHUNKS - 1)

        def ahead(eng, it, by=1):
            key = str(eng.engine)
            if key not in next_reg:
                next_reg[key] = eng.alloc_register("next_chunk")
            eng.reg_alu(next_reg[key], it + by, CHUNKS - 1, ALU.min)
            return eng.snap(next_reg[key], min_val=0, max_val=CHUNKS - 1)

        next_reg = {}

        def in_parts(dve, link, parts, x, last):
            V = nc.vector
            link(V.tensor_copy(parts[:, :, 0, :], x))
            link(V.tensor_tensor(x, x, parts[:, :, 0, :], ALU.subtract))
            link(V.tensor_copy(parts[:, :, 1, :], x))
            V.tensor_tensor(parts[:, :, 2, :], x, parts[:, :, 1, :], ALU.subtract).then_inc(last, 1)

        parts_t = area(Q, 5000, 396).bitcast(BF16).rearrange("p (j q f) -> p j q f", j=J, q=3)
        stat_parts = area(Q, 5400, 24).bitcast(BF16).rearrange("p (j q f) -> p j q f", j=J, q=3)

        def flat_parts(parts):
            return parts.rearrange("p j q f -> p j (q f)")

        def node_gat_tables(tag, x_in, layer):
            S = {n: psem(f"{tag}_{n}") for n in ("x_for_norm", "x_in", "x_turned", "h_ready", "logits", "x_used", "rows_ready",
                                                "rows_stored", "var_ready", "std_ready", "norm_link", "link")}
            per = 1 + 4 + 3
            with nc.Block() as block:
                @block.sync
                def _(sp):
                    def load_for_norm(c):
                        sp.dma_start(xh_t, chunk(x_in, c)).then_inc(S["x_for_norm"], 16)

                    def load(c):
                        sp.dma_start(x_t, chunk(x_in, c)).then_inc(S["x_in"], 16)

                    def store(c):
                        sp.wait_ge(S["rows_ready"], c + 2)
                        sp.nop(nofuse=True)
                        sp.dma_start(chunk(srctab_d, c), s_row).then_inc(S["rows_stored"], 16)
                        sp.dma_start(chunk(dsttab_d, c), flat_parts(parts_t)).then_inc(S["rows_stored"], 16)

                    load_for_norm(0)
                    load(0)
                    sp.wait_ge(S["rows_ready"], 1)
                    sp.dma_start(trash_d[0:Q, :].rearrange("p (j f) -> p j f", j=J), s_row).then_inc(S["rows_stored"], 16)
                    with sp.Fori(0, CHUNKS - 1) as it:
                        sp.wait_ge(S["var_ready"], it + 1)
                        sp.wait_ge(S["x_turned"], it + 1)
                        sp.nop(nofuse=True)
                        load_for_norm(it + 1)
                        sp.wait_ge(S["x_used"], it + 1)
                        sp.nop(nofuse=True)
                        load(it + 1)
                        store(it)
                    store(CHUNKS - 1)
                    sp.wait_ge(S["rows_stored"], 32 * CHUNKS + 16)

                @block.tensor
                def _(pe):
                    with pe.Fori(0, CHUNKS) as it:
                        pe.wait_ge(S["x_for_norm"], it * 16 + 16)
                        for j in range(J):
                            mm = pe.matmul(bank[0][0:F, j * Q:(j + 1) * Q], xh_t[:, j, :], ident[0:Q, 0:Q], start=True, stop=True)
                        mm.then_inc(S["x_turned"], 1)
                        pe.wait_ge(S["h_ready"], it + 1)
                        pe.wait_ge(S["rows_ready"], it + 1)
                        for j in range(J):
                            mm = pe.matmul(bank[1][0:Q, 2 * j:2 * j + 2], t_a[0:F, j * Q:(j + 1) * Q], wt(f"U{layer}"), start=True, stop=True)
                        mm.then_inc(S["logits"], 1)

                @block.scalar
                def _(act):
                    def copy_turned(c):
                        act.wait_ge(S["x_turned"], c + 1)
                        nc.scalar.copy(t_a[0:F, :], bank[0][0:F, 0:CH]).then_inc(S["h_ready"], 1)

                    nc.scalar.activation(warm, warm, ACT.Sqrt)
                    copy_turned(0)
                    with act.Fori(0, CHUNKS - 1) as it:
                        deviation(act, S, it)
                        act.wait_ge(S["logits"], it + 1)
                        copy_turned(it + 1)
                    deviation(act, S, CHUNKS - 1)

                @block.vector
                def _(dve):
                    V = nc.vector

                    def squares(c):
                        dve.wait_ge(S["x_for_norm"], c * 16 + 16)
                        V.tensor_tensor(sq_t, xh_t, xh_t, ALU.mult).then_inc(S["norm_link"], 1)
                        dve.wait_ge(S["norm_link"], c * 2 + 1)
                        V.tensor_reduce(m4, sq_t, AX.X, ALU.add).then_inc(S["norm_link"], 1)
                        dve.wait_ge(S["norm_link"], c * 2 + 2)
                        V.tensor_scalar(m2, m4, COS_EPS2, None, ALU.max).then_inc(S["var_ready"], 1)

                    def norm(c):
                        link = linker(dve, S["link"], c, per)
                        dve.wait_ge(S["std_ready"], c + 1)
                        link(V.reciprocal(m1, m3))
                        return link

                    def make_rows(c, link):
                        V.memset(d_row[:, :, F + 1], 1.0)
                        dve.wait_ge(S["x_in"], c * 16 + 16)
                        link(V.tensor_tensor(d_row[:, :, 0:F], x_t, wide(m1), ALU.mult))
                        dve.wait_ge(S["logits"], c + 1)
                        lg = jf(bank[1][0:Q, 0:2 * J], 2)
                        link(V.tensor_copy(d_row[:, :, F], lg[:, :, 0]))
                        dve.wait_ge(S["rows_stored"], c * 32 + 16)
                        V.tensor_copy(s_row[:, :, 0:F], x_t).then_inc(S["x_used"], 1)
                        dve.wait_ge(S["x_used"], c + 1)
                        link(V.tensor_copy(s_row[:, :, F + 1], m1))
                        link(V.tensor_copy(s_row[:, :, F], lg[:, :, 1]))
                        in_parts(dve, link, parts_t, d_row, S["rows_ready"])
                        dve.wait_ge(S["rows_ready"], c + 2)
                        assert link.count[0] == per

                    V.memset(work[0:Q, 2600:2600 + 528], 1.0).then_inc(S["rows_ready"], 1)
                    dve.wait_ge(S["rows_ready"], 1)
                    squares(0)
                    with dve.Fori(0, CHUNKS - 1) as it:
                        link = norm(it)
                        squares(it + 1)
                        make_rows(it, link)
                    make_rows(CHUNKS - 1, norm(CHUNKS - 1))

        def node_stats(tag, layer):
            S = {n: psem(f"{tag}_{n}") for n in ("rows_copied", "stats_turned", "stats_ready", "stats_stored", "link", "cos_exped")}
            stat_t = jf(area(Q, 2600, 16), 4)
            mix = wts[0:Q, wcols["mix"][0] + 2 * layer:wcols["mix"][0] + 2 * layer + 2]
            per = 4 + 4
            with nc.Block() as block:
                @block.sync
                def _(sp):
                    sp.wait_ge(S["stats_ready"], 1)
                    sp.dma_start(trash_d[0:Q, 0:16].rearrange("p (j f) -> p j f", j=J), stat_t).then_inc(S["stats_stored"], 16)
                    with sp.Fori(0, CHUNKS) as it:
                        sp.wait_ge(S["stats_ready"], it + 2)
                        sp.nop(nofuse=True)
                        sp.dma_start(chunk(stat_d, it), flat_parts(stat_parts)).then_inc(S["stats_stored"], 16)
                    sp.wait_ge(S["stats_stored"], 16 * CHUNKS + 16)

                @block.scalar
                def _(act):
                    nc.scalar.activation(ecos[:], ecos[:], ACT.Exp).then_inc(S["cos_exped"], 1)
                    act.wait_ge(S["cos_exped"], 1)

                @block.tensor
                def _(pe):
                    with pe.Fori(0, CHUNKS) as it:
                        pe.wait_ge(S["rows_copied"], it + 1)
                        for j in range(J):
                            pe.matmul(bank[0][0:Q, 4 * j:4 * j + 1], t_a[0:1, j * Q:(j + 1) * Q], ident[0:1, 0:1], start=True, stop=True)
                            mm = pe.matmul(bank[0][0:Q, 4 * j + 1:4 * j + 3], t_b[0:2, j * Q:(j + 1) * Q], ident[0:2, 0:2], start=True, stop=True)
                        mm.then_inc(S["stats_turned"], 1)

                @block.vector
                def _(dve):
                    V = nc.vector
                    V.memset(stat_t, 1.0).then_inc(S["stats_ready"], 1)
                    dve.wait_ge(S["stats_ready"], 1)
                    with dve.Fori(0, CHUNKS) as it:
                        link = linker(dve, S["link"], it, per)
                        link(V.tensor_copy(jp(t_a[0:1, :]), by_j(top, 1, it)))
                        V.tensor_copy(jp(t_b[0:2, :]), by_j(acc, 2, it)).then_inc(S["rows_copied"], 1)
                        dve.wait_ge(S["stats_turned"], it + 1)
                        dve.wait_ge(S["stats_stored"], it * 16 + 16)
                        ps = jf(bank[0][0:Q, 0:16], 4)
                        link(V.tensor_copy(stat_t[:, :, 0], ps[:, :, 0]))
                        link(V.tensor_scalar(stat_t[:, :, 1:3], ps[:, :, 1:3], SM_EPS, None, ALU.add))
                        link(V.reciprocal(stat_t[:, :, 1:3], stat_t[:, :, 1:3]))
                        V.memset(stat_t[:, :, 3], 1.0)
                        link(V.tensor_tensor(stat_t[:, :, 1:3], stat_t[:, :, 1:3], mix.unsqueeze(1).to_broadcast([Q, J, 2]), ALU.mult))
                        in_parts(dve, link, stat_parts, stat_t, S["stats_ready"])
                        dve.wait_ge(S["stats_ready"], it + 2)
                        assert link.count[0] == per

        def node_gat_out(tag, layer, h_out, twice):
            S = {n: psem(f"{tag}_{n}") for n in ("h_ready", "out_ready", "low", "exped", "h_made", "h_stored", "link")}
            rounds = 2 if twice else 1
            per = 4 + 1 + (rounds - 1) * 2
            with nc.Block() as block:
                @block.sync
                def _(sp):
                    sp.dma_start(trash_d[0:Q, 0:256].rearrange("p (j f) -> p j f", j=J), y_t).then_inc(S["h_stored"], 16)
                    with sp.Fori(0, CHUNKS) as it:
                        sp.wait_ge(S["h_made"], it + 1)
                        sp.nop(nofuse=True)
                        sp.dma_start(chunk(h_out, it), y_t).then_inc(S["h_stored"], 16)
                    sp.wait_ge(S["h_stored"], 16 * CHUNKS + 16)

                @block.tensor
                def _(pe):
                    with pe.Fori(0, CHUNKS) as it:
                        pe.wait_ge(S["h_ready"], it + 1)
                        for j in range(J):
                            mm = pe.matmul(bank[0][0:Q, j * (F + 1):(j + 1) * (F + 1)], t_a[0:F + 1, j * Q:(j + 1) * Q],
                                           wt(f"G{layer}", F + 1), start=True, stop=True)
                        mm.then_inc(S["out_ready"], 1)

                @block.scalar
                def _(act):
                    with act.Fori(0, CHUNKS) as it:
                        for r in range(rounds):
                            act.wait_ge(S["low"], it * rounds + r + 1)
                            nc.scalar.activation(sq_t, sq_t, ACT.Exp).then_inc(S["exped"], 1)

                @block.vector
                def _(dve):
                    V = nc.vector
                    with dve.Fori(0, CHUNKS) as it:
                        link = linker(dve, S["link"], it, per)
                        V.tensor_copy(jp(t_a[0:F + 1, :]), by_j(acc, F + 1, it)).then_inc(S["h_ready"], 1)
                        dve.wait_ge(S["out_ready"], it + 1)
                        ps = jf(bank[0][0:Q, 0:J * (F + 1)], F + 1)
                        link(V.tensor_scalar(m1, ps[:, :, F], SM_EPS, None, ALU.add))
                        link(V.reciprocal(m1, m1))
                        dve.wait_ge(S["h_stored"], it * 16 + 16)
                        link(V.tensor_tensor(y_t, ps[:, :, 0:F], wide(m1), ALU.mult))
                        link(V.tensor_tensor(y_t, y_t, bs(f"bg{layer}", Q).unsqueeze(1).to_broadcast([Q, J, F]), ALU.add))
                        for r in range(rounds):
                            V.tensor_scalar(sq_t, y_t, 0.0, None, ALU.min).then_inc(S["low"], 1)
                            link(V.tensor_scalar(y_t, y_t, 0.0, None, ALU.max))
                            dve.wait_ge(S["exped"], it * rounds + r + 1)
                            last = V.scalar_tensor_tensor(y_t, sq_t, -1.0, y_t, ALU.add, ALU.add)
                            if r < rounds - 1:
                                link(last)
                        last.then_inc(S["h_made"], 1)
                        dve.wait_ge(S["h_made"], it + 1)
                        assert link.count[0] == per

        def typed(link, last, x):
            V = nc.vector
            for t in range(NT):
                ins = V.tensor_tensor(typed_t[:, :, t, :], x, wide(masks[t]), ALU.mult)
                if t < NT - 1:
                    link(ins)
            ins.then_inc(last, 1)

        def make_masks(link):
            V = nc.vector
            link(V.tensor_copy(typ_f, typ_i))
            for t in range(NT):
                link(V.tensor_scalar(masks[t], typ_f, float(t), None, ALU.is_equal))

        def turn_typed(pe, signal):
            for h in range(2):
                for j in range(J):
                    mm = pe.matmul(bank[h][:, j * Q:(j + 1) * Q], typed_t[:, j, 2 * h:2 * h + 2, :].rearrange("p t f -> p (t f)"),
                                   ident[0:Q, 0:Q], start=True, stop=True)
            mm.then_inc(signal, 1)

        types = io["node_type_4"].rearrange("(n j) -> n j", j=J)
        rel_t = top[0:Q, 0:NR * J * 2 * F].rearrange("p (r j f) -> p r j f", r=NR, j=J)

        def node_relations(tag, x_in):
            S = {n: psem(f"{tag}_{n}") for n in ("x_in", "typed", "turned", "half0", "half1", "kv", "k_copied", "v_copied", "q_ready",
                                                "rel_out", "att_copied", "msg_copied", "q_copied", "q_set", "stored", "link")}
            per = 5 + NT - 1 + 4
            wk, wq, wv = (wt(n, P).rearrange("p (h e) -> p h e", h=2) for n in ("K", "Qw", "V"))
            with nc.Block() as block:
                @block.sync
                def _(sp):
                    def load(at_it):
                        sp.dma_start(x_t, chunk(x_in, at_it)).then_inc(S["x_in"], 16)
                        sp.dma_start(typ_i, types[bass.ds(at_it * Q, Q), :]).then_inc(S["x_in"], 16)

                    load(0)
                    sp.wait_ge(S["q_set"], 1)
                    sp.dma_start(trash_d[0:Q, :].rearrange("p (j f) -> p j f", j=J), d_row).then_inc(S["stored"], 16)
                    with sp.Fori(0, CHUNKS) as it:
                        sp.wait_ge(S["typed"], it + 1)
                        sp.nop(nofuse=True)
                        load(ahead(sp, it))
                        sp.wait_ge(S["q_copied"], it + 1)
                        sp.nop(nofuse=True)
                        sp.dma_start(chunk(dsttab_d, it), flat_parts(parts_t)).then_inc(S["stored"], 16)
                        sp.wait_ge(S["att_copied"], it * J + J)
                        sp.wait_ge(S["msg_copied"], it * J + J)
                        sp.nop(nofuse=True)
                        for r in range(NR):
                            sp.dma_start(reltab_d[r * N:(r + 1) * N, :][bass.ds(it * CH, CH), :].rearrange("(p j) f -> p j f", j=J),
                                         rel_t[:, r, :, :]).then_inc(S["stored"], 16)
                    sp.wait_ge(S["stored"], 16 + (NR + 1) * 16 * CHUNKS)
                    sp.wait_ge(S["x_in"], 32 * (CHUNKS + 1))

                @block.tensor
                def _(pe):
                    with pe.Fori(0, CHUNKS) as it:
                        pe.wait_ge(S["typed"], it + 1)
                        turn_typed(pe, S["turned"])
                        pe.wait_ge(S["half0"], it + 1)
                        pe.wait_ge(S["half1"], it + 1)
                        for b, w_ in ((2, wk), (3, wv)):
                            for h in range(2):
                                mm = pe.matmul(bank[b][0:F, 0:CH], w_[:, h, :], (t_a, t_b)[h], start=h == 0, stop=h == 1)
                        mm.then_inc(S["kv"], 1)
                        for j in range(J):
                            for h in range(2):
                                mm = pe.matmul(bank[4][0:Q, j * F:(j + 1) * F], (t_a, t_b)[h][:, j * Q:(j + 1) * Q], wq[:, h, :],
                                               start=h == 0, stop=h == 1)
                        mm.then_inc(S["q_ready"], 1)
                        pe.wait_ge(S["k_copied"], it + 1)
                        pe.wait_ge(S["v_copied"], it + 1)
                        for j in range(J):
                            if j >= 2:
                                pe.wait_ge(S["att_copied"], it * J + j - 1)
                                pe.wait_ge(S["msg_copied"], it * J + j - 1)
                            pe.matmul(bank[5 + j % 2][0:Q, :], t_c[0:F, j * Q:(j + 1) * Q], wt("RA"), start=True, stop=True)
                            pe.matmul(bank[7 * (1 - j % 2)][0:Q, :], vT[0:F, j * Q:(j + 1) * Q], wt("RM"), start=True, stop=True).then_inc(S["rel_out"], 1)
                        pe.wait_ge(S["msg_copied"], it * J + J)

                @block.scalar
                def _(act):
                    with act.Fori(0, CHUNKS) as it:
                        act.wait_ge(S["turned"], it + 1)
                        nc.scalar.copy(t_a, bank[0][:, 0:CH]).then_inc(S["half0"], 1)
                        act.wait_ge(S["kv"], it + 1)
                        nc.scalar.copy(t_c[0:F, :], bank[2][0:F, 0:CH]).then_inc(S["k_copied"], 1)
                        act.wait_ge(S["stored"], it * (NR + 1) * 16 + 16)
                        for j in range(J):
                            act.wait_ge(S["rel_out"], it * J + j + 1)
                            nc.scalar.copy(rel_t[:, :, j, 0:F], bank[5 + j % 2][0:Q, :].rearrange("p (r d) -> p r d", r=NR)).then_inc(S["att_copied"], 1)

                @block.vector
                def _(dve):
                    V = nc.vector
                    V.memset(d_row, 1.0).then_inc(S["q_set"], 1)
                    dve.wait_ge(S["q_set"], 1)
                    with dve.Fori(0, CHUNKS) as it:
                        link = linker(dve, S["link"], it, per)
                        dve.wait_ge(S["x_in"], it * 32 + 32)
                        make_masks(link)
                        typed(link, S["typed"], x_t)
                        dve.wait_ge(S["turned"], it + 1)
                        V.tensor_copy(t_b, bank[1][:, 0:CH]).then_inc(S["half1"], 1)
                        dve.wait_ge(S["kv"], it + 1)
                        V.tensor_copy(vT[0:F, :], bank[3][0:F, 0:CH]).then_inc(S["v_copied"], 1)
                        dve.wait_ge(S["stored"], it * (NR + 1) * 16 + 16)
                        dve.wait_ge(S["q_ready"], it + 1)
                        V.memset(d_row[:, :, F:], 1.0)
                        link(V.tensor_copy(d_row[:, :, 0:F], jf(bank[4][0:Q, 0:256])))
                        in_parts(dve, link, parts_t, d_row, S["q_copied"])
                        for j in range(J):
                            dve.wait_ge(S["rel_out"], it * J + j + 1)
                            V.tensor_copy(rel_t[:, :, j, F:2 * F], bank[7 * (1 - j % 2)][0:Q, :].rearrange("p (r d) -> p r d", r=NR)).then_inc(S["msg_copied"], 1)
                        assert link.count[0] == per

        vT = area(P, 4400, 500)

        def node_last(tag, x_in):
            S = {n: psem(f"{tag}_{n}") for n in ("x_in", "h_ready", "sums_turned", "typed", "turned", "half0", "half1", "mapped", "x_used",
                                                "y_ready", "y_stored", "var_ready", "std_ready", "link")}
            per = 5 + 4 + NT - 1 + LN_LINKS
            wa = wt("A", P).rearrange("p (h e) -> p h e", h=2)
            with nc.Block() as block:
                @block.sync
                def _(sp):
                    def load(at_it):
                        sp.dma_start(x_t, chunk(x_in, at_it)).then_inc(S["x_in"], 16)
                        sp.dma_start(typ_i, types[bass.ds(at_it * Q, Q), :]).then_inc(S["x_in"], 16)

                    load(0)
                    sp.dma_start(trash_d[0:Q, 0:256].rearrange("p (j f) -> p j f", j=J), y_t).then_inc(S["y_stored"], 16)
                    with sp.Fori(0, CHUNKS) as it:
                        sp.wait_ge(S["x_used"], it + 1)
                        sp.nop(nofuse=True)
                        load(ahead(sp, it))
                        sp.wait_ge(S["y_ready"], it + 1)
                        sp.nop(nofuse=True)
                        sp.dma_start(chunk(out, it), y_t).then_inc(S["y_stored"], 16)
                    sp.wait_ge(S["y_stored"], 16 * (CHUNKS + 1))
                    sp.wait_ge(S["x_in"], 32 * (CHUNKS + 1))

                @block.tensor
                def _(pe):
                    with pe.Fori(0, CHUNKS) as it:
                        pe.wait_ge(S["h_ready"], it + 1)
                        for j in range(J):
                            mm = pe.matmul(bank[2][0:Q, j * (F + 1):(j + 1) * (F + 1)], t_c[0:F + 1, j * Q:(j + 1) * Q],
                                           ident[0:F + 1, 0:F + 1], start=True, stop=True)
                        mm.then_inc(S["sums_turned"], 1)
                        pe.wait_ge(S["typed"], it + 1)
                        turn_typed(pe, S["turned"])
                        pe.wait_ge(S["half0"], it + 1)
                        pe.wait_ge(S["half1"], it + 1)
                        for j in range(J):
                            for h in range(2):
                                mm = pe.matmul(bank[3][0:Q, j * F:(j + 1) * F], (t_a, t_b)[h][:, j * Q:(j + 1) * Q], wa[:, h, :],
                                               start=h == 0, stop=h == 1)
                        mm.then_inc(S["mapped"], 1)

                @block.scalar
                def _(act):
                    nc.scalar.activation(warm, warm, ACT.Sqrt)
                    with act.Fori(0, CHUNKS) as it:
                        act.wait_ge(S["turned"], it + 1)
                        nc.scalar.copy(t_a, bank[0][:, 0:CH]).then_inc(S["half0"], 1)
                        deviation(act, S, it)

                @block.vector
                def _(dve):
                    V = nc.vector
                    with dve.Fori(0, CHUNKS) as it:
                        link = linker(dve, S["link"], it, per)
                        V.tensor_copy(jp(t_c[0:F + 1, :]), by_j(acc, F + 1, it)).then_inc(S["h_ready"], 1)
                        dve.wait_ge(S["x_in"], it * 32 + 32)
                        make_masks(link)
                        dve.wait_ge(S["sums_turned"], it + 1)
                        ps = jf(bank[2][0:Q, 0:J * (F + 1)], F + 1)
                        link(V.tensor_scalar(m1, ps[:, :, F], 0.0, None, ALU.is_equal))
                        link(V.tensor_tensor(m1, m1, ps[:, :, F], ALU.add))
                        link(V.reciprocal(m1, m1))
                        link(V.tensor_tensor(more_t, ps[:, :, 0:F], wide(m1), ALU.mult))
                        typed(link, S["typed"], more_t)
                        dve.wait_ge(S["turned"], it + 1)
                        V.tensor_copy(t_b, bank[1][:, 0:CH]).then_inc(S["half1"], 1)
                        dve.wait_ge(S["mapped"], it + 1)
                        dve.wait_ge(S["y_stored"], it * 16 + 16)
                        V.tensor_tensor(y_t, jf(bank[3][0:Q, 0:256]), x_t, ALU.add).then_inc(S["x_used"], 1)
                        dve.wait_ge(S["x_used"], it + 1)
                        layernorm(dve, link, y_t, S, it)
                        dve.wait_ge(S["y_ready"], it + 1)
                        assert link.count[0] == per

        run_sweep("s0", "sum_attr", io["x"], src_d)
        node_mlp("n0", io["x"], x1_d, "W01", "b01", "W02", "b02", F, F, "x_and_sums")
        next_phase()
        run_sweep("s1", "sum", x1_d, src_d)
        node_mlp("n1", x1_d, x2_d, "W11", "b11", "W12", "b12", P, P, "sums")
        next_phase()
        for layer, x_l, h_l in ((0, x2_d, h1_d), (1, h1_d, h2_d)):
            node_gat_tables(f"t{layer}", x_l, layer)
            next_phase()
            run_sweep(f"a{layer}", "gat", srctab_d, src_d)
            node_stats(f"st{layer}", layer)
            next_phase()
            run_sweep(f"b{layer}", "mix")
            node_gat_out(f"h{layer}", layer, h_l, layer == 0)
            next_phase()
        node_mlp("n2", x2_d, x3_d, "R1", "rb1", "R2", "rb2", F, F, "x", extra=h2_d)
        next_phase()
        node_relations("r", x3_d)
        next_phase()
        run_sweep("s3", "hgt", reltab_d, rel_d)
        node_last("last", x3_d)
        next_phase()


_INS = ['x', 'src', 'dst', 'edge_attr_64', 'edge_type_8', 'edge_weight', 'node_type_4', 'L0_gnn_W1', 'L0_gnn_b1',
        'L0_gnn_W2', 'L0_gnn_b2', 'L1_gnn_W1', 'L1_gnn_b1', 'L1_gnn_W2', 'L1_gnn_b2', 'L2_gnn_W0', 'L2_gnn_att0',
        'L2_gnn_beta0', 'L2_gnn_b0', 'L2_gnn_W1', 'L2_gnn_att1', 'L2_gnn_beta1', 'L2_gnn_b1', 'L2_gnn_rW1',
        'L2_gnn_rb1', 'L2_gnn_rW2', 'L2_gnn_rb2', 'L3_gnn_k_lin', 'L3_gnn_q_lin', 'L3_gnn_v_lin', 'L3_gnn_a_lin',
        'L3_gnn_rel_att', 'L3_gnn_rel_msg', 'L3_gnn_rel_pri', 'L3_gnn_skip']


def kernel(**inputs):
    import numpy as _np
    import concourse.bacc as _bacc
    from concourse import mybir as _mybir
    from concourse.bass_utils import run_bass_kernel_spmd as _run

    nc = _bacc.Bacc("TRN2", target_bir_lowering=False, num_devices=1)
    arrays, io = {}, {}
    for name in _INS:
        a = _np.asarray(inputs[name])
        if name == "L3_gnn_rel_att":
            a = a.transpose(2, 0, 1).reshape(64, -1)
        elif name == "L3_gnn_rel_msg":
            a = a.transpose(1, 0, 2).reshape(64, -1)
        elif name.endswith("_lin"):
            a = a.reshape(-1, a.shape[-1])
        a = _np.ascontiguousarray(a)
        arrays[f"in_{name}_dram"] = a
        io[name] = nc.dram_tensor(f"in_{name}_dram", a.shape, _mybir.dt.from_np(a.dtype), kind="ExternalInput").ap()
    out = nc.dram_tensor("out_0_dram", (12500, 64), _mybir.dt.float32, kind="ExternalOutput").ap()
    build(nc, io, out)
    r = _run(nc, [arrays], core_ids=[0])
    return r.results[0]["out_0_dram"]
```
